# Optimizing a Trainium2 kernel written in Bass

```python
import numpy as np
import jax
import jax.numpy as jnp

def _softmax(x, axis=-1):
    return jax.nn.softmax(x, axis=axis)

def _gelu(x):
    return jax.nn.gelu(x, approximate=True)

def _silu(x):
    return jax.nn.silu(x)

def _sigmoid(x):
    return jax.nn.sigmoid(x)

def _layernorm(x, axis=-1, eps=1e-05):
    m = jnp.mean(x, axis=axis, keepdims=True)
    v = jnp.var(x, axis=axis, keepdims=True)
    return (x - m) / jnp.sqrt(v + eps)

def _scatter_add(tgt, idx, src, axis=0):
    return tgt.at[idx].add(src)

def _segment_sum(src, seg, n):
    return jax.ops.segment_sum(src, seg, n)
kernel_name = 'mk_conv_attn_hybrid_d4_conv_nchw512_r4_acbb0f'

def setup_inputs(seed: int=0):
    np.random.seed(seed)
    _w = jnp.asarray

    def _rec_inputs():
        import jax
        import jax.numpy as jnp
        _gk = jax.random.key(seed)
        x = -0.000125 + 0.9999 * jax.random.normal(jax.random.fold_in(_gk, 1), (16, 128, 16, 16), jnp.float32)
        return x
    x = _rec_inputs()

    def _L0_conv_setup():
        import jax, jax.numpy as jnp
        from jax import lax
        import numpy as np
        key = jax.random.key(seed)
        ks = jax.random.split(key, 16)
        N, C, H, W = (16, 128, 16, 16)
        Cm, planes, k = (32, 128, 5)
        s = 0.05
        return {'x': jax.random.normal(ks[0], (N, C, H, W), jnp.float32), 'conv_w': jax.random.normal(ks[1], (Cm, C, 1, 1), jnp.float32) * s, 'conv_b': jax.random.normal(ks[2], (Cm,), jnp.float32) * s, 'conv_k_w': jax.random.normal(ks[3], (1, 2, 1, 1), jnp.float32) * s, 'conv_k_b': jax.random.normal(ks[4], (1,), jnp.float32) * s, 'conv_k2_w': jax.random.normal(ks[5], (1, 2, 1, 1), jnp.float32) * s, 'conv_k2_b': jax.random.normal(ks[6], (1,), jnp.float32) * s, 'conv_kernel_w': jax.random.normal(ks[7], (k * k, 1, 1, 1), jnp.float32) * s, 'conv_kernel_b': jax.random.normal(ks[8], (k * k,), jnp.float32) * s, 'conv_kernel2_w': jax.random.normal(ks[9], (9, 1, 1, 1), jnp.float32) * s, 'conv_kernel2_b': jax.random.normal(ks[10], (9,), jnp.float32) * s, 'adap_bias': jax.random.normal(ks[11], (Cm,), jnp.float32) * s, 'atrous_bias': jax.random.normal(ks[12], (Cm,), jnp.float32) * s, 'fuse_w': jax.random.normal(ks[13], (planes, 2 * Cm, 1, 1), jnp.float32) * s, 'fuse_b': jax.random.normal(ks[14], (planes,), jnp.float32) * s}
    _L0_conv_all = _L0_conv_setup()
    _L0_conv_in = {k: v for k, v in _L0_conv_all.items() if k in ('conv_w', 'conv_b', 'conv_k_w', 'conv_k_b', 'conv_k2_w', 'conv_k2_b', 'conv_kernel_w', 'conv_kernel_b', 'conv_kernel2_w', 'conv_kernel2_b', 'adap_bias', 'atrous_bias', 'fuse_w', 'fuse_b')}
    del _L0_conv_all

    def _L1_conv_setup():
        import jax, jax.numpy as jnp
        import numpy as np
        key = jax.random.key(seed)
        x = jax.random.normal(key, (16, 128, 40, 40), dtype=jnp.float32)
        return {'x': x}
    _L1_conv_all = _L1_conv_setup()
    _L1_conv_in = {k: v for k, v in _L1_conv_all.items() if k in ()}
    del _L1_conv_all

    def _L2_attn_setup():
        import jax, jax.numpy as jnp
        import numpy as np
        EMBED_DIM = 128
        NUM_HEADS = 8
        HEAD_DIM = EMBED_DIM // NUM_HEADS

        def _split_heads(x, B, S):
            return x.reshape(B, S, NUM_HEADS, HEAD_DIM).transpose(0, 2, 1, 3)
        key = jax.random.key(seed)
        ks = jax.random.split(key, 6)
        B, S, D = (2, 1024, EMBED_DIM)
        scale = 1.0 / np.sqrt(D)
        inputs = jax.random.normal(ks[0], (B, S, D), dtype=jnp.float32)
        Wq = jax.random.normal(ks[1], (D, D), dtype=jnp.float32) * scale
        Wk = jax.random.normal(ks[2], (D, D), dtype=jnp.float32) * scale
        Wv = jax.random.normal(ks[3], (D, D), dtype=jnp.float32) * scale
        Wo = jax.random.normal(ks[4], (D, D), dtype=jnp.float32) * scale
        zeros = jnp.zeros((D,), dtype=jnp.float32)
        return {'inputs': inputs, 'Wq': Wq, 'bq': zeros, 'Wk': Wk, 'bk': zeros, 'Wv': Wv, 'bv': zeros, 'Wo': Wo, 'bo': zeros}
    _L2_attn_all = _L2_attn_setup()
    _L2_attn_in = {k: v for k, v in _L2_attn_all.items() if k in ('Wq', 'bq', 'Wk', 'bk', 'Wv', 'bv', 'Wo', 'bo')}
    del _L2_attn_all

    def _L2_ffn_setup():
        import jax, jax.numpy as jnp
        import numpy as np
        B, S, D, H, E, K = (2, 512, 128, 256, 8, 2)

        def _moe(x, router_w, w_gate, w_up, w_down):
            bsz, seq, d = x.shape
            flat = x.reshape(-1, d)
            logits = flat @ router_w.T
            topk_vals, topk_idx = jax.lax.top_k(logits, K)
            topk_w = jax.nn.softmax(topk_vals, axis=-1)
            s = flat.shape[0]
            dense_w = jnp.zeros((s, E), dtype=flat.dtype).at[jnp.arange(s)[:, None], topk_idx].add(topk_w)
            g = jnp.einsum('sd,edh->esh', flat, w_gate)
            u = jnp.einsum('sd,edh->esh', flat, w_up)
            y = jnp.einsum('esh,ehd->esd', jax.nn.silu(g) * u, w_down)
            out = jnp.einsum('esd,se->sd', y, dense_w)
            return out.reshape(bsz, seq, d)
        key = jax.random.key(seed)
        k1, k2, k3, k4, k5 = jax.random.split(key, 5)
        return {'x': jax.random.normal(k1, (B, S, D), dtype=jnp.float32), 'router_w': jax.random.normal(k2, (E, D), dtype=jnp.float32) * D ** (-0.5), 'w_gate': jax.random.normal(k3, (E, D, H), dtype=jnp.float32) * D ** (-0.5), 'w_up': jax.random.normal(k4, (E, D, H), dtype=jnp.float32) * D ** (-0.5), 'w_down': jax.random.normal(k5, (E, H, D), dtype=jnp.float32) * H ** (-0.5)}
    _L2_ffn_all = _L2_ffn_setup()
    _L2_ffn_in = {k: v for k, v in _L2_ffn_all.items() if k in ('router_w', 'w_gate', 'w_up', 'w_down')}
    del _L2_ffn_all

    def _L3_attn_setup():
        import jax, jax.numpy as jnp
        import numpy as np
        NUM_HEADS = 8
        EPS = 1e-06
        key = jax.random.key(seed)
        k1, k2, k3 = jax.random.split(key, 3)
        B, N, C = (8, 1024, 128)
        x = jax.random.normal(k1, (B, N, C), dtype=jnp.float32)
        Wq = jax.random.normal(k2, (C, C), dtype=jnp.float32) * (1.0 / np.sqrt(C))
        Wkv = jax.random.normal(k3, (2 * C, C), dtype=jnp.float32) * (1.0 / np.sqrt(C))
        return {'x': x, 'Wq': Wq, 'Wkv': Wkv}
    _L3_attn_all = _L3_attn_setup()
    _L3_attn_in = {k: v for k, v in _L3_attn_all.items() if k in ('Wq', 'Wkv')}
    del _L3_attn_all

    def _L3_ffn_setup():
        import jax, jax.numpy as jnp
        import numpy as np
        B, S, D, F, E, K = (4, 512, 128, 512, 8, 2)
        key = jax.random.key(seed)
        kx, kg, kw, kv, k2 = jax.random.split(key, 5)
        scale = 0.02
        return {'x': jax.random.normal(kx, (B, S, D), dtype=jnp.float32), 'Wg': jax.random.normal(kg, (D, E), dtype=jnp.float32) * scale, 'W': jax.random.normal(kw, (E, D, F), dtype=jnp.float32) * scale, 'V': jax.random.normal(kv, (E, D, F), dtype=jnp.float32) * scale, 'W2': jax.random.normal(k2, (E, F, D), dtype=jnp.float32) * scale}
    _L3_ffn_all = _L3_ffn_setup()
    _L3_ffn_in = {k: v for k, v in _L3_ffn_all.items() if k in ('Wg', 'W', 'V', 'W2')}
    del _L3_ffn_all
    return {'x': x, 'L0_conv_conv_w': _L0_conv_in['conv_w'], 'L0_conv_conv_b': _L0_conv_in['conv_b'], 'L0_conv_conv_k_w': _L0_conv_in['conv_k_w'], 'L0_conv_conv_k_b': _L0_conv_in['conv_k_b'], 'L0_conv_conv_k2_w': _L0_conv_in['conv_k2_w'], 'L0_conv_conv_k2_b': _L0_conv_in['conv_k2_b'], 'L0_conv_conv_kernel_w': _L0_conv_in['conv_kernel_w'], 'L0_conv_conv_kernel_b': _L0_conv_in['conv_kernel_b'], 'L0_conv_conv_kernel2_w': _L0_conv_in['conv_kernel2_w'], 'L0_conv_conv_kernel2_b': _L0_conv_in['conv_kernel2_b'], 'L0_conv_adap_bias': _L0_conv_in['adap_bias'], 'L0_conv_atrous_bias': _L0_conv_in['atrous_bias'], 'L0_conv_fuse_w': _L0_conv_in['fuse_w'], 'L0_conv_fuse_b': _L0_conv_in['fuse_b'], 'L2_attn_Wq': _L2_attn_in['Wq'], 'L2_attn_bq': _L2_attn_in['bq'], 'L2_attn_Wk': _L2_attn_in['Wk'], 'L2_attn_bk': _L2_attn_in['bk'], 'L2_attn_Wv': _L2_attn_in['Wv'], 'L2_attn_bv': _L2_attn_in['bv'], 'L2_attn_Wo': _L2_attn_in['Wo'], 'L2_attn_bo': _L2_attn_in['bo'], 'L2_ffn_router_w': _L2_ffn_in['router_w'], 'L2_ffn_w_gate': _L2_ffn_in['w_gate'], 'L2_ffn_w_up': _L2_ffn_in['w_up'], 'L2_ffn_w_down': _L2_ffn_in['w_down'], 'L3_attn_Wq': _L3_attn_in['Wq'], 'L3_attn_Wkv': _L3_attn_in['Wkv'], 'L3_ffn_Wg': _L3_ffn_in['Wg'], 'L3_ffn_W': _L3_ffn_in['W'], 'L3_ffn_V': _L3_ffn_in['V'], 'L3_ffn_W2': _L3_ffn_in['W2']}

def reference(x, L0_conv_conv_w, L0_conv_conv_b, L0_conv_conv_k_w, L0_conv_conv_k_b, L0_conv_conv_k2_w, L0_conv_conv_k2_b, L0_conv_conv_kernel_w, L0_conv_conv_kernel_b, L0_conv_conv_kernel2_w, L0_conv_conv_kernel2_b, L0_conv_adap_bias, L0_conv_atrous_bias, L0_conv_fuse_w, L0_conv_fuse_b, L2_attn_Wq, L2_attn_bq, L2_attn_Wk, L2_attn_bk, L2_attn_Wv, L2_attn_bv, L2_attn_Wo, L2_attn_bo, L2_ffn_router_w, L2_ffn_w_gate, L2_ffn_w_up, L2_ffn_w_down, L3_attn_Wq, L3_attn_Wkv, L3_ffn_Wg, L3_ffn_W, L3_ffn_V, L3_ffn_W2):
    import jax
    import jax.numpy as jnp

    def _L0_conv_ref(x, conv_w, conv_b, conv_k_w, conv_k_b, conv_k2_w, conv_k2_b, conv_kernel_w, conv_kernel_b, conv_kernel2_w, conv_kernel2_b, adap_bias, atrous_bias, fuse_w, fuse_b):
        import jax, jax.numpy as jnp
        from jax import lax
        import numpy as np
        N, C, H, W = x.shape
        Cm = conv_w.shape[0]
        kk = conv_kernel_w.shape[0]
        k = int(round(kk ** 0.5))
        pad = (k - 1) // 2
        cw = conv_w[:, :, 0, 0]
        f = jax.nn.relu(jnp.einsum('nchw,oc->nohw', x, cw) + conv_b[None, :, None, None])
        g = jax.nn.relu(jnp.einsum('nc,oc->no', x.mean((2, 3)), cw) + conv_b)
        wk = conv_kernel_w[:, 0, 0, 0]
        K_img = g[:, :, None] * wk[None, None, :] + conv_kernel_b[None, None, :]
        K_dom = K_img.mean(0)
        gk = jax.nn.relu(conv_k_w[0, 0, 0, 0] * K_img + conv_k_w[0, 1, 0, 0] * K_dom[None] + conv_k_b[0])
        Wd = gk.reshape(N * Cm, 1, k, k)
        wk2 = conv_kernel2_w[:, 0, 0, 0]
        K2_img = g[:, :, None] * wk2[None, None, :] + conv_kernel2_b[None, None, :]
        K2_dom = K2_img.mean(0)
        gk2 = jax.nn.relu(conv_k2_w[0, 0, 0, 0] * K2_img + conv_k2_w[0, 1, 0, 0] * K2_dom[None] + conv_k2_b[0])
        W2 = gk2.reshape(N * Cm, 1, 3, 3)
        fr = f.reshape(1, N * Cm, H, W)
        y1 = lax.conv_general_dilated(fr, Wd, (1, 1), [(pad, pad), (pad, pad)], feature_group_count=N * Cm)
        y1 = y1.reshape(N, Cm, H, W) + adap_bias[None, :, None, None]
        y2 = lax.conv_general_dilated(fr, W2, (1, 1), [(2, 2), (2, 2)], rhs_dilation=(2, 2), feature_group_count=N * Cm)
        y2 = y2.reshape(N, Cm, H, W) + atrous_bias[None, :, None, None]
        y = jnp.concatenate([y1, y2], axis=1)
        out = jnp.einsum('nchw,oc->nohw', y, fuse_w[:, :, 0, 0]) + fuse_b[None, :, None, None]
        return out

    def _L1_conv_ref(x):
        import jax, jax.numpy as jnp
        import numpy as np
        C = x.shape[1]
        kernel = jnp.ones((C, 1, 3, 3), dtype=x.dtype)
        return jax.lax.conv_general_dilated(x, kernel, window_strides=(1, 1), padding=((1, 1), (1, 1)), dimension_numbers=('NCHW', 'OIHW', 'NCHW'), feature_group_count=C)

    def _L2_attn_ref(inputs, Wq, bq, Wk, bk, Wv, bv, Wo, bo):
        import jax, jax.numpy as jnp
        import numpy as np
        EMBED_DIM = 128
        NUM_HEADS = 8
        HEAD_DIM = EMBED_DIM // NUM_HEADS

        def _split_heads(x, B, S):
            return x.reshape(B, S, NUM_HEADS, HEAD_DIM).transpose(0, 2, 1, 3)
        B, S, D = inputs.shape
        q = _split_heads(inputs @ Wq + bq, B, S)
        k = _split_heads(inputs @ Wk + bk, B, S)
        v = _split_heads(inputs @ Wv + bv, B, S)
        scale = 1.0 / jnp.sqrt(jnp.asarray(HEAD_DIM, dtype=inputs.dtype))
        scores = jnp.einsum('bhqd,bhkd->bhqk', q, k) * scale
        weights = jax.nn.softmax(scores, axis=-1)
        attn = jnp.einsum('bhqk,bhkd->bhqd', weights, v)
        attn = attn.transpose(0, 2, 1, 3).reshape(B, S, D)
        return attn @ Wo + bo

    def _L2_ffn_ref(x, router_w, w_gate, w_up, w_down):
        import jax, jax.numpy as jnp
        import numpy as np
        B, S, D, H, E, K = (2, 512, 128, 256, 8, 2)

        def _moe(x, router_w, w_gate, w_up, w_down):
            bsz, seq, d = x.shape
            flat = x.reshape(-1, d)
            logits = flat @ router_w.T
            topk_vals, topk_idx = jax.lax.top_k(logits, K)
            topk_w = jax.nn.softmax(topk_vals, axis=-1)
            s = flat.shape[0]
            dense_w = jnp.zeros((s, E), dtype=flat.dtype).at[jnp.arange(s)[:, None], topk_idx].add(topk_w)
            g = jnp.einsum('sd,edh->esh', flat, w_gate)
            u = jnp.einsum('sd,edh->esh', flat, w_up)
            y = jnp.einsum('esh,ehd->esd', jax.nn.silu(g) * u, w_down)
            out = jnp.einsum('esd,se->sd', y, dense_w)
            return out.reshape(bsz, seq, d)
        return _moe(x, router_w, w_gate, w_up, w_down)

    def _L3_attn_ref(x, Wq, Wkv):
        import jax, jax.numpy as jnp
        import numpy as np
        NUM_HEADS = 8
        EPS = 1e-06
        B, N, C = x.shape
        h = NUM_HEADS
        d = C // h
        q = (x @ Wq.T).reshape(B, N, h, d)
        kv = (x @ Wkv.T).reshape(B, N, 2, h, d)
        k = kv[:, :, 0]
        v = kv[:, :, 1]
        Q = jax.nn.elu(q) + 1.0
        K = jax.nn.elu(k) + 1.0
        v_length = v.shape[1]
        v = v / v_length
        KV = jnp.einsum('nshd,nshv->nhdv', K, v)
        Z = 1.0 / (jnp.einsum('nlhd,nhd->nlh', Q, K.sum(axis=1)) + EPS)
        out = jnp.einsum('nlhd,nhdv,nlh->nlhv', Q, KV, Z) * v_length
        return out.reshape(B, N, C)

    def _L3_ffn_ref(x, Wg, W, V, W2):
        import jax, jax.numpy as jnp
        import numpy as np
        B, S, D, F, E, K = (4, 512, 128, 512, 8, 2)
        gate_logits = jnp.einsum('bsd,de->bse', x, Wg)
        topv, topi = jax.lax.top_k(gate_logits, K)
        w = jax.nn.softmax(topv, axis=-1)
        gw = jnp.sum(w[..., None] * jax.nn.one_hot(topi, E, dtype=x.dtype), axis=-2)
        y = jnp.zeros_like(x)
        n_experts = W.shape[0]
        for e in range(n_experts):
            h = jax.nn.silu(jnp.einsum('bsd,df->bsf', x, W[e])) * jnp.einsum('bsd,df->bsf', x, V[e])
            y = y + gw[..., e:e + 1] * jnp.einsum('bsf,fd->bsd', h, W2[e])
        return y

    def _gn(v, G=32, eps=1e-05):
        B_, C_, H_, W_ = v.shape
        g = v.reshape(B_, G, C_ // G, H_, W_)
        m = jnp.mean(g, axis=(2, 3, 4), keepdims=True)
        s = jnp.var(g, axis=(2, 3, 4), keepdims=True)
        return ((g - m) / jnp.sqrt(s + eps)).reshape(v.shape)

    def _ln_c(v, eps=1e-06):
        m = jnp.mean(v, axis=1, keepdims=True)
        s = jnp.var(v, axis=1, keepdims=True)
        return (v - m) / jnp.sqrt(s + eps)

    def _ln_t(v, eps=1e-05):
        m = jnp.mean(v, axis=-1, keepdims=True)
        s = jnp.var(v, axis=-1, keepdims=True)
        return (v - m) / jnp.sqrt(s + eps)

    def _to_tokens(v):
        B_, C_, H_, W_ = v.shape
        return v.reshape(B_, C_, H_ * W_).transpose(0, 2, 1)

    def _from_tokens(t, like):
        B_, C_, H_, W_ = like.shape
        return t.transpose(0, 2, 1).reshape(B_, C_, H_, W_)
    x = x + _L0_conv_ref(_gn(x), L0_conv_conv_w, L0_conv_conv_b, L0_conv_conv_k_w, L0_conv_conv_k_b, L0_conv_conv_k2_w, L0_conv_conv_k2_b, L0_conv_conv_kernel_w, L0_conv_conv_kernel_b, L0_conv_conv_kernel2_w, L0_conv_conv_kernel2_b, L0_conv_adap_bias, L0_conv_atrous_bias, L0_conv_fuse_w, L0_conv_fuse_b)
    x = x + _L1_conv_ref(_gn(x))
    t = _to_tokens(x)
    t = t + _L2_attn_ref(_ln_t(t), L2_attn_Wq, L2_attn_bq, L2_attn_Wk, L2_attn_bk, L2_attn_Wv, L2_attn_bv, L2_attn_Wo, L2_attn_bo)
    t = t + _L2_ffn_ref(_ln_t(t), L2_ffn_router_w, L2_ffn_w_gate, L2_ffn_w_up, L2_ffn_w_down)
    t = t + _L3_attn_ref(_ln_t(t), L3_attn_Wq, L3_attn_Wkv)
    t = t + _L3_ffn_ref(_ln_t(t), L3_ffn_Wg, L3_ffn_W, L3_ffn_V, L3_ffn_W2)
    x = _from_tokens(t, x)
    return x

_drawn_inputs = setup_inputs


def setup_inputs(seed=0):
    import zlib

    import numpy as np

    out = dict(_drawn_inputs(seed))
    spreads = {'L2_attn_bq': (0.0, 0.8),
     'L2_attn_bk': (0.0, 2.0),
     'L2_attn_bv': (0.0, 0.1),
     'L2_attn_bo': (0.0, 0.1)}
    factors = {'L0_conv_conv_b': 4.505,
     'L0_conv_conv_k2_w': 41.327,
     'L0_conv_conv_kernel2_w': 8.0,
     'L0_conv_conv_kernel2_b': 8.0,
     'L3_attn_Wq': 8.0,
     'L3_ffn_Wg': 8.0,
     'L3_ffn_W': 8.0,
     'L3_ffn_V': 8.0,
     'L3_ffn_W2': 8.0}
    for name, (base, spread) in spreads.items():
        noise = np.random.default_rng([zlib.crc32(name.encode()), seed]).standard_normal(out[name].shape)
        drawn = base * np.exp(spread * noise) if base else spread * noise
        out[name] = jnp.asarray(drawn.astype(out[name].dtype))
    for name, factor in factors.items():
        out[name] = (out[name] * factor).astype(out[name].dtype)
    return out
```

```python
from contextlib import ExitStack

import concourse.bass as bass
from concourse import mybir

F32 = mybir.dt.float32
F32R = mybir.dt.float32r
U32 = mybir.dt.uint32
I32 = mybir.dt.int32
ALU = mybir.AluOpType
ACT = mybir.ActivationFunctionType
AX_X = mybir.AxisListType.X

P = 128
N, C, H, W = 16, 128, 16, 16
PIX = H * W
TOK = N * PIX
TILES = TOK // P
GN_GROUP = C // 32
CM = 32
QUADS = P // CM
KS = 5
TAP_TILES = 7
FR, FC = 21, 20
GN_EPS, LN_EPS = 1e-5, 1e-5


def tap_of(t, quad):
    if t < KS:
        return (t, quad), True
    if t == KS:
        return (quad, KS - 1), True
    return (KS - 1, KS - 1), quad == QUADS - 1


class Chain:

    def __init__(self, eng, sem, base=0):
        self.eng, self.sem, self.n = eng, sem, base

    def __call__(self, ins):
        ins.then_inc(self.sem, 1)
        self.n = self.n + 1
        self.eng.wait_ge(self.sem, self.n)


class Kit:

    used = []

    def __init__(self, nc, ctx):
        self.nc, self.ctx = nc, ctx

    def sb(self, name, shape, dt=F32):
        return self.ctx.enter_context(self.nc.sbuf_tensor(name, shape, dt))

    def sem(self, name):
        s = self.ctx.enter_context(self.nc.semaphore(name))
        Kit.used.append(s)
        return s


def clear_semaphores(nc):
    numbers = sorted(s.num for s in Kit.used)
    assert numbers[-1] - numbers[0] + 1 == len(numbers)
    Kit.used.clear()
    with nc.Block() as block:
        @block.gpsimd
        def _(pool):
            nc.gpsimd.sem_clear(range(numbers[0], numbers[-1] + 1))


def channel_means(nc, step, stats, out):
    step(nc.vector.tensor_tensor(out, stats[:, :, 1], stats[:, :, 4], ALU.add))
    return nc.vector.tensor_scalar(out, out, 0.5, None, ALU.mult)


def variances(nc, step, stats, tmp, out, count):
    step(nc.vector.tensor_tensor(tmp, stats[:, :, 1], stats[:, :, 4], ALU.subtract))
    step(nc.vector.scalar_tensor_tensor(tmp, tmp, 0.25, tmp, ALU.mult, ALU.mult))
    step(nc.vector.tensor_tensor(out, stats[:, :, 2], stats[:, :, 5], ALU.add))
    return nc.vector.scalar_tensor_tensor(out, out, 1.0 / count, tmp, ALU.mult, ALU.add)


def adaptive_conv(nc, top, x_dram, cw_dram, cb_dram, f1_dram, f2_dram, fuse_dram, ab_dram, fb_dram,
                  taps_dram, scal_dram):
    X, ps = top.X, top.ps
    with ExitStack() as ctx:
        k = Kit(nc, ctx)
        xn = top.T[:].rearrange("p t c -> p (t c)")
        cw = k.sb("cw", [P, P])
        cb = k.sb("cb", [P, 1])
        f1 = k.sb("f1", [P, P])
        f2 = k.sb("f2", [P, P])
        fuse = k.sb("fuse", [2 * CM, P])
        ab = k.sb("ab", [2 * CM, 1])
        fb = k.sb("fb", [P, 1])
        taps = k.sb("taps", [P, 4, TAP_TILES])
        scal = k.sb("scal", [P, 6])
        gavg = top.gavg
        stats = k.sb("stats", [P, N, 6])
        mean_c = k.sb("mean_c", [P, N])
        dev = k.sb("dev", [P, N])
        sq = k.sb("sq", [P, N])
        pooled = k.sb("pooled", [P, N])
        g = k.sb("g", [P, N])
        kimg = k.sb("kimg", [P, N, TAP_TILES])
        kdom = k.sb("kdom", [P, TAP_TILES])
        counts = k.sb("counts", [P, 2, TAP_TILES])
        gk = k.sb("gk", [P, 2, N, TAP_TILES])
        cbias = k.sb("cbias", [P, 1])
        wimg = k.sb("wimg", [P, 2, TAP_TILES, P])
        fcol = k.sb("fcol", [P, N, FR * FC])
        frow = k.sb("frow", [P, N, FR * FC])
        fcol_v = fcol[:].rearrange("p n (r c) -> p n r c", c=FC)
        frow_v = frow[:].rearrange("p n (r c) -> p n r c", c=FC)
        x_in = [k.sem(f"x_in{i}") for i in range(4)]
        w_in, taps_in = k.sem("w_in"), k.sem("taps_in")
        pool_chain, dve_chain = k.sem("pool_chain_a"), k.sem("dve_chain_a")
        consts_ready, pads_ready = k.sem("consts_ready"), k.sem("pads_ready")
        mean_ready, mean_ps, var_ready, var_ps = (k.sem(s) for s in ("mean_rd", "mean_ps", "var_rd", "var_ps"))
        std_ready, xn_ready = k.sem("std_ready"), k.sem("xn_ready")
        pooled_ready, g_ps, g_ready, bias_ps = (k.sem(s) for s in ("pooled_rd", "g_ps", "g_rd", "bias_ps"))
        feat_ps, feat_act, feat_dve = k.sem("feat_ps"), k.sem("feat_act"), k.sem("feat_dve")
        wimg_ready, wimg_used, out_read = (k.sem(s) for s in ("wimg_rd", "wimg_used", "out_read"))
        wimg_half = k.sem("wimg_half")

        MEAN, VAR = ps[:, 4, 0:N], ps[:, 4, N:2 * N]
        G, BIAS = ps[:, 5, 0:N], ps[:, 5, N:N + 1]

        block = ctx.enter_context(nc.Block())

        @block.sync
        def _(sp):
            for i in range(4):
                sp.dma_start(X[:, i * (TOK // 4):(i + 1) * (TOK // 4)],
                             x_dram[:, i * (TOK // 4):(i + 1) * (TOK // 4)]).then_inc(x_in[i], 16)
            for dst, src in ((cw, cw_dram), (cb, cb_dram), (f1, f1_dram), (f2, f2_dram), (fuse, fuse_dram),
                             (ab, ab_dram), (fb, fb_dram)):
                sp.dma_start(dst[:], src).then_inc(w_in, 16)
            sp.dma_start(taps[:], taps_dram).then_inc(taps_in, 16)
            sp.dma_start(scal[:], scal_dram.partition_broadcast(P)).then_inc(taps_in, 16)

        @block.gpsimd
        def _(pool):
            step = Chain(pool, pool_chain)
            step(nc.gpsimd.memset(top.ident[:], 1.0))
            step(nc.gpsimd.affine_select(out=top.ident[:], in_=top.ident[:], compare_op=ALU.is_equal, fill=0.0,
                                         base=0, pattern=[[-1, P]], channel_multiplier=1))
            step(nc.gpsimd.memset(gavg[:], 1.0 / GN_GROUP))
            gv = gavg[:].rearrange("p (g r) -> p g r", r=GN_GROUP)
            step(nc.gpsimd.affine_select(out=gv, in_=gv, compare_op=ALU.is_ge, fill=0.0, base=0,
                                         pattern=[[-GN_GROUP, P // GN_GROUP], [0, GN_GROUP]], channel_multiplier=1))
            nc.gpsimd.affine_select(out=gv, in_=gv, compare_op=ALU.is_ge, fill=0.0, base=GN_GROUP - 1,
                                    pattern=[[GN_GROUP, P // GN_GROUP], [0, GN_GROUP]],
                                    channel_multiplier=-1).then_inc(consts_ready, 1)
            nc.gpsimd.memset(fcol[:], 0.0).then_inc(pads_ready, 1)

        @block.scalar
        def _(act):
            act.wait_ge(var_ps, 1)
            act.wait_ge(std_ready, 1)
            nc.scalar.activation(top.rstd[:], VAR, ACT.Sqrt, bias=top.eps5[:]).then_inc(std_ready, 1)
            act.wait_ge(w_in, 7 * 16)
            act.wait_ge(pads_ready, 2)
            with act.Fori(0, N // 4) as i:
                for b in range(2):
                    act.wait_ge(feat_ps, 2 * i + b + 1)
                    src = ps[:, b, :].rearrange("p (n r c) -> p n r c", n=2, c=W)
                    for q in range(3):
                        rows = slice(q * CM, (q + 1) * CM)
                        for dst, r0, c0 in ((fcol_v, 3, 3 - q), (frow_v, 3 - q, 2)):
                            o = dst[rows, bass.ds(4 * i + 2 * b, 2), r0:r0 + H, c0:c0 + W]
                            last = nc.scalar.activation(o, src[rows], ACT.Relu, bias=cb[rows])
                    last.then_inc(feat_act, 1)

        @block.tensor
        def _(pe):
            pe.wait_ge(mean_ready, 1)
            pe.wait_ge(consts_ready, 1)
            nc.tensor.matmul(MEAN, gavg[:], mean_c[:], start=True, stop=True).then_inc(mean_ps, 1)
            pe.wait_ge(var_ready, 1)
            nc.tensor.matmul(VAR, gavg[:], sq[:], start=True, stop=True).then_inc(var_ps, 1)
            pe.wait_ge(w_in, 7 * 16)
            pe.wait_ge(pooled_ready, 1)
            nc.tensor.matmul(G, cw[:], pooled[:], start=True, stop=True).then_inc(g_ps, 1)
            pe.wait_ge(g_ready, 1)
            nc.tensor.matmul(BIAS, fuse[:], ab[:], start=True, stop=True).then_inc(bias_ps, 1)

            def features(pair, b):
                nc.tensor.matmul(ps[:, b, :], cw[:], xn[:, bass.ds(pair * 2 * PIX, 2 * PIX)],
                                 start=True, stop=True).then_inc(feat_ps, 1)

            def convolve(pair, b):
                for a in range(2):
                    pe.wait_ge(wimg_ready, 2 * pair + a + 1)
                    for t in range(TAP_TILES):
                        src, r0, c0 = (fcol_v, 1 + t, 1) if t < KS else (frow_v, 1 + t - KS, KS - 1)
                        rhs = src[:, bass.ds(2 * pair + a, 1), r0:r0 + H, c0:c0 + W]
                        last = nc.tensor.matmul(ps[:, 2 + b, a * PIX:(a + 1) * PIX], wimg[:, a, t, :],
                                                rhs.rearrange("p n r c -> p (n r) c"),
                                                start=(t == 0), stop=(t == TAP_TILES - 1))
                    last.then_inc(wimg_used, 1)

            pe.wait_ge(xn_ready, 8)
            for b in range(2):
                features(b, b)
            with pe.Fori(0, N // 4 - 1) as i:
                for b in range(2):
                    pair = 2 * i + b
                    pe.wait_ge(feat_act, pair + 1)
                    pe.wait_ge(feat_dve, pair + 1)
                    pe.wait_ge(out_read, pair + 1)
                    convolve(pair, b)
                    features(pair + 2, b)
            for b in range(2):
                pair = N // 2 - 2 + b
                pe.wait_ge(feat_act, pair + 1)
                pe.wait_ge(feat_dve, pair + 1)
                pe.wait_ge(out_read, pair + 1)
                convolve(pair, b)

        @block.vector
        def _(dve):
            step = Chain(dve, dve_chain)
            nc.vector.memset(top.eps5[:], GN_EPS).then_inc(std_ready, 1)
            nc.vector.memset(frow[:], 0.0).then_inc(pads_ready, 1)
            step(nc.vector.memset(counts[:, 0, :], 1.0))
            step(nc.vector.memset(counts[:, 1, :], 0.0))
            for q in range(QUADS):
                for t in range(TAP_TILES):
                    (row, col), real = tap_of(t, q)
                    rows = slice(q * CM, (q + 1) * CM)
                    if not real:
                        step(nc.vector.memset(counts[rows, 0, t:t + 1], 0.0))
                    elif row % 2 == 0 and col % 2 == 0:
                        step(nc.vector.memset(counts[rows, 1, t:t + 1], 1.0))
            for n in range(N):
                if n % 4 == 0:
                    dve.wait_ge(x_in[n // 4], 16)
                last = nc.vector.bn_stats(stats[:, n, :], X[:, n * PIX:(n + 1) * PIX])
            step(last)
            channel_means(nc, step, stats, mean_c[:]).then_inc(mean_ready, 1)
            dve.wait_ge(mean_ready, 1)
            step(variances(nc, step, stats, dev[:], sq[:], PIX))
            dve.wait_ge(mean_ps, 1)
            step(nc.vector.tensor_copy(top.mean[:], MEAN))
            step(nc.vector.tensor_tensor(dev[:], mean_c[:], top.mean[:], ALU.subtract))
            step(nc.vector.tensor_tensor(dev[:], dev[:], dev[:], ALU.mult))
            nc.vector.tensor_tensor(sq[:], sq[:], dev[:], ALU.add).then_inc(var_ready, 1)
            dve.wait_ge(std_ready, 2)
            step(nc.vector.reciprocal(top.rstd[:], top.rstd[:]))
            step(nc.vector.tensor_tensor(pooled[:], mean_c[:], top.mean[:], ALU.subtract))
            nc.vector.tensor_tensor(pooled[:], pooled[:], top.rstd[:], ALU.mult).then_inc(pooled_ready, 1)
            with dve.Fori(0, 8) as i:
                for a in range(2):
                    n = 2 * i + a
                    last = nc.vector.tensor_scalar(
                        xn[:, bass.ds(n * PIX, PIX)], X[:, bass.ds(n * PIX, PIX)], top.mean[:, bass.ds(n, 1)],
                        top.rstd[:, bass.ds(n, 1)], ALU.subtract, ALU.mult)
                last.then_inc(xn_ready, 1)
            dve.wait_ge(g_ps, 1)
            dve.wait_ge(w_in, 7 * 16)
            dve.wait_ge(taps_in, 2 * 16)
            nc.vector.tensor_scalar(g[:], G, cb[:], 0.0, ALU.add, ALU.max).then_inc(g_ready, 1)
            dve.wait_ge(g_ready, 1)
            for m in range(2):
                each = lambda ap: ap.unsqueeze(1).broadcast_to([P, N, TAP_TILES])
                step(nc.vector.tensor_tensor(kimg[:], g[:].unsqueeze(2).broadcast_to([P, N, TAP_TILES]),
                                             each(taps[:, 2 * m, :]), ALU.mult))
                step(nc.vector.tensor_tensor(kimg[:], kimg[:], each(taps[:, 2 * m + 1, :]), ALU.add))
                step(nc.vector.tensor_reduce(kdom[:], kimg[:].rearrange("p n t -> p t n"), AX_X, ALU.add))
                step(nc.vector.tensor_scalar(kdom[:], kdom[:], 1.0 / N, scal[:, 3 * m + 1:3 * m + 2],
                                             ALU.mult, ALU.mult))
                step(nc.vector.tensor_scalar(kdom[:], kdom[:], scal[:, 3 * m + 2:3 * m + 3], None, ALU.add))
                step(nc.vector.scalar_tensor_tensor(kimg[:], kimg[:], scal[:, 3 * m:3 * m + 1], each(kdom[:]),
                                                    ALU.mult, ALU.add))
                step(nc.vector.scalar_tensor_tensor(gk[:, m, :, :], kimg[:], 0.0, each(counts[:, m, :]),
                                                    ALU.max, ALU.mult))
            dve.wait_ge(bias_ps, 1)
            step(nc.vector.tensor_tensor(cbias[:], BIAS, fb[:], ALU.add))
            dve.wait_ge(pads_ready, 2)

            def quadrant_three(pair, b):
                dve.wait_ge(feat_ps, pair + 1)
                rows = slice(3 * CM, 4 * CM)
                src = ps[:, b, :].rearrange("p (n r c) -> p n r c", n=2, c=W)
                for dst, r0, c0 in ((fcol_v, 3, 0), (frow_v, 0, 2)):
                    for a in range(2):
                        o = dst[rows, bass.ds(2 * pair + a, 1), r0:r0 + H, c0:c0 + W]
                        last = nc.vector.tensor_scalar(o.rearrange("p n r c -> p (n r) c"), src[rows, a], cb[rows],
                                                       0.0, ALU.add, ALU.max)
                last.then_inc(feat_dve, 1)

            def stationary(pair, a):
                n = 2 * pair + a
                dve.wait_ge(wimg_used, n + 1)
                for t in range(TAP_TILES):
                    last = nc.vector.tensor_scalar(wimg[:, a, t, :], f1[:], gk[:, 0, bass.ds(n, 1), t], None, ALU.mult)
                last.then_inc(wimg_half, 1)
                dve.wait_ge(wimg_half, n + 1)
                for t in (0, 2, 4, 5, 6):
                    last = nc.vector.scalar_tensor_tensor(wimg[:, a, t, :], f2[:], gk[:, 1, bass.ds(n, 1), t],
                                                          wimg[:, a, t, :], ALU.mult, ALU.add)
                last.then_inc(wimg_ready, 1)

            def outputs(pair, b):
                dve.wait_ge(wimg_used, 2 * pair + 4)
                at = X[:, bass.ds(pair * 2 * PIX, 2 * PIX)]
                nc.vector.scalar_tensor_tensor(at, ps[:, 2 + b, :], cbias[:], at, ALU.add,
                                               ALU.add).then_inc(out_read, 1)
                dve.wait_ge(out_read, pair + 3)
                for a in range(2):
                    n = 2 * pair + a
                    nc.vector.bn_stats(top.gn_stats[:, bass.ds(n, 1), :].rearrange("p a s -> p (a s)"),
                                       X[:, bass.ds(n * PIX, PIX)])

            dve.sem_inc(wimg_used, 2)
            dve.sem_inc(out_read, 2)
            for b in range(2):
                quadrant_three(b, b)
            for a in range(2):
                stationary(0, a)
            with dve.Fori(0, N // 4 - 1) as i:
                for b in range(2):
                    for a in range(2):
                        stationary(2 * i + b + 1, a)
                    outputs(2 * i + b, b)
                    quadrant_three(2 * i + b + 2, b)
            for a in range(2):
                stationary(N // 2 - 1, a)
            outputs(N // 2 - 2, 0)
            outputs(N // 2 - 1, 1)


def box_conv(nc, top):
    X, T, ps = top.X, top.T, top.ps
    PH, PW = H + 2, W + 2
    with ExitStack() as ctx:
        k = Kit(nc, ctx)
        mean_c = k.sb("mean_c2", [P, N])
        dev = k.sb("dev2", [P, N])
        sq = k.sb("sq2", [P, N])
        shift = k.sb("shift", [P, N])
        pad = k.sb("pad", [P, 2, PH * PW])
        rows = k.sb("rows", [P, 2, PH * W])
        mid = k.sb("mid", [P, 2, PIX])
        gavg = top.gavg
        dve_chain = k.sem("dve_chain_b")
        mean_ready, mean_ps, var_ready, var_ps, std_ready, norm_ready = (
            k.sem(s) for s in ("b_mean_rd", "b_mean_ps", "b_var_rd", "b_var_ps", "b_std_rd", "b_norm_rd"))
        pad_ready, rows_half, rows_ready, mid_ready, tok_ps, tok_ready = (
            k.sem(s) for s in ("pad_rd", "rows_half", "rows_rd", "mid_rd", "tok_ps", "tok_rd"))
        MEAN, VAR = ps[:, 4, 0:N], ps[:, 4, N:2 * N]
        image = lambda n: X[:, bass.ds(n * PIX, PIX)]

        block = ctx.enter_context(nc.Block())

        @block.scalar
        def _(act):
            act.wait_ge(var_ps, 1)
            nc.scalar.activation(top.rstd[:], VAR, ACT.Sqrt, bias=top.eps5[:]).then_inc(std_ready, 1)
            act.wait_ge(norm_ready, 1)

            def normed(n, b):
                act.wait_ge(rows_ready, n + 1)
                inner = pad[:, b, :].rearrange("p (r c) -> p r c", c=PW)[:, 1:1 + H, 1:1 + W]
                nc.scalar.activation(inner, image(n).rearrange("p (r c) -> p r c", c=W), ACT.Identity,
                                     bias=shift[:, bass.ds(n, 1)],
                                     scale=top.rstd[:, bass.ds(n, 1)]).then_inc(pad_ready, 1)

            def tokens(n, b):
                act.wait_ge(tok_ps, n + 3)
                nc.scalar.activation(T[:, bass.ds(2 * n, 2), :].rearrange("p t c -> p (t c)"),
                                     ps[:, b, 0:2 * P], ACT.Copy).then_inc(tok_ready, 1)

            act.sem_inc(tok_ready, 2)
            for b in range(2):
                normed(b, b)
            with act.Fori(0, N // 2 - 1) as i:
                for b in range(2):
                    normed(2 * i + b + 2, b)
                    tokens(2 * i + b, b)
            for b in range(2):
                tokens(N - 2 + b, b)

        @block.gpsimd
        def _(pool):
            with pool.Fori(0, N // 2) as i:
                for b in range(2):
                    n = 2 * i + b
                    pool.wait_ge(rows_ready, n + 3)
                    pool.wait_ge(tok_ps, n + 1)
                    nc.gpsimd.tensor_tensor(mid[:, b, :], image(n), rows[:, b, W:W + PIX],
                                            ALU.add).then_inc(mid_ready, 1)

        @block.tensor
        def _(pe):
            pe.wait_ge(mean_ready, 1)
            nc.tensor.matmul(MEAN, gavg[:], mean_c[:], start=True, stop=True).then_inc(mean_ps, 1)
            pe.wait_ge(var_ready, 1)
            nc.tensor.matmul(VAR, gavg[:], sq[:], start=True, stop=True).then_inc(var_ps, 1)
            pe.sem_inc(tok_ps, 2)
            with pe.Fori(0, N // 2) as i:
                for b in range(2):
                    n = 2 * i + b
                    pe.wait_ge(mid_ready, n + 1)
                    pe.wait_ge(tok_ready, n + 1)
                    for half in range(2):
                        o = ps[:, b, half * P:(half + 1) * P]
                        at = half * P
                        nc.tensor.matmul(o, rows[:, b, at:at + P], top.ident[:], start=True, stop=False)
                        nc.tensor.matmul(o, rows[:, b, at + 2 * W:at + 2 * W + P], top.ident[:], start=False, stop=False)
                        last = nc.tensor.matmul(o, mid[:, b, at:at + P], top.ident[:], start=False, stop=True)
                    last.then_inc(tok_ps, 1)

        @block.vector
        def _(dve):
            step = Chain(dve, dve_chain)
            stats = top.gn_stats
            nc.vector.memset(pad[:], 0.0).then_inc(rows_ready, 2)
            channel_means(nc, step, stats, mean_c[:]).then_inc(mean_ready, 1)
            dve.wait_ge(mean_ready, 1)
            step(variances(nc, step, stats, dev[:], sq[:], PIX))
            dve.wait_ge(mean_ps, 1)
            step(nc.vector.tensor_copy(top.mean[:], MEAN))
            step(nc.vector.tensor_tensor(dev[:], mean_c[:], top.mean[:], ALU.subtract))
            step(nc.vector.tensor_tensor(dev[:], dev[:], dev[:], ALU.mult))
            nc.vector.tensor_tensor(sq[:], sq[:], dev[:], ALU.add).then_inc(var_ready, 1)
            dve.wait_ge(std_ready, 1)
            step(nc.vector.reciprocal(top.rstd[:], top.rstd[:]))
            nc.vector.scalar_tensor_tensor(shift[:], top.mean[:], -1.0, top.rstd[:], ALU.mult,
                                           ALU.mult).then_inc(norm_ready, 1)

            def row_sums(n, b):
                dve.wait_ge(pad_ready, n + 1)
                dve.wait_ge(tok_ps, n + 1)
                p = pad[:, b, :].rearrange("p (r c) -> p r c", c=PW)
                o = rows[:, b, :].rearrange("p (r c) -> p r c", c=W)
                nc.vector.tensor_tensor(o, p[:, :, 0:W], p[:, :, 1:1 + W], ALU.add).then_inc(rows_half, 1)
                dve.wait_ge(rows_half, n + 1)
                nc.vector.tensor_tensor(o, o, p[:, :, 2:2 + W], ALU.add).then_inc(rows_ready, 1)

            def statistics(n):
                dve.wait_ge(tok_ready, n + 3)
                token_statistics(nc, top, n)

            row_sums(0, 0)
            row_sums(1, 1)
            with dve.Fori(0, N // 2 - 1) as i:
                for b in range(2):
                    row_sums(2 * i + b + 2, b)
                    statistics(2 * i + b)
            for b in range(2):
                statistics(N - 2 + b)


def prepare_norm(nc, top, block, k, tag):
    chain, var_ready, std_ready, norm_ready = (
        k.sem(f"{tag}_{s}") for s in ("ln_chain", "ln_var_rd", "ln_std_rd", "ln_rd"))
    tmp = k.sb(f"{tag}_ln_tmp", [P, TILES])

    def on_vector(dve):
        step = Chain(dve, chain)
        step(channel_means(nc, step, top.ln_stats, top.ln_mean[:]))
        variances(nc, step, top.ln_stats, tmp[:], top.ln_rstd[:], C).then_inc(var_ready, 1)
        dve.wait_ge(std_ready, 1)
        nc.vector.reciprocal(top.ln_rstd[:], top.ln_rstd[:]).then_inc(norm_ready, 1)
        dve.wait_ge(norm_ready, 1)

    def on_scalar(act):
        act.wait_ge(var_ready, 1)
        nc.scalar.activation(top.ln_rstd[:], top.ln_rstd[:], ACT.Sqrt, bias=top.eps5[:]).then_inc(std_ready, 1)

    return on_vector, on_scalar


def wait_apart(eng, sem, value, passed):
    eng.wait_ge(sem, value)
    eng.sem_inc(passed, 1)


def image_loop(eng, body, ahead=0):
    body(0, 0, True, False)
    with eng.Fori(0, (N - 2) // 2) as i:
        for b in (1, 2):
            body(2 * i + b, b % 2, False, False)
    body(N - 1, (N - 1) % 2, False, True)


def softmax_attention(nc, top, wq_dram, wk_dram, wv_dram, wo_dram, bq_dram, bk_dram, bv_dram, bo_dram):
    T, ps, ident = top.T, top.ps, top.ident
    NH, HD = 8, 16
    HG = 4
    SCALE = HD ** -0.5
    ROW_MAX = HD
    with ExitStack() as ctx:
        k = Kit(nc, ctx)
        wq = k.sb("wq", [P, 2, P])
        wk = k.sb("wk", [P, 2, P])
        wv = k.sb("wv", [P, P])
        wo = k.sb("wo", [P, P])
        bq = k.sb("bq", [P, 2])
        bk = k.sb("bk", [P, 2])
        bv = k.sb("bv", [P, 1])
        bo = k.sb("bo", [P, 2, P])
        upper = k.sb("upper", [P, 1])
        lower = k.sb("lower", [P, 1])
        one_row = k.sb("one_row", [P, 1])
        bq_up = k.sb("bq_up", [P, 2])
        bq_low = k.sb("bq_low", [P, 2])
        xn = k.sb("xn_c", [P, 2, 2, C])
        xT = k.sb("xT_c", [P, 2, PIX])
        q_low = k.sb("q_low", [P, 2, 2, PIX], F32R)
        q_up = k.sb("q_up", [P, 2, 2, PIX], F32R)
        qa = k.sb("qa", [P, 2, 2, PIX], F32R)
        qb = k.sb("qb", [P, 2, 2, PIX], F32R)
        ka = k.sb("ka", [P, 2, 2, PIX], F32R)
        kl = k.sb("kl", [P, 2, 2, PIX])
        kb = k.sb("kb", [P, 2, 2, PIX], F32R)
        negmax = k.sb("negmax", [P, 2, 2, P])
        vaug = k.sb("vaug", [P, 2, 2, NH, 32])
        prob = k.sb("prob", [P, NH, 2, PIX])
        heads_T = k.sb("heads_T", [P, 2, PIX])
        inv = k.sb("inv", [P, 2 * NH])
        heads = k.sb("heads", [P, 2, P])
        att = k.sb("att", [P, PIX])
        w_in, masks_ready, chain, chain2, zeros_ready = (
            k.sem(f"c_{s}") for s in ("w_in", "masks", "chain", "chain2", "zeros"))
        xn_ready, xT_ps, xT_ready, q_ps, k_ps, v_ps = (
            k.sem(f"c_{s}") for s in ("xn_rd", "xT_ps", "xT_rd", "q_ps", "k_ps", "v_ps"))
        q_halves, qa_ready, ka_ready, kl_ready, kb_ready, v_ready = (
            k.sem(f"c_{s}") for s in ("q_halves", "qa_rd", "ka_rd", "kl_rd", "kb_rd", "v_rd"))
        max_ps, max_ready, maxT_ps, qb_ready, score_ps, prob_ready = (
            k.sem(f"c_{s}") for s in ("max_ps", "max_rd", "maxT_ps", "qb_rd", "score_ps", "prob_rd"))
        passed_pool = k.sem("c_passed_pool")
        pv_ps, headsT_ready, heads_ps, inv_ready, heads_ready, att_ps, att_ready, out_ps, bo_added, tok_ready = (
            k.sem(f"c_{s}") for s in ("pv_ps", "headsT_rd", "heads_ps", "inv_rd", "heads_rd", "att_ps", "att_rd",
                                      "out_ps", "bo_added", "tok_rd"))

        Q = ps[:, 4, :].rearrange("p (g t) -> p g t", g=2)
        K = ps[:, 5, :].rearrange("p (g t) -> p g t", g=2)
        MAXT = K
        PV = ps[:, 6, :].rearrange("p (g t) -> p g t", g=2)
        HEADS = ps[:, 6, :].rearrange("p (t g c) -> p t g c", t=2, g=2)
        ATT = ps[:, 6, 0:PIX]
        OUT = ps[:, 6, PIX:2 * PIX]
        XT = ps[:, 7, 0:PIX]
        V = ps[:, 7, PIX:2 * PIX]

        block = ctx.enter_context(nc.Block())
        norm_on_vector, norm_on_scalar = prepare_norm(nc, top, block, k, "c")

        @block.sync
        def _(sp):
            for dst, src in ((wq, wq_dram), (wk, wk_dram)):
                sp.dma_start(dst[:].rearrange("p g c -> p (g c)"), src).then_inc(w_in, 16)
            for dst, src in ((wv, wv_dram), (wo, wo_dram), (bq, bq_dram), (bk, bk_dram), (bv, bv_dram)):
                sp.dma_start(dst[:], src).then_inc(w_in, 16)
            for t in range(2):
                sp.dma_start(bo[:, t, :], bo_dram.partition_broadcast(P)).then_inc(w_in, 16)

        @block.gpsimd
        def _(pool):
            nc.gpsimd.memset(vaug[:, 1], 0.0).then_inc(chain2, 1)
            pool.wait_ge(chain2, 1)
            nc.gpsimd.memset(vaug[:, 1, :, :, 0:1], 1.0).then_inc(zeros_ready, 1)
            pool.wait_ge(masks_ready, 1)
            pool.wait_ge(w_in, 9 * 16)

            def keys_low(n, b, first, last):
                wait_apart(pool, kl_ready, n + 1, passed_pool)
                nc.gpsimd.tensor_scalar(kb[:, b], kl[:, b], upper[:], one_row[:], ALU.mult,
                                        ALU.add).then_inc(kb_ready, 1)
                pool.wait_ge(xn_ready, n + 1)
                t = T[:, bass.ds(2 * n, 2), :]
                nc.gpsimd.tensor_tensor(t, t, bo[:], ALU.add).then_inc(bo_added, 1)

            image_loop(pool, keys_low)

        @block.scalar
        def _(act):
            norm_on_scalar(act)
            act.wait_ge(w_in, 9 * 16)
            act.wait_ge(masks_ready, 1)
            act.wait_ge(zeros_ready, 2)

            def transposed(m, b):
                act.wait_ge(xT_ps, m + 1)
                nc.scalar.activation(xT[:, b, :], XT, ACT.Copy).then_inc(xT_ready, 1)

            def queries(m, b):
                act.wait_ge(q_ps, m + 1)
                for g in range(2):
                    nc.scalar.activation(q_low[:, b, g], Q[:, g], ACT.Identity, bias=bq_low[:, g:g + 1], scale=lower[:])
                for g in range(2):
                    last = nc.scalar.activation(q_up[:, b, g], Q[:, g], ACT.Identity, bias=bq_up[:, g:g + 1],
                                                scale=upper[:])
                last.then_inc(q_halves, 1)

            def keys(m, b):
                act.wait_ge(k_ps, m + 1)
                for g in range(2):
                    last = nc.scalar.activation(ka[:, b, g], K[:, g], ACT.Identity, bias=bk[:, g:g + 1])
                last.then_inc(ka_ready, 1)

            def values(m, b):
                act.wait_ge(v_ps, m + 1)
                nc.scalar.activation(vaug[:, b, :, :, 1:1 + HD],
                                     V.rearrange("p (t h d) -> p t h d", t=2, d=HD), ACT.Copy).then_inc(v_ready, 1)

            def exps(n, h, first):
                act.wait_ge(score_ps, NH * n + h + 1)
                if not first:
                    act.wait_ge(pv_ps, 2 * n - 1 + h // HG)
                nc.scalar.activation(prob[:, h].rearrange("p t q -> p (t q)"), ps[:, h % 2, :], ACT.Exp,
                                     scale=SCALE).then_inc(prob_ready, 1)

            transposed(0, 0)
            queries(0, 0)
            keys(0, 0)
            values(0, 0)

            def unnormed(n):
                act.wait_ge(pv_ps, 2 * n + 2)
                nc.scalar.activation(heads_T[:], PV, ACT.Copy).then_inc(headsT_ready, 1)

            def attention(n):
                act.wait_ge(att_ps, n + 1)
                nc.scalar.activation(att[:], ATT, ACT.Identity, bias=bv[:]).then_inc(att_ready, 1)

            def image(n, b, first, last):
                exps(n, 0, first)
                if not last:
                    transposed(n + 1, 1 - b)
                exps(n, 1, first)
                if not last:
                    queries(n + 1, 1 - b)
                exps(n, 2, first)
                if not first:
                    attention(n - 1)
                if not last:
                    keys(n + 1, 1 - b)
                exps(n, 3, first)
                if not last:
                    values(n + 1, 1 - b)
                for h in range(4, NH):
                    exps(n, h, first)
                unnormed(n)

            image_loop(act, image)
            attention(N - 1)

        @block.tensor
        def _(pe):
            pe.wait_ge(w_in, 9 * 16)

            def transpose(m, b, first=False):
                pe.wait_ge(xn_ready, m + 1)
                if not first:
                    pe.wait_ge(v_ready, m)
                for t in range(2):
                    last = nc.tensor.transpose(XT[:, t * P:(t + 1) * P], xn[:, b, t, :], ident[:])
                last.then_inc(xT_ps, 1)

            def project_q(m, b):
                pe.wait_ge(xT_ready, m + 1)
                for g in range(2):
                    last = nc.tensor.matmul(Q[:, g], wq[:, g, :], xT[:, b, :], start=True, stop=True)
                last.then_inc(q_ps, 1)

            def project_k(m, b):
                for g in range(2):
                    last = nc.tensor.matmul(K[:, g], wk[:, g, :], xT[:, b, :], start=True, stop=True)
                last.then_inc(k_ps, 1)

            def project_v(m, b):
                for t in range(2):
                    last = nc.tensor.matmul(V[:, t * P:(t + 1) * P], xT[:, b, t * P:(t + 1) * P], wv[:],
                                            start=True, stop=True)
                last.then_inc(v_ps, 1)

            def max_scores(m, b, h, first=False):
                g, rows = h // HG, slice(32 * (h % HG), 32 * (h % HG) + 32)
                if h == 0:
                    pe.wait_ge(qa_ready, m + 1)
                    pe.wait_ge(ka_ready, m + 1)
                if not first or h >= 2:
                    pe.wait_ge(max_ready, NH * m + h - 1)
                for t in range(2):
                    last = nc.tensor.matmul(ps[:, 2 + h % 2, t * PIX:(t + 1) * PIX],
                                            qa[rows, b, g, t * P:(t + 1) * P], ka[rows, b, g, :],
                                            start=True, stop=True)
                last.then_inc(max_ps, 1)

            def transpose_maxima(n):
                pe.wait_ge(max_ready, NH * n + NH)
                pe.wait_ge(kb_ready, n + 1)
                for g in range(2):
                    for t in range(2):
                        last = nc.tensor.transpose(MAXT[:, g, t * P:(t + 1) * P], negmax[:, t, g, :], ident[:])
                last.then_inc(maxT_ps, 1)

            def scores(n, b, h, first):
                g, rows = h // HG, slice(32 * (h % HG), 32 * (h % HG) + 32)
                if h == 0:
                    pe.wait_ge(qb_ready, n + 1)
                if not first or h >= 2:
                    pe.wait_ge(prob_ready, NH * n + h - 1)
                for t in range(2):
                    o = ps[:, h % 2, t * PIX:(t + 1) * PIX]
                    keys = slice(t * P, (t + 1) * P)
                    nc.tensor.matmul(o, ka[rows, b, g, keys], qa[rows, b, g, :], start=True, stop=False)
                    last = nc.tensor.matmul(o, kb[rows, b, g, keys], qb[rows, b, g, :], start=False, stop=True)
                last.then_inc(score_ps, 1)

            def probs_v(n, b, g, first):
                pe.wait_ge(prob_ready, NH * n + HG * (g + 1))
                pe.wait_ge(v_ready, n + 1)
                if g == 0 and not first:
                    pe.wait_ge(tok_ready, n)
                for t in range(2):
                    for j in range(HG):
                        last = nc.tensor.matmul(PV[32 * j:32 * j + 32, g, :], vaug[:, b, t, HG * g + j, :],
                                                prob[:, HG * g + j, t, :], start=(t == 0), stop=(t == 1),
                                                skip_group_check=True)
                last.then_inc(pv_ps, 1)

            def heads_to_tokens(n):
                pe.wait_ge(headsT_ready, n + 1)
                for t in range(2):
                    for g in range(2):
                        last = nc.tensor.transpose(HEADS[:, t, g, :], heads_T[:, g, t * P:(t + 1) * P], ident[:])
                last.then_inc(heads_ps, 1)

            def heads_to_channels(n):
                pe.wait_ge(heads_ready, n + 1)
                for t in range(2):
                    last = nc.tensor.transpose(ATT[:, t * P:(t + 1) * P], heads[:, t, :], ident[:])
                last.then_inc(att_ps, 1)

            def output(n):
                pe.wait_ge(att_ready, n + 1)
                for t in range(2):
                    last = nc.tensor.matmul(OUT[:, t * C:(t + 1) * C], att[:, t * P:(t + 1) * P], wo[:],
                                            start=True, stop=True)
                last.then_inc(out_ps, 1)

            transpose(0, 0, True)
            project_q(0, 0)
            project_k(0, 0)
            project_v(0, 0)
            for h in range(NH):
                max_scores(0, 0, h, True)

            def image(n, b, first, last):
                transpose_maxima(n)
                if not first:
                    heads_to_tokens(n - 1)
                scores(n, b, 0, first)
                if not last:
                    transpose(n + 1, 1 - b)
                scores(n, b, 1, first)
                if not last:
                    project_q(n + 1, 1 - b)
                if not first:
                    heads_to_channels(n - 1)
                scores(n, b, 2, first)
                if not last:
                    project_k(n + 1, 1 - b)
                    project_v(n + 1, 1 - b)
                scores(n, b, 3, first)
                if not first:
                    output(n - 1)
                if not last:
                    max_scores(n + 1, 1 - b, 0)
                scores(n, b, 4, first)
                if not last:
                    max_scores(n + 1, 1 - b, 1)
                probs_v(n, b, 0, first)
                for h in range(5, NH):
                    if not last:
                        max_scores(n + 1, 1 - b, h - 3)
                    scores(n, b, h, first)
                if not last:
                    max_scores(n + 1, 1 - b, 5)
                probs_v(n, b, 1, first)
                if not last:
                    max_scores(n + 1, 1 - b, 6)
                    max_scores(n + 1, 1 - b, 7)

            image_loop(pe, image)
            heads_to_tokens(N - 1)
            heads_to_channels(N - 1)
            output(N - 1)

        @block.vector
        def _(dve):
            step = Chain(dve, chain)
            nc.vector.memset(vaug[:, 0, :, :, 1:], 0.0)
            nc.vector.memset(vaug[:, 0, :, :, 0:1], 1.0).then_inc(zeros_ready, 1)
            nc.vector.memset(negmax[:], 0.0)
            norm_on_vector(dve)
            rows = ident[:].rearrange("p (j r) -> p j r", r=32)
            XY = mybir.AxisListType.XY
            nc.vector.tensor_reduce(upper[:], rows[:, :, 0:HD], XY, ALU.add)
            nc.vector.tensor_reduce(lower[:], rows[:, :, HD:32], XY, ALU.add)
            step(nc.vector.tensor_reduce(one_row[:], rows[:, :, ROW_MAX:ROW_MAX + 1], XY, ALU.add))
            dve.wait_ge(w_in, 9 * 16)
            nc.vector.tensor_scalar(bq_up[:], bq[:], upper[:], None, ALU.mult)
            nc.vector.tensor_scalar(bq_low[:], bq[:], lower[:], None, ALU.mult).then_inc(masks_ready, 1)

            def normed(m, b):
                for t in range(2):
                    tile = 2 * m + t
                    last = nc.vector.tensor_scalar(
                        xn[:, b, t, :], T[:, bass.ds(tile, 1), :].rearrange("p t c -> p (t c)"),
                        top.ln_mean[:, bass.ds(tile, 1)], top.ln_rstd[:, bass.ds(tile, 1)], ALU.subtract, ALU.mult)
                last.then_inc(xn_ready, 1)

            def queries(m, b):
                dve.wait_ge(q_halves, m + 1)
                for g in range(2):
                    last = nc.vector.scalar_tensor_tensor(qa[:, b, g], Q[:, g], bq[:, g:g + 1], q_low[:, b, g],
                                                          ALU.add, ALU.subtract)
                last.then_inc(qa_ready, 1)

            def keys(m, b):
                dve.wait_ge(ka_ready, m + 1)
                for g in range(2):
                    last = nc.vector.scalar_tensor_tensor(kl[:, b, g], K[:, g], bk[:, g:g + 1], ka[:, b, g],
                                                          ALU.add, ALU.subtract)
                last.then_inc(kl_ready, 1)

            def maxima(m, h):
                dve.wait_ge(max_ps, NH * m + h + 1)
                col = 32 * (h % HG) + ROW_MAX
                nc.vector.tensor_reduce(negmax[:, :, h // HG, col:col + 1],
                                        ps[:, 2 + h % 2, :].rearrange("p (t k) -> p t k", t=2), AX_X, ALU.max,
                                        negate=True).then_inc(max_ready, 1)

            def queries_low(n, b):
                dve.wait_ge(maxT_ps, n + 1)
                nc.vector.tensor_tensor(qb[:, b], MAXT, q_up[:, b], ALU.add).then_inc(qb_ready, 1)

            def normalise(n):
                dve.wait_ge(heads_ps, n + 1)
                h = ps[:, 6, :].rearrange("p (h r) -> p h r", r=32)
                nc.vector.reciprocal(inv[:], h[:, :, 0]).then_inc(inv_ready, 1)
                dve.wait_ge(inv_ready, n + 1)
                nc.vector.tensor_tensor(heads[:].rearrange("p t (h d) -> p (t h) d", d=HD), h[:, :, 1:1 + HD],
                                        inv[:].unsqueeze(2).broadcast_to([P, 2 * NH, HD]),
                                        ALU.mult).then_inc(heads_ready, 1)

            def add_output(n):
                dve.wait_ge(out_ps, n + 1)
                dve.wait_ge(bo_added, n + 1)
                t = T[:, bass.ds(2 * n, 2), :].rearrange("p t c -> p (t c)")
                nc.vector.tensor_tensor(t, OUT, t, ALU.add).then_inc(tok_ready, 1)
                dve.wait_ge(tok_ready, n + 1)
                token_statistics(nc, top, n)

            normed(0, 0)
            queries(0, 0)
            keys(0, 0)
            for h in range(NH):
                maxima(0, h)

            def image(n, b, first, last):
                queries_low(n, b)
                if not last:
                    normed(n + 1, 1 - b)
                if not first:
                    normalise(n - 1)
                if not last:
                    queries(n + 1, 1 - b)
                    keys(n + 1, 1 - b)
                    maxima(n + 1, 0)
                if not first:
                    add_output(n - 1)
                if not last:
                    for h in range(1, NH):
                        maxima(n + 1, h)

            image_loop(dve, image)
            normalise(N - 1)
            add_output(N - 1)


def token_statistics(nc, top, n):
    for a in range(2):
        t = 2 * n + a
        last = nc.vector.bn_stats(top.ln_stats[:, bass.ds(t, 1), :].rearrange("p a s -> p (a s)"),
                                  top.T[:, bass.ds(t, 1), :].rearrange("p a c -> p (a c)"))
    return last


def linear_attention(nc, top, wq_dram, wkv_dram):
    T, ps, ident = top.T, top.ps, top.ident
    NH, HD = 8, 16
    EPS = 1e-6
    AW = C + NH
    with ExitStack() as ctx:
        k = Kit(nc, ctx)
        wq = k.sb("e_wq", [P, C])
        wkv = k.sb("e_wkv", [P, 2 * C])
        own = k.sb("e_own", [P, AW])
        xn = k.sb("e_xn", [P, 2, 2, C])
        xT = k.sb("e_xT", [P, 2, PIX])
        q_exp = k.sb("e_q_exp", [P, PIX])
        q_pos = k.sb("e_q_pos", [P, PIX])
        q = k.sb("e_q", [P, 2, PIX])
        k_exp = k.sb("e_k_exp", [P, 2, C])
        k_pos = k.sb("e_k_pos", [P, 2, C])
        kf = k.sb("e_k", [P, 2, 2, C])
        v = k.sb("e_v", [P, 2, 2, C + 1])
        kv = k.sb("e_kv", [P, 2, AW])
        inv = k.sb("e_inv", [P, 2, NH])
        heads = k.sb("e_heads", [P, 2, 2, C])
        w_in, chain, chain_pool, own_ready, ones_ready = (
            k.sem(f"e_{s}") for s in ("w_in", "chain", "chain_pool", "own_rd", "ones_rd"))
        xn_ready, xT_ps, xT_ready, q_ps, kv_ps, q_parts, kv_parts, qf_ready, kf_ready = (
            k.sem(f"e_{s}") for s in ("xn_rd", "xT_ps", "xT_rd", "q_ps", "kv_ps", "q_parts", "kv_parts",
                                      "qf_rd", "kf_rd"))
        sum_ps, sum_ready, out_ps, inv_ready, heads_ready, tok_ready = (
            k.sem(f"e_{s}") for s in ("sum_ps", "sum_rd", "out_ps", "inv_rd", "heads_rd", "tok_rd"))

        XT = lambda b: ps[:, 4 * b, 0:PIX]
        Q = lambda b: ps[:, 4 * b, PIX:2 * PIX]
        KV = lambda b: ps[:, 4 * b + 1, :].rearrange("p (t w c) -> p t w c", t=2, w=2)
        SUM = lambda b: ps[:, 4 * b + 2, 0:C + 1]
        OUT = lambda b: ps[:, 4 * b + 3, 0:2 * AW].rearrange("p (t c) -> p t c", t=2)

        block = ctx.enter_context(nc.Block())
        norm_on_vector, norm_on_scalar = prepare_norm(nc, top, block, k, "e")

        @block.sync
        def _(sp):
            sp.dma_start(wq[:], wq_dram).then_inc(w_in, 16)
            sp.dma_start(wkv[:], wkv_dram).then_inc(w_in, 16)

        @block.gpsimd
        def _(pool):
            step = Chain(pool, chain_pool)
            nc.gpsimd.memset(v[:, :, :, C:], 1.0).then_inc(ones_ready, 1)
            step(nc.gpsimd.memset(own[:], 1.0))
            for cols, width in ((own[:, 0:C].rearrange("p (h d) -> p h d", d=HD), HD),
                                (own[:, C:].unsqueeze(2), 1)):
                step(nc.gpsimd.affine_select(out=cols, in_=cols, compare_op=ALU.is_ge, fill=0.0, base=0,
                                             pattern=[[-HD, NH], [0, width]], channel_multiplier=1))
                step(nc.gpsimd.affine_select(out=cols, in_=cols, compare_op=ALU.is_ge, fill=0.0, base=HD - 1,
                                             pattern=[[HD, NH], [0, width]], channel_multiplier=-1))
            nc.gpsimd.memset(top.pool_scratch[:], 0.0).then_inc(own_ready, 1)

            def add_output(n, b, first, last):
                pool.wait_ge(heads_ready, n + 1)
                t = T[:, bass.ds(2 * n, 2), :]
                nc.gpsimd.tensor_tensor(t, t, heads[:, b], ALU.add).then_inc(tok_ready, 1)

            image_loop(pool, add_output)

        @block.scalar
        def _(act):
            norm_on_scalar(act)
            act.wait_ge(ones_ready, 1)

            def transposed(m, b):
                act.wait_ge(xT_ps, m + 1)
                nc.scalar.activation(xT[:, b, :], XT(b), ACT.Copy).then_inc(xT_ready, 1)

            def parts(m, b, first):
                act.wait_ge(q_ps, m + 1)
                if not first:
                    act.wait_ge(qf_ready, m)
                nc.scalar.activation(q_exp[:], Q(b), ACT.Exp)
                nc.scalar.activation(q_pos[:], Q(b), ACT.Relu).then_inc(q_parts, 1)
                act.wait_ge(kv_ps, m + 1)
                if not first:
                    act.wait_ge(kf_ready, m)
                nc.scalar.activation(k_exp[:], KV(b)[:, :, 0, :], ACT.Exp)
                nc.scalar.activation(k_pos[:], KV(b)[:, :, 0, :], ACT.Relu)
                nc.scalar.activation(v[:, b, :, 0:C], KV(b)[:, :, 1, :], ACT.Copy).then_inc(kv_parts, 1)

            def image(n, b, first, last):
                if not last:
                    transposed(n + 1, 1 - b)
                parts(n, b, first)

            transposed(0, 0)
            image_loop(act, image)

        @block.tensor
        def _(pe):
            pe.wait_ge(w_in, 2 * 16)

            def transpose(m, b):
                pe.wait_ge(xn_ready, m + 1)
                for t in range(2):
                    last = nc.tensor.transpose(XT(b)[:, t * P:(t + 1) * P], xn[:, b, t, :], ident[:])
                last.then_inc(xT_ps, 1)

            def project(n, b):
                pe.wait_ge(xT_ready, n + 1)
                nc.tensor.matmul(Q(b), wq[:], xT[:, b, :], start=True, stop=True).then_inc(q_ps, 1)
                for t in range(2):
                    last = nc.tensor.matmul(KV(b)[:, t].rearrange("p w c -> p (w c)"), xT[:, b, t * P:(t + 1) * P],
                                            wkv[:], start=True, stop=True)
                last.then_inc(kv_ps, 1)

            def sum_tokens(n, b):
                pe.wait_ge(kf_ready, n + 1)
                for t in range(2):
                    last = nc.tensor.matmul(SUM(b), kf[:, b, t, :], v[:, b, t, :], start=(t == 0), stop=(t == 1))
                last.then_inc(sum_ps, 1)

            def output(n, b):
                pe.wait_ge(sum_ready, n + 1)
                for t in range(2):
                    last = nc.tensor.matmul(OUT(b)[:, t, :], q[:, b, t * P:(t + 1) * P], kv[:, b, :],
                                            start=True, stop=True)
                last.then_inc(out_ps, 1)

            def image(n, b, first, last):
                if not last:
                    transpose(n + 1, 1 - b)
                project(n, b)
                if not first:
                    output(n - 1, 1 - b)
                sum_tokens(n, b)

            transpose(0, 0)
            image_loop(pe, image)
            output(N - 1, 1)

        @block.vector
        def _(dve):
            norm_on_vector(dve)
            dve.wait_ge(own_ready, 1)

            def normed(m, b):
                for t in range(2):
                    tile = 2 * m + t
                    last = nc.vector.tensor_scalar(
                        xn[:, b, t, :], T[:, bass.ds(tile, 1), :].rearrange("p t c -> p (t c)"),
                        top.ln_mean[:, bass.ds(tile, 1)], top.ln_rstd[:, bass.ds(tile, 1)], ALU.subtract, ALU.mult)
                last.then_inc(xn_ready, 1)

            def features(n, b):
                dve.wait_ge(q_parts, n + 1)
                nc.vector.scalar_tensor_tensor(q[:, b, :], q_exp[:], 1.0, q_pos[:], ALU.min,
                                               ALU.add).then_inc(qf_ready, 1)
                dve.wait_ge(kv_parts, n + 1)
                nc.vector.scalar_tensor_tensor(kf[:, b], k_exp[:], 1.0, k_pos[:], ALU.min,
                                               ALU.add).then_inc(kf_ready, 1)

            def sums(n, b):
                dve.wait_ge(sum_ps, n + 1)
                nc.vector.tensor_tensor(kv[:, b, 0:C], SUM(b)[:, 0:C], own[:, 0:C], ALU.mult)
                nc.vector.tensor_scalar(kv[:, b, C:], own[:, C:], SUM(b)[:, C:], None, ALU.mult).then_inc(sum_ready, 1)

            def normalise(n, b):
                dve.wait_ge(out_ps, n + 1)
                nc.vector.tensor_scalar(inv[:], OUT(b)[:, :, C:], EPS, None, ALU.add).then_inc(inv_ready, 1)
                dve.wait_ge(inv_ready, 2 * n + 1)
                nc.vector.reciprocal(inv[:], inv[:]).then_inc(inv_ready, 1)
                dve.wait_ge(inv_ready, 2 * n + 2)
                for t in range(2):
                    last = nc.vector.tensor_tensor(
                        heads[:, b, t, :].rearrange("p (h d) -> p h d", d=HD),
                        OUT(b)[:, t, 0:C].rearrange("p (h d) -> p h d", d=HD),
                        inv[:, t, :].unsqueeze(2).broadcast_to([P, NH, HD]), ALU.mult)
                last.then_inc(heads_ready, 1)

            def statistics(n):
                dve.wait_ge(tok_ready, n + 1)
                token_statistics(nc, top, n)

            def image(n, b, first, last):
                if not last:
                    normed(n + 1, 1 - b)
                features(n, b)
                if not first:
                    normalise(n - 1, 1 - b)
                sums(n, b)
                if not first:
                    statistics(n - 1)

            normed(0, 0)
            image_loop(dve, image)
            normalise(N - 1, 1)
            statistics(N - 1)


class Step:

    def __init__(self, i, c):
        self.i, self.c = i, c

    def __add__(self, d):
        return Step(self.i, self.c + d)

    @property
    def n(self):
        return 2 * self.i + self.c

    @property
    def half(self):
        return self.i + self.c // 2

    @property
    def b(self):
        return self.c % 2

    @property
    def reuses(self):
        return not (isinstance(self.i, int) and self.c < 2)


def pipeline(eng, stages, items):
    lags = [lag for lag, _ in stages]
    full = max(lags) + 1, items - 2 + min(lags)
    full = full[0], full[0] + (full[1] + 1 - full[0]) // 2 * 2

    def step(at, known=None):
        for lag, body in stages:
            item = None if known is None else known - lag
            if item is None or 0 <= item < items:
                body(at + -lag, item == 0, item == items - 1)

    for s in range(min(lags), full[0]):
        step(Step(0, s), s)
    with eng.Fori(0, (full[1] - full[0]) // 2) as i:
        for c in range(2):
            step(Step(i, full[0] + c))
    for s in range(full[1], items + max(lags)):
        step(Step(0, s), s)


class Moe:

    E, TOP = 8, 2
    SLOT_TILES = -(-(TOP * TOK + E * (P - 1)) // P) // 2 * 2

    def __init__(self, nc, k, hidden, tag):
        self.F = hidden
        self.tag = tag
        self.w_in, self.w_out = (k.sb(f"{tag}_{s}", shape) for s, shape in
                                 (("w_in", [P, self.E, 2 * hidden]), ("w_out", [P, self.E, hidden // P, C])))
        self.gather = k.sb(f"{tag}_gather", [P, self.SLOT_TILES], U32)
        self.scatter = k.sb(f"{tag}_scatter", [P, self.SLOT_TILES], U32)
        self.expert = k.sb(f"{tag}_expert", [P, self.SLOT_TILES], I32)
        self.weight = k.sb(f"{tag}_weight", [P, self.TOP, TILES])
        self.weights_in = k.sem(f"{tag}_weights_in")
        self.xn_dram = nc.dram_tensor(f"{tag}_normed", [TOK, C], F32, kind="Internal").ap()
        self.y_dram = nc.dram_tensor(f"{tag}_results", [TOK * self.TOP, C], F32, kind="Internal").ap()


def route(nc, top, moe, router_dram, w_in_dram, w_out_dram):
    T, ps, ident = top.T, top.ps, top.ident
    E, SLOT_TILES = moe.E, moe.SLOT_TILES
    GROUP = 4
    NEVER = 4.0 * TOK
    tag = moe.tag
    with ExitStack() as ctx:
        k = Kit(nc, ctx)
        sb = lambda name, shape, dt=F32: k.sb(f"{tag}_{name}", shape, dt)
        sem = lambda *names: [k.sem(f"{tag}_{s}") for s in names]
        router = sb("router", [P, E])
        xn = top.X[:].rearrange("p (t c) -> p t c", c=C)
        xT = sb("xT", [P, 2, GROUP * P])
        logits = sb("logits", [P, TILES, E])
        rest = sb("rest", [P, TILES, E])
        same = sb("same", [P, TILES, E])
        chosen = sb("chosen", [P, 2, TILES, E])
        both = sb("both", [P, TILES, E])
        best = sb("best", [P, 2, TILES])
        rank = sb("rank", [P, TILES])
        ratio = sb("ratio", [P, TILES])
        scan = sb("scan", [P, 2, TILES, E])
        total = sb("total", [P, TILES, E])
        place = sb("place", [P, TILES, E])
        beyond = sb("beyond", [P, E, TILES])
        used = sb("used", [P, E])
        ends = sb("ends", [P, 2, E])
        base = sb("base", [P, E])
        slot = sb("slot", [P, 2, TILES])
        slot_i = sb("slot_i", [P, 2, TILES], I32)
        part_i = sb("part_i", [P, 2, 2, TILES], I32)
        part = sb("part", [P, 2, 2, TILES])
        passed = sb("passed", [P, SLOT_TILES, E])
        tile_expert = sb("tile_expert", [P, SLOT_TILES])
        descending = sb("descending", [P, E])
        up_to = sb("up_to", [P, P])
        multiples = sb("multiples", [P, TILES])
        number = sb("number", [P, TILES])
        before = sb("before", [P, P])
        ones = sb("ones", [P, P])
        column = sb("column", [P, 2, 2, SLOT_TILES], F32R)
        row = sb("row", [P, 2, 2, P], F32R)
        found = sb("found", [P, 2, SLOT_TILES])
        token = sb("token", [P, SLOT_TILES])
        empty = sb("empty", [P, SLOT_TILES])
        target = sb("target", [P, SLOT_TILES])
        router_in, xn_stored, chain, chain_pool, consts_ready = sem(
            "router_in", "xn_stored", "chain", "chain_pool", "consts_rd")
        xn_ready, xT_ps, xT_ready, logit_ps, logit_ready = sem("xn_rd", "xT_ps", "xT_rd", "logit_ps", "logit_rd")
        gap_ready, ratio_ready, both_ready, count_ps, hot_ready, table_ps = sem(
            "gap_rd", "ratio_rd", "both_rd", "count_ps", "hot_rd", "table_ps")

        PLACE = ps[:, 4, 0:TILES * E]
        TOTAL = ps[:, 4, TILES * E:2 * TILES * E]
        FOUND = ps[:, 5:7, 0:SLOT_TILES]

        block = ctx.enter_context(nc.Block())
        norm_on_vector, norm_on_scalar = prepare_norm(nc, top, block, k, tag)

        @block.sync
        def _(sp):
            sp.dma_start(router[:], router_dram).then_inc(router_in, 16)
            groups = moe.xn_dram.rearrange("(g t p) c -> g p t c", p=P, t=GROUP)
            for g in range(TILES // GROUP):
                sp.wait_ge(xn_ready, g + 1)
                sp.dma_start(groups[g], xn[:, g * GROUP:(g + 1) * GROUP, :]).then_inc(xn_stored, 16)
            for dst, src in ((moe.w_in, w_in_dram), (moe.w_out, w_out_dram)):
                sp.dma_start(dst[:], src).then_inc(moe.weights_in, 16)
            sp.wait_ge(xn_stored, 16 * (TILES // GROUP))

        @block.gpsimd
        def _(pool):
            step = Chain(pool, chain_pool)
            whole = dict(allow_small_or_imprecise_dtypes=True)
            nc.gpsimd.iota(up_to[:], pattern=[[1, P]], base=0, channel_multiplier=0, **whole)
            nc.gpsimd.iota(descending[:], pattern=[[-1, E]], base=E, channel_multiplier=0, **whole)
            nc.gpsimd.iota(multiples[:], pattern=[[P, TILES]], base=0, channel_multiplier=0, **whole)
            nc.gpsimd.iota(number[:], pattern=[[P, TILES]], base=1, channel_multiplier=1, **whole)
            nc.gpsimd.memset(ones[:], 1.0)
            step(nc.gpsimd.memset(before[:], 1.0))
            nc.gpsimd.affine_select(out=before[:], in_=before[:], compare_op=ALU.is_ge, fill=0.0, base=-1,
                                    pattern=[[1, P]], channel_multiplier=-1).then_inc(consts_ready, 1)

        @block.scalar
        def _(act):
            norm_on_scalar(act)
            with act.Fori(0, TILES // GROUP // 2) as i:
                for b in range(2):
                    g = 2 * i + b
                    act.wait_ge(xT_ps, g + 1)
                    act.wait_ge(logit_ps, g + 1)
                    nc.scalar.activation(xT[:, b, :], ps[:, b, :], ACT.Copy).then_inc(xT_ready, 1)
                    act.wait_ge(logit_ps, g + 3)
                    nc.scalar.activation(logits[:, bass.ds(g * GROUP, GROUP), :].rearrange("p t e -> p (t e)"),
                                         ps[:, 2 + b, 0:GROUP * E], ACT.Copy).then_inc(logit_ready, 1)
            act.wait_ge(gap_ready, 1)
            nc.scalar.activation(ratio[:], rank[:], ACT.Exp).then_inc(ratio_ready, 1)

        @block.tensor
        def _(pe):
            pe.wait_ge(router_in, 16)
            pe.sem_inc(logit_ps, 2)
            pe.sem_inc(xT_ready, 2)
            for g in range(TILES // GROUP):
                b = g % 2
                pe.wait_ge(xn_ready, g + 1)
                pe.wait_ge(xT_ready, g + 1)
                for t in range(GROUP):
                    last = nc.tensor.transpose(ps[:, b, t * P:(t + 1) * P], xn[:, g * GROUP + t, :], ident[:])
                last.then_inc(xT_ps, 1)
                pe.wait_ge(xT_ready, g + 3)
                for t in range(GROUP):
                    last = nc.tensor.matmul(ps[:, 2 + b, t * E:(t + 1) * E], xT[:, b, t * P:(t + 1) * P],
                                            router[:], start=True, stop=True)
                last.then_inc(logit_ps, 1)
            pe.wait_ge(consts_ready, 1)
            pe.wait_ge(both_ready, 1)
            m = both[:].rearrange("p t e -> p (t e)")
            nc.tensor.matmul(PLACE, before[:], m, start=True, stop=True)
            nc.tensor.matmul(TOTAL, ones[:], m, start=True, stop=True).then_inc(count_ps, 1)
            pe.sem_inc(table_ps, 2)

            def add_tile(at, first, last):
                pe.wait_ge(hot_ready, at.n + 1)
                for c in range(2):
                    ins = nc.tensor.matmul(FOUND[:, c, :], row[:, at.b, c, :], column[:, at.b, c, :],
                                           start=first, stop=last, skip_group_check=True)
                ins.then_inc(table_ps, 1)

            pipeline(pe, [(0, add_tile)], TILES)

        @block.vector
        def _(dve):
            step = Chain(dve, chain)
            norm_on_vector(dve)
            with dve.Fori(0, TILES // GROUP) as g:
                for t in range(GROUP):
                    tile = g * GROUP + t
                    last = nc.vector.tensor_scalar(
                        xn[:, bass.ds(tile, 1), :].rearrange("p t c -> p (t c)"),
                        T[:, bass.ds(tile, 1), :].rearrange("p t c -> p (t c)"),
                        top.ln_mean[:, bass.ds(tile, 1)], top.ln_rstd[:, bass.ds(tile, 1)], ALU.subtract, ALU.mult)
                last.then_inc(xn_ready, 1)
            dve.wait_ge(consts_ready, 1)
            dve.wait_ge(logit_ready, TILES // GROUP)
            by_tile = lambda ap: ap.unsqueeze(2).broadcast_to([P, TILES, E])
            by_expert = lambda ap: ap.unsqueeze(1).broadcast_to([P, TILES, E])
            for c, left in enumerate((logits, rest)):
                step(nc.vector.tensor_reduce(best[:, c], left[:], AX_X, ALU.max))
                step(nc.vector.tensor_tensor(same[:], left[:], by_tile(best[:, c]), ALU.is_equal))
                step(nc.vector.tensor_tensor(same[:], same[:], by_expert(descending[:]), ALU.mult))
                step(nc.vector.tensor_reduce(rank[:], same[:], AX_X, ALU.max))
                step(nc.vector.tensor_tensor(chosen[:, c], by_expert(descending[:]), by_tile(rank[:]), ALU.is_equal))
                if c == 0:
                    step(nc.vector.scalar_tensor_tensor(rest[:], chosen[:, 0], -1e30, logits[:], ALU.mult, ALU.add))
            nc.vector.tensor_tensor(both[:], chosen[:, 0], chosen[:, 1], ALU.add).then_inc(both_ready, 1)
            nc.vector.tensor_tensor(rank[:], best[:, 1], best[:, 0], ALU.subtract).then_inc(gap_ready, 1)
            dve.wait_ge(count_ps, 1)
            flat = lambda ap: ap.rearrange("p t e -> p (t e)")
            step(nc.vector.tensor_copy(flat(total[:]), TOTAL))
            src, shift = total[:], 1
            for i in range(5):
                dst = scan[:, i % 2]
                nc.vector.tensor_copy(dst[:, 0:shift], src[:, 0:shift])
                step(nc.vector.tensor_tensor(dst[:, shift:], src[:, shift:], src[:, 0:TILES - shift], ALU.add))
                src, shift = dst, 2 * shift
            count = src[:, TILES - 1]
            step(nc.vector.tensor_tensor(beyond[:], count.unsqueeze(2).broadcast_to([P, E, TILES]),
                                         multiples[:].unsqueeze(1).broadcast_to([P, E, TILES]), ALU.is_gt))
            step(nc.vector.tensor_reduce(used[:], beyond[:], AX_X, ALU.add))
            sums, shift = used[:], 1
            for i in range(3):
                dst = ends[:, i % 2]
                nc.vector.tensor_copy(dst[:, 0:shift], sums[:, 0:shift])
                step(nc.vector.tensor_tensor(dst[:, shift:], sums[:, shift:], sums[:, 0:E - shift], ALU.add))
                sums, shift = dst, 2 * shift
            step(nc.vector.tensor_tensor(base[:], sums, used[:], ALU.subtract))
            step(nc.vector.tensor_tensor(place[:], src, total[:], ALU.subtract))
            step(nc.vector.tensor_tensor(flat(place[:]), PLACE, flat(place[:]), ALU.add))
            step(nc.vector.scalar_tensor_tensor(place[:], by_expert(base[:]), float(P), place[:], ALU.mult, ALU.add))
            for c in range(2):
                step(nc.vector.tensor_tensor(same[:], chosen[:, c], place[:], ALU.mult))
                step(nc.vector.tensor_reduce(slot[:, c], same[:], AX_X, ALU.add))
            step(nc.vector.tensor_copy(slot_i[:], slot[:]))
            nc.vector.tensor_scalar(part_i[:, 0], slot_i[:], 7, None, ALU.logical_shift_right)
            step(nc.vector.tensor_scalar(part_i[:, 1], slot_i[:], P - 1, None, ALU.bitwise_and))
            step(nc.vector.tensor_copy(part[:], part_i[:]))

            def one_hots(at, first, last):
                wait_apart(dve, table_ps, at.n + 1, chain)
                t = bass.ds(at.n, 1)
                for c in range(2):
                    nc.vector.tensor_scalar(row[:, at.b, c, :], up_to[:], part[:, 1, c, t], None, ALU.is_equal)
                    ins = nc.vector.tensor_scalar(column[:, at.b, c, :], up_to[:, 0:SLOT_TILES], part[:, 0, c, t],
                                                  number[:, t], ALU.is_equal, ALU.mult)
                ins.then_inc(hot_ready, 1)

            pipeline(dve, [(0, one_hots)], TILES)
            step = Chain(dve, chain, step.n + TILES)
            step(nc.vector.tensor_tensor(passed[:], up_to[:, 0:SLOT_TILES].unsqueeze(2).broadcast_to([P, SLOT_TILES, E]),
                                         sums.unsqueeze(1).broadcast_to([P, SLOT_TILES, E]), ALU.is_ge))
            step(nc.vector.tensor_reduce(tile_expert[:], passed[:], AX_X, ALU.add))
            nc.vector.tensor_scalar(moe.expert[:], tile_expert[:], float(E - 1), None, ALU.min)
            dve.wait_ge(ratio_ready, 1)
            step(nc.vector.tensor_scalar(moe.weight[:, 0], ratio[:], 1.0, None, ALU.add))
            step(nc.vector.reciprocal(moe.weight[:, 0], moe.weight[:, 0]))
            nc.vector.tensor_tensor(moe.weight[:, 1], ratio[:], moe.weight[:, 0], ALU.mult)
            dve.wait_ge(table_ps, TILES + 2)
            step(nc.vector.tensor_copy(found[:], FOUND))
            step(nc.vector.tensor_tensor(token[:], found[:, 0], found[:, 1], ALU.add))
            nc.vector.tensor_scalar(moe.gather[:], token[:], 1.0, 0.0, ALU.subtract, ALU.max)
            nc.vector.tensor_scalar(empty[:], token[:], 0.0, NEVER, ALU.is_equal, ALU.mult)
            step(nc.vector.tensor_scalar(target[:], token[:], 2.0, -2.0, ALU.mult, ALU.add))
            step(nc.vector.tensor_tensor(target[:], target[:], empty[:], ALU.add))
            nc.vector.scalar_tensor_tensor(moe.scatter[:], found[:, 1], 0.0, target[:], ALU.is_gt, ALU.add)


def experts(nc, top, moe):
    ps, ident = top.ps, top.ident
    F, SLOT_TILES = moe.F, moe.SLOT_TILES
    CHUNKS = F // P
    tag = moe.tag
    with ExitStack() as ctx:
        k = Kit(nc, ctx)
        sb = lambda name, shape, dt=F32: k.sb(f"{tag}_{name}", shape, dt)
        sem = lambda *names: [k.sem(f"{tag}_{s}") for s in names]
        xg = sb("xg", [P, 2, C])
        xgT = sb("xgT", [P, 2, P])
        silu = sb("silu", [P, 2, F])
        h = sb("h", [P, 2, F])
        hT = sb("hT", [P, 2, F])
        y = sb("y", [P, 2, C])
        from_row = sb("from_row", [P, 2, 1], U32)
        to_row = sb("to_row", [P, 2, 1], U32)
        gathered, scattered = sem("gathered0", "gathered1"), sem("scattered0", "scattered1")
        xg_ps, xg_ready, gu_ps, silu_ready, h_ready, h_ps, hT_ready, y_ps, y_ready, passed = sem(
            "xg_ps", "xg_rd", "gu_ps", "silu_rd", "h_rd", "h_ps", "hT_rd", "y_ps", "y_rd", "passed")
        from_ready, to_ready = sem("from_rd", "to_rd")

        if 2 * F <= 512:
            GATE = lambda b: ps[:, 2 * b, 0:F]
            UP = lambda b: ps[:, 2 * b, F:2 * F]
        else:
            GATE = lambda b: ps[:, 2 * b, 0:F]
            UP = lambda b: ps[:, 2 * b + 1, 0:F]
        XT = lambda b: ps[:, 6, b * P:(b + 1) * P]
        HT = lambda b: ps[:, 4 + b, 0:F]
        Y = lambda b: ps[:, 7, b * C:(b + 1) * C]

        block = ctx.enter_context(nc.Block())

        @block.gpsimd
        def _(pool):
            def gather(at, first, last):
                wait_apart(pool, xg_ps, at.n + 1, passed)
                wait_apart(pool, from_ready, at.n + 1, passed)
                nc.gpsimd.indirect_dma_start(
                    xg[:, at.b, :], None, moe.xn_dram,
                    bass.IndirectOffsetOnAxis(ap=from_row[:, at.b, :], axis=0)).then_inc(gathered[at.b], 16)

            def scatter(at, first, last):
                wait_apart(pool, to_ready, at.n + 1, passed)
                wait_apart(pool, y_ready, at.n + 3, passed)
                nc.gpsimd.indirect_dma_start(
                    moe.y_dram, bass.IndirectOffsetOnAxis(ap=to_row[:, at.b, :], axis=0),
                    y[:, at.b, :], None, bounds_check=TOK * moe.TOP - 1,
                    oob_is_err=False).then_inc(scattered[at.b], 16)

            pipeline(pool, [(-2, gather), (2, scatter)], SLOT_TILES)
            for b in range(2):
                pool.wait_ge(scattered[b], 16 * (SLOT_TILES // 2))

        @block.tensor
        def _(pe):
            pe.wait_ge(moe.weights_in, 2 * 16)
            pe.sem_inc(xg_ps, 2)
            pe.sem_inc(h_ps, 2)
            pe.sem_inc(y_ps, 2)

            def transpose_x(at, first, last):
                pe.wait_ge(gathered[at.b], 16 * (at.half + 1))
                pe.wait_ge(xg_ready, at.n + 1)
                nc.tensor.transpose(XT(at.b), xg[:, at.b, :], ident[:]).then_inc(xg_ps, 1)

            def gate_up(at, first, last):
                pe.wait_ge(xg_ready, at.n + 2)
                pe.wait_ge(h_ready, at.n + 1)
                e = pe.value_load(moe.expert[0:1, bass.ds(at.n, 1)], min_val=0, max_val=moe.E - 1)
                w = moe.w_in[:, bass.ds(e, 1), :].rearrange("p e f -> p (e f)")
                if 2 * F <= 512:
                    ins = nc.tensor.matmul(ps[:, 2 * at.b, 0:2 * F], xgT[:, at.b, :], w, start=True, stop=True)
                else:
                    for o, cols in ((GATE(at.b), slice(0, F)), (UP(at.b), slice(F, 2 * F))):
                        ins = nc.tensor.matmul(o, xgT[:, at.b, :], w[:, cols], start=True, stop=True)
                ins.then_inc(gu_ps, 1)

            def transpose_h(at, first, last):
                pe.wait_ge(h_ready, at.n + 3)
                pe.wait_ge(hT_ready, at.n + 1)
                for c in range(CHUNKS):
                    ins = nc.tensor.transpose(HT(at.b)[:, c * P:(c + 1) * P], h[:, at.b, c * P:(c + 1) * P], ident[:])
                ins.then_inc(h_ps, 1)

            def down(at, first, last):
                pe.wait_ge(hT_ready, at.n + 3)
                pe.wait_ge(y_ready, at.n + 2)
                e = pe.value_load(moe.expert[0:1, bass.ds(at.n, 1)], min_val=0, max_val=moe.E - 1)
                for c in range(CHUNKS):
                    ins = nc.tensor.matmul(Y(at.b), hT[:, at.b, c * P:(c + 1) * P],
                                           moe.w_out[:, bass.ds(e, 1), c, :].rearrange("p e c -> p (e c)"),
                                           start=(c == 0), stop=(c == CHUNKS - 1))
                ins.then_inc(y_ps, 1)

            pipeline(pe, [(0, gate_up), (-1, transpose_x), (1, transpose_h), (2, down)], SLOT_TILES)

        @block.scalar
        def _(act):
            act.sem_inc(xg_ready, 1)
            act.sem_inc(hT_ready, 2)

            def gate(at, first, last):
                act.wait_ge(gu_ps, at.n + 1)
                act.wait_ge(h_ready, at.n + 1)
                nc.scalar.activation(silu[:, at.b, :], GATE(at.b), ACT.Silu).then_inc(silu_ready, 1)

            def copy_x(at, first, last):
                act.wait_ge(xg_ps, at.n + 3)
                nc.scalar.activation(xgT[:, at.b, :], XT(at.b), ACT.Copy).then_inc(xg_ready, 1)

            def copy_h(at, first, last):
                act.wait_ge(h_ps, at.n + 3)
                act.wait_ge(y_ps, at.n + 1)
                nc.scalar.activation(hT[:, at.b, :], HT(at.b), ACT.Copy).then_inc(hT_ready, 1)

            pipeline(act, [(0, gate), (-1, copy_x), (1, copy_h)], SLOT_TILES)

        @block.vector
        def _(dve):
            dve.sem_inc(h_ready, 2)
            dve.sem_inc(y_ready, 2)

            def hidden(at, first, last):
                dve.wait_ge(silu_ready, at.n + 1)
                dve.wait_ge(h_ps, at.n + 1)
                nc.vector.tensor_tensor(h[:, at.b, :], UP(at.b), silu[:, at.b, :], ALU.mult).then_inc(h_ready, 1)

            def result(at, first, last):
                dve.wait_ge(y_ps, at.n + 3)
                if at.reuses:
                    dve.wait_ge(scattered[at.b], 16 * at.half)
                nc.vector.tensor_copy(to_row[:, at.b, :], moe.scatter[:, bass.ds(at.n, 1)]).then_inc(to_ready, 1)
                nc.vector.tensor_copy(y[:, at.b, :], Y(at.b)).then_inc(y_ready, 1)

            def source(at, first, last):
                if at.reuses:
                    dve.wait_ge(gathered[at.b], 16 * at.half)
                nc.vector.tensor_copy(from_row[:, at.b, :], moe.gather[:, bass.ds(at.n, 1)]).then_inc(from_ready, 1)

            pipeline(dve, [(0, hidden), (2, result), (-3, source)], SLOT_TILES)


def combine(nc, top, moe):
    T = top.T
    with ExitStack() as ctx:
        k = Kit(nc, ctx)
        tag = moe.tag
        PARTS = 4
        STEP = TILES // PARTS
        ys = k.sb(f"{tag}_ys", [P, TILES, moe.TOP, C])
        ys_in = [k.sem(f"{tag}_ys_in{i}") for i in range(PARTS)]
        half_added, added = k.sem(f"{tag}_half_added"), k.sem(f"{tag}_added")
        block = ctx.enter_context(nc.Block())
        tile = lambda t: T[:, t, :]

        @block.sync
        def _(sp):
            parts = moe.y_dram.rearrange("(i t p c) d -> i p t c d", t=STEP, p=P, c=moe.TOP)
            for i in range(PARTS):
                sp.dma_start(ys[:, i * STEP:(i + 1) * STEP], parts[i]).then_inc(ys_in[i], 16)

        @block.vector
        def _(dve):
            for i in range(PARTS):
                dve.wait_ge(ys_in[i], 16)
                for t in range(i * STEP, (i + 1) * STEP):
                    nc.vector.scalar_tensor_tensor(tile(t), ys[:, t, 0], moe.weight[:, 0, t:t + 1], tile(t), ALU.mult,
                                                   ALU.add).then_inc(half_added, 1)
                for t in range(i * STEP, (i + 1) * STEP):
                    dve.wait_ge(half_added, t + 1)
                    nc.vector.scalar_tensor_tensor(tile(t), ys[:, t, 1], moe.weight[:, 1, t:t + 1], tile(t), ALU.mult,
                                                   ALU.add).then_inc(added, 1)
                for t in range(i * STEP, (i + 1) * STEP):
                    dve.wait_ge(added, t + 1)
                    nc.vector.bn_stats(top.ln_stats[:, t, :], tile(t))


def experts_layer(nc, top, hidden, tag, router_dram, w_in_dram, w_out_dram):
    with ExitStack() as ctx:
        moe = Moe(nc, Kit(nc, ctx), hidden, tag)
        route(nc, top, moe, router_dram, w_in_dram, w_out_dram)
        experts(nc, top, moe)
        combine(nc, top, moe)


class Top:

    def __init__(self, nc, ctx):
        k = Kit(nc, ctx)
        self.X = k.sb("X", [P, TOK])
        self.T = k.sb("T", [P, TILES, C])
        self.ps = ctx.enter_context(nc.psum_tensor("ps", [P, 8, 512], F32))
        self.ident = k.sb("ident", [P, P])
        self.pool_scratch = k.sb("pool_scratch", [P, 1])
        self.gavg = k.sb("gavg", [P, P])
        self.eps5 = k.sb("eps5", [P, 1])
        self.mean = k.sb("mean", [P, N])
        self.rstd = k.sb("rstd", [P, N])
        self.gn_stats = k.sb("gn_stats", [P, N, 6])
        self.ln_stats = k.sb("ln_stats", [P, TILES, 6])
        self.ln_mean = k.sb("ln_mean", [P, TILES])
        self.ln_rstd = k.sb("ln_rstd", [P, TILES])


def layouts(i):
    import numpy as np

    i = {k: np.asarray(v) for k, v in i.items()}
    idx1 = np.zeros((TAP_TILES, QUADS), np.int64)
    idx2 = np.zeros((TAP_TILES, QUADS), np.int64)
    for t in range(TAP_TILES):
        for q in range(QUADS):
            (row, col), _ = tap_of(t, q)
            idx1[t, q] = row * KS + col
            if row % 2 == 0 and col % 2 == 0:
                idx2[t, q] = row // 2 * 3 + col // 2

    def tap_values(v, idx):
        return np.repeat(v.reshape(-1)[idx].T, CM, axis=0)

    fuse = i["L0_conv_fuse_w"].reshape(C, 2 * CM).T
    out = {
        "x": i["x"].transpose(1, 0, 2, 3).reshape(C, TOK),
        "cw": np.tile(i["L0_conv_conv_w"].reshape(CM, C).T, (1, QUADS)),
        "cb": np.tile(i["L0_conv_conv_b"].reshape(CM, 1), (QUADS, 1)),
        "f1": np.tile(fuse[:CM], (QUADS, 1)),
        "f2": np.tile(fuse[CM:], (QUADS, 1)),
        "fuse": fuse,
        "ab": np.concatenate([i["L0_conv_adap_bias"], i["L0_conv_atrous_bias"]]).reshape(2 * CM, 1),
        "fb": i["L0_conv_fuse_b"].reshape(C, 1),
        "taps": np.stack([tap_values(i["L0_conv_conv_kernel_w"], idx1), tap_values(i["L0_conv_conv_kernel_b"], idx1),
                          tap_values(i["L0_conv_conv_kernel2_w"], idx2), tap_values(i["L0_conv_conv_kernel2_b"], idx2)],
                         axis=1),
        "scal": np.concatenate([i[f"L0_conv_{n}"].reshape(-1) for n in
                                ("conv_k_w", "conv_k_b", "conv_k2_w", "conv_k2_b")]),
    }

    def heads_apart(w, front, copies):
        w = w.reshape(w.shape[0], 8, 16)
        o = np.zeros((w.shape[0], 8, 32), w.dtype)
        for c in range(copies):
            o[:, :, front + 16 * c:front + 16 * c + 16] = w
        return o.reshape(w.shape[0], 256)

    def as_partitions(v):
        return v.reshape(2, P).T

    out |= {
        "wq": heads_apart(i["L2_attn_Wq"], 0, 2),
        "wk": heads_apart(i["L2_attn_Wk"], 0, 2),
        "wv": i["L2_attn_Wv"],
        "wo": i["L2_attn_Wo"],
        "bq": as_partitions(heads_apart(i["L2_attn_bq"][None], 0, 2)),
        "bk": as_partitions(heads_apart(i["L2_attn_bk"][None], 0, 2)),
        "bv": i["L2_attn_bv"][:, None],
        "bo": i["L2_attn_bo"],
        "lin_wq": i["L3_attn_Wq"].T,
        "lin_wkv": i["L3_attn_Wkv"].T,
    }

    def expert_weights(gate, up, down):
        e, f, c = down.shape
        return (np.concatenate([gate, up], axis=2).transpose(1, 0, 2),
                down.reshape(e, f // P, P, c).transpose(2, 0, 1, 3))

    out["d_router"] = i["L2_ffn_router_w"].T
    out["d_in"], out["d_out"] = expert_weights(i["L2_ffn_w_gate"], i["L2_ffn_w_up"], i["L2_ffn_w_down"])
    out["f_router"] = i["L3_ffn_Wg"]
    out["f_in"], out["f_out"] = expert_weights(i["L3_ffn_W"], i["L3_ffn_V"], i["L3_ffn_W2"])
    return {k: np.ascontiguousarray(v) for k, v in out.items()}


def program(nc, d, out):
    Kit.used.clear()
    with ExitStack() as ctx:
        top = Top(nc, ctx)
        adaptive_conv(nc, top, *[d[n] for n in ("x", "cw", "cb", "f1", "f2", "fuse", "ab", "fb", "taps", "scal")])
        box_conv(nc, top)
        softmax_attention(nc, top, *[d[n] for n in ("wq", "wk", "wv", "wo", "bq", "bk", "bv", "bo")])
        clear_semaphores(nc)
        experts_layer(nc, top, 256, "d", d["d_router"], d["d_in"], d["d_out"])
        linear_attention(nc, top, d["lin_wq"], d["lin_wkv"])
        experts_layer(nc, top, 512, "f", d["f_router"], d["f_in"], d["f_out"])
        stored = ctx.enter_context(nc.semaphore("stored"))
        with nc.Block() as block:
            @block.sync
            def _(sp):
                sp.dma_start(out.rearrange("(t p) c -> p t c", p=P), top.T[:]).then_inc(stored, 16)
                sp.wait_ge(stored, 16)


def kernel(**inputs):
    import concourse.bacc as _bacc
    from concourse.bass_utils import run_bass_kernel_spmd as _run

    nc = _bacc.Bacc("TRN2", target_bir_lowering=False, num_devices=1)
    laid_out = layouts(inputs)
    drams = {name: nc.dram_tensor(f"in_{name}", a.shape, mybir.dt.from_np(a.dtype), kind="ExternalInput").ap()
             for name, a in laid_out.items()}
    out = nc.dram_tensor("out_tokens", (TOK, C), F32, kind="ExternalOutput").ap()
    program(nc, drams, out)
    r = _run(nc, [{f"in_{name}": a for name, a in laid_out.items()}], core_ids=[0])
    tokens = r.results[0]["out_tokens"]
    return tokens.reshape(N, PIX, C).transpose(0, 2, 1).reshape(N, C, H, W)
```

```python
from contextlib import ExitStack

import concourse.bass as bass
from concourse import mybir

F32 = mybir.dt.float32
F32R = mybir.dt.float32r
U32 = mybir.dt.uint32
I32 = mybir.dt.int32
ALU = mybir.AluOpType
ACT = mybir.ActivationFunctionType
AX_X = mybir.AxisListType.X

P = 128
N, C, H, W = 16, 128, 16, 16
PIX = H * W
TOK = N * PIX
TILES = TOK // P
GN_GROUP = C // 32
CM = 32
QUADS = P // CM
KS = 5
TAP_TILES = 7
FR, FC = 21, 20
GN_EPS, LN_EPS = 1e-5, 1e-5


def tap_of(t, quad):
    if t < KS:
        return (t, quad), True
    if t == KS:
        return (quad, KS - 1), True
    return (KS - 1, KS - 1), quad == QUADS - 1


class Chain:

    def __init__(self, eng, sem, base=0):
        self.eng, self.sem, self.n = eng, sem, base

    def __call__(self, ins):
        ins.then_inc(self.sem, 1)
        self.n = self.n + 1
        self.eng.wait_ge(self.sem, self.n)


class Kit:

    used = []

    def __init__(self, nc, ctx):
        self.nc, self.ctx = nc, ctx

    def sb(self, name, shape, dt=F32):
        return self.ctx.enter_context(self.nc.sbuf_tensor(name, shape, dt))

    def sem(self, name):
        s = self.ctx.enter_context(self.nc.semaphore(name))
        Kit.used.append(s)
        return s


def clear_semaphores(nc):
    numbers = sorted(s.num for s in Kit.used)
    assert numbers[-1] - numbers[0] + 1 == len(numbers)
    Kit.used.clear()
    with nc.Block() as block:
        @block.gpsimd
        def _(pool):
            nc.gpsimd.sem_clear(range(numbers[0], numbers[-1] + 1))


def channel_means(nc, step, stats, out):
    step(nc.vector.tensor_tensor(out, stats[:, :, 1], stats[:, :, 4], ALU.add))
    return nc.vector.tensor_scalar(out, out, 0.5, None, ALU.mult)


def variances(nc, step, stats, tmp, out, count):
    step(nc.vector.tensor_tensor(tmp, stats[:, :, 1], stats[:, :, 4], ALU.subtract))
    step(nc.vector.scalar_tensor_tensor(tmp, tmp, 0.25, tmp, ALU.mult, ALU.mult))
    step(nc.vector.tensor_tensor(out, stats[:, :, 2], stats[:, :, 5], ALU.add))
    return nc.vector.scalar_tensor_tensor(out, out, 1.0 / count, tmp, ALU.mult, ALU.add)


def adaptive_conv(nc, top, x_dram, cw_dram, cb_dram, f1_dram, f2_dram, fuse_dram, ab_dram, fb_dram,
                  taps_dram, scal_dram):
    X, ps = top.X, top.ps
    with ExitStack() as ctx:
        k = Kit(nc, ctx)
        xn = top.T[:].rearrange("p t c -> p (t c)")
        cw = k.sb("cw", [P, P])
        cb = k.sb("cb", [P, 1])
        f1 = k.sb("f1", [P, P])
        f2 = k.sb("f2", [P, P])
        fuse = k.sb("fuse", [2 * CM, P])
        ab = k.sb("ab", [2 * CM, 1])
        fb = k.sb("fb", [P, 1])
        taps = k.sb("taps", [P, 4, TAP_TILES])
        scal = k.sb("scal", [P, 6])
        gavg = top.gavg
        stats = k.sb("stats", [P, N, 6])
        mean_c = k.sb("mean_c", [P, N])
        dev = k.sb("dev", [P, N])
        sq = k.sb("sq", [P, N])
        shift = k.sb("shift_a", [P, N])
        pooled = k.sb("pooled", [P, N])
        g = k.sb("g", [P, N])
        kimg = k.sb("kimg", [P, N, TAP_TILES])
        kdom = k.sb("kdom", [P, TAP_TILES])
        counts = k.sb("counts", [P, 2, TAP_TILES])
        gk = k.sb("gk", [P, 2, N, TAP_TILES])
        cbias = k.sb("cbias", [P, 1])
        wimg = k.sb("wimg", [P, 2, TAP_TILES, P])
        fcol = k.sb("fcol", [P, N, FR * FC])
        frow = k.sb("frow", [P, N, FR * FC])
        fcol_v = fcol[:].rearrange("p n (r c) -> p n r c", c=FC)
        frow_v = frow[:].rearrange("p n (r c) -> p n r c", c=FC)
        x_in = [k.sem(f"x_in{i}") for i in range(4)]
        w_in, taps_in = k.sem("w_in"), k.sem("taps_in")
        pool_chain, dve_chain = k.sem("pool_chain_a"), k.sem("dve_chain_a")
        consts_ready, pads_ready = k.sem("consts_ready"), k.sem("pads_ready")
        mean_ready, mean_ps, var_ready, var_ps = (k.sem(s) for s in ("mean_rd", "mean_ps", "var_rd", "var_ps"))
        std_ready, xn_ready = k.sem("std_ready"), k.sem("xn_ready")
        pooled_ready, g_ps, g_ready, bias_ps = (k.sem(s) for s in ("pooled_rd", "g_ps", "g_rd", "bias_ps"))
        feat_ps, feat_act, shift_ready = k.sem("feat_ps"), k.sem("feat_act"), k.sem("shift_rd")
        wimg_ready, wimg_used, out_read = (k.sem(s) for s in ("wimg_rd", "wimg_used", "out_read"))
        wimg_half = k.sem("wimg_half")

        MEAN, VAR = ps[:, 4, 0:N], ps[:, 4, N:2 * N]
        G, BIAS = ps[:, 5, 0:N], ps[:, 5, N:N + 1]

        block = ctx.enter_context(nc.Block())

        @block.sync
        def _(sp):
            for i in range(4):
                sp.dma_start(X[:, i * (TOK // 4):(i + 1) * (TOK // 4)],
                             x_dram[:, i * (TOK // 4):(i + 1) * (TOK // 4)]).then_inc(x_in[i], 16)
            for dst, src in ((cw, cw_dram), (cb, cb_dram), (f1, f1_dram), (f2, f2_dram), (fuse, fuse_dram),
                             (ab, ab_dram), (fb, fb_dram)):
                sp.dma_start(dst[:], src).then_inc(w_in, 16)
            sp.dma_start(taps[:], taps_dram).then_inc(taps_in, 16)
            sp.dma_start(scal[:], scal_dram.partition_broadcast(P)).then_inc(taps_in, 16)

        @block.gpsimd
        def _(pool):
            step = Chain(pool, pool_chain)
            step(nc.gpsimd.memset(top.ident[:], 1.0))
            step(nc.gpsimd.affine_select(out=top.ident[:], in_=top.ident[:], compare_op=ALU.is_equal, fill=0.0,
                                         base=0, pattern=[[-1, P]], channel_multiplier=1))
            step(nc.gpsimd.memset(gavg[:], 1.0 / GN_GROUP))
            gv = gavg[:].rearrange("p (g r) -> p g r", r=GN_GROUP)
            step(nc.gpsimd.affine_select(out=gv, in_=gv, compare_op=ALU.is_ge, fill=0.0, base=0,
                                         pattern=[[-GN_GROUP, P // GN_GROUP], [0, GN_GROUP]], channel_multiplier=1))
            nc.gpsimd.affine_select(out=gv, in_=gv, compare_op=ALU.is_ge, fill=0.0, base=GN_GROUP - 1,
                                    pattern=[[GN_GROUP, P // GN_GROUP], [0, GN_GROUP]],
                                    channel_multiplier=-1).then_inc(consts_ready, 1)
            nc.gpsimd.memset(fcol[:], 0.0)
            nc.gpsimd.memset(frow[:], 0.0).then_inc(pads_ready, 1)

        @block.scalar
        def _(act):
            act.wait_ge(var_ps, 1)
            act.wait_ge(std_ready, 1)
            nc.scalar.activation(top.rstd[:], VAR, ACT.Sqrt, bias=top.eps5[:]).then_inc(std_ready, 1)
            act.wait_ge(shift_ready, 1)
            with act.Fori(0, N // 2) as i:
                for a in range(2):
                    n = 2 * i + a
                    last = nc.scalar.activation(xn[:, bass.ds(n * PIX, PIX)], X[:, bass.ds(n * PIX, PIX)], ACT.Identity,
                                                bias=shift[:, bass.ds(n, 1)], scale=top.rstd[:, bass.ds(n, 1)])
                last.then_inc(xn_ready, 1)
            act.wait_ge(w_in, 7 * 16)
            act.wait_ge(pads_ready, 1)
            with act.Fori(0, N // 4) as i:
                for b in range(2):
                    act.wait_ge(feat_ps, 2 * i + b + 1)
                    src = ps[:, b, :].rearrange("p (n r c) -> p n r c", n=2, c=W)
                    for q in range(QUADS):
                        rows = slice(q * CM, (q + 1) * CM)
                        for dst, r0, c0 in ((fcol_v, 3, 3 - q), (frow_v, 3 - q, 2)):
                            o = dst[rows, bass.ds(4 * i + 2 * b, 2), r0:r0 + H, c0:c0 + W]
                            last = nc.scalar.activation(o, src[rows], ACT.Relu, bias=cb[rows])
                    last.then_inc(feat_act, 1)

        @block.tensor
        def _(pe):
            pe.wait_ge(mean_ready, 1)
            pe.wait_ge(consts_ready, 1)
            nc.tensor.matmul(MEAN, gavg[:], mean_c[:], start=True, stop=True).then_inc(mean_ps, 1)
            pe.wait_ge(var_ready, 1)
            nc.tensor.matmul(VAR, gavg[:], sq[:], start=True, stop=True).then_inc(var_ps, 1)
            pe.wait_ge(w_in, 7 * 16)
            pe.wait_ge(pooled_ready, 1)
            nc.tensor.matmul(G, cw[:], pooled[:], start=True, stop=True).then_inc(g_ps, 1)
            pe.wait_ge(g_ready, 1)
            nc.tensor.matmul(BIAS, fuse[:], ab[:], start=True, stop=True).then_inc(bias_ps, 1)

            def features(pair, b):
                pe.wait_ge(xn_ready, pair + 1)
                nc.tensor.matmul(ps[:, b, :], cw[:], xn[:, bass.ds(pair * 2 * PIX, 2 * PIX)],
                                 start=True, stop=True).then_inc(feat_ps, 1)

            def convolve(pair, b):
                for a in range(2):
                    pe.wait_ge(wimg_ready, 2 * pair + a + 1)
                    for t in range(TAP_TILES):
                        src, r0, c0 = (fcol_v, 1 + t, 1) if t < KS else (frow_v, 1 + t - KS, KS - 1)
                        rhs = src[:, bass.ds(2 * pair + a, 1), r0:r0 + H, c0:c0 + W]
                        last = nc.tensor.matmul(ps[:, 2 + b, a * PIX:(a + 1) * PIX], wimg[:, a, t, :],
                                                rhs.rearrange("p n r c -> p (n r) c"),
                                                start=(t == 0), stop=(t == TAP_TILES - 1))
                    last.then_inc(wimg_used, 1)

            for b in range(2):
                features(b, b)
            with pe.Fori(0, N // 4 - 1) as i:
                for b in range(2):
                    pair = 2 * i + b
                    pe.wait_ge(feat_act, pair + 1)
                    pe.wait_ge(out_read, pair + 1)
                    convolve(pair, b)
                    features(pair + 2, b)
            for b in range(2):
                pair = N // 2 - 2 + b
                pe.wait_ge(feat_act, pair + 1)
                pe.wait_ge(out_read, pair + 1)
                convolve(pair, b)

        @block.vector
        def _(dve):
            step = Chain(dve, dve_chain)
            nc.vector.memset(top.eps5[:], GN_EPS).then_inc(std_ready, 1)
            step(nc.vector.memset(counts[:, 0, :], 1.0))
            step(nc.vector.memset(counts[:, 1, :], 0.0))
            for q in range(QUADS):
                for t in range(TAP_TILES):
                    (row, col), real = tap_of(t, q)
                    rows = slice(q * CM, (q + 1) * CM)
                    if not real:
                        step(nc.vector.memset(counts[rows, 0, t:t + 1], 0.0))
                    elif row % 2 == 0 and col % 2 == 0:
                        step(nc.vector.memset(counts[rows, 1, t:t + 1], 1.0))
            for n in range(N):
                if n % 4 == 0:
                    dve.wait_ge(x_in[n // 4], 16)
                last = nc.vector.bn_stats(stats[:, n, :], X[:, n * PIX:(n + 1) * PIX])
            step(last)
            channel_means(nc, step, stats, mean_c[:]).then_inc(mean_ready, 1)
            dve.wait_ge(mean_ready, 1)
            step(variances(nc, step, stats, dev[:], sq[:], PIX))
            dve.wait_ge(mean_ps, 1)
            step(nc.vector.tensor_copy(top.mean[:], MEAN))
            step(nc.vector.tensor_tensor(dev[:], mean_c[:], top.mean[:], ALU.subtract))
            step(nc.vector.tensor_tensor(dev[:], dev[:], dev[:], ALU.mult))
            nc.vector.tensor_tensor(sq[:], sq[:], dev[:], ALU.add).then_inc(var_ready, 1)
            dve.wait_ge(std_ready, 2)
            step(nc.vector.reciprocal(top.rstd[:], top.rstd[:]))
            step(nc.vector.tensor_tensor(pooled[:], mean_c[:], top.mean[:], ALU.subtract))
            nc.vector.scalar_tensor_tensor(shift[:], top.mean[:], -1.0, top.rstd[:], ALU.mult,
                                           ALU.mult).then_inc(shift_ready, 1)
            nc.vector.tensor_tensor(pooled[:], pooled[:], top.rstd[:], ALU.mult).then_inc(pooled_ready, 1)
            dve.wait_ge(g_ps, 1)
            dve.wait_ge(w_in, 7 * 16)
            dve.wait_ge(taps_in, 2 * 16)
            nc.vector.tensor_scalar(g[:], G, cb[:], 0.0, ALU.add, ALU.max).then_inc(g_ready, 1)
            dve.wait_ge(g_ready, 1)
            for m in range(2):
                each = lambda ap: ap.unsqueeze(1).broadcast_to([P, N, TAP_TILES])
                step(nc.vector.tensor_tensor(kimg[:], g[:].unsqueeze(2).broadcast_to([P, N, TAP_TILES]),
                                             each(taps[:, 2 * m, :]), ALU.mult))
                step(nc.vector.tensor_tensor(kimg[:], kimg[:], each(taps[:, 2 * m + 1, :]), ALU.add))
                step(nc.vector.tensor_reduce(kdom[:], kimg[:].rearrange("p n t -> p t n"), AX_X, ALU.add))
                step(nc.vector.tensor_scalar(kdom[:], kdom[:], 1.0 / N, scal[:, 3 * m + 1:3 * m + 2],
                                             ALU.mult, ALU.mult))
                step(nc.vector.tensor_scalar(kdom[:], kdom[:], scal[:, 3 * m + 2:3 * m + 3], None, ALU.add))
                step(nc.vector.scalar_tensor_tensor(kimg[:], kimg[:], scal[:, 3 * m:3 * m + 1], each(kdom[:]),
                                                    ALU.mult, ALU.add))
                step(nc.vector.scalar_tensor_tensor(gk[:, m, :, :], kimg[:], 0.0, each(counts[:, m, :]),
                                                    ALU.max, ALU.mult))
            dve.wait_ge(bias_ps, 1)
            step(nc.vector.tensor_tensor(cbias[:], BIAS, fb[:], ALU.add))

            def stationary(pair, a):
                n = 2 * pair + a
                dve.wait_ge(wimg_used, n + 1)
                for t in range(TAP_TILES):
                    last = nc.vector.tensor_scalar(wimg[:, a, t, :], f1[:], gk[:, 0, bass.ds(n, 1), t], None, ALU.mult)
                last.then_inc(wimg_half, 1)
                dve.wait_ge(wimg_half, n + 1)
                for t in (0, 2, 4, 5, 6):
                    last = nc.vector.scalar_tensor_tensor(wimg[:, a, t, :], f2[:], gk[:, 1, bass.ds(n, 1), t],
                                                          wimg[:, a, t, :], ALU.mult, ALU.add)
                last.then_inc(wimg_ready, 1)

            def outputs(pair, b):
                dve.wait_ge(wimg_used, 2 * pair + 4)
                at = X[:, bass.ds(pair * 2 * PIX, 2 * PIX)]
                nc.vector.scalar_tensor_tensor(at, ps[:, 2 + b, :], cbias[:], at, ALU.add,
                                               ALU.add).then_inc(out_read, 1)
                dve.wait_ge(out_read, pair + 3)
                for a in range(2):
                    n = 2 * pair + a
                    nc.vector.bn_stats(top.gn_stats[:, bass.ds(n, 1), :].rearrange("p a s -> p (a s)"),
                                       X[:, bass.ds(n * PIX, PIX)])

            dve.sem_inc(wimg_used, 2)
            dve.sem_inc(out_read, 2)
            for a in range(2):
                stationary(0, a)
            with dve.Fori(0, N // 4 - 1) as i:
                for b in range(2):
                    for a in range(2):
                        stationary(2 * i + b + 1, a)
                    outputs(2 * i + b, b)
            for a in range(2):
                stationary(N // 2 - 1, a)
            outputs(N // 2 - 2, 0)
            outputs(N // 2 - 1, 1)


def box_conv(nc, top):
    X, T, ps = top.X, top.T, top.ps
    PH, PW = H + 2, W + 2
    with ExitStack() as ctx:
        k = Kit(nc, ctx)
        mean_c = k.sb("mean_c2", [P, N])
        dev = k.sb("dev2", [P, N])
        sq = k.sb("sq2", [P, N])
        shift = k.sb("shift", [P, N])
        pad = k.sb("pad", [P, 2, PH * PW])
        rows = k.sb("rows", [P, 2, PH * W])
        mid = k.sb("mid", [P, 2, PIX])
        gavg = top.gavg
        dve_chain = k.sem("dve_chain_b")
        mean_ready, mean_ps, var_ready, var_ps, std_ready, norm_ready = (
            k.sem(s) for s in ("b_mean_rd", "b_mean_ps", "b_var_rd", "b_var_ps", "b_std_rd", "b_norm_rd"))
        pad_ready, rows_half, rows_ready, mid_ready, tok_ps, tok_ready = (
            k.sem(s) for s in ("pad_rd", "rows_half", "rows_rd", "mid_rd", "tok_ps", "tok_rd"))
        MEAN, VAR = ps[:, 4, 0:N], ps[:, 4, N:2 * N]
        image = lambda n: X[:, bass.ds(n * PIX, PIX)]

        block = ctx.enter_context(nc.Block())

        @block.scalar
        def _(act):
            act.wait_ge(var_ps, 1)
            nc.scalar.activation(top.rstd[:], VAR, ACT.Sqrt, bias=top.eps5[:]).then_inc(std_ready, 1)
            act.wait_ge(norm_ready, 1)

            def normed(n, b):
                act.wait_ge(rows_ready, n + 1)
                inner = pad[:, b, :].rearrange("p (r c) -> p r c", c=PW)[:, 1:1 + H, 1:1 + W]
                nc.scalar.activation(inner, image(n).rearrange("p (r c) -> p r c", c=W), ACT.Identity,
                                     bias=shift[:, bass.ds(n, 1)],
                                     scale=top.rstd[:, bass.ds(n, 1)]).then_inc(pad_ready, 1)

            def tokens(n, b):
                act.wait_ge(tok_ps, n + 3)
                nc.scalar.activation(T[:, bass.ds(2 * n, 2), :].rearrange("p t c -> p (t c)"),
                                     ps[:, b, 0:2 * P], ACT.Copy).then_inc(tok_ready, 1)

            act.sem_inc(tok_ready, 2)
            for b in range(2):
                normed(b, b)
            with act.Fori(0, N // 2 - 1) as i:
                for b in range(2):
                    normed(2 * i + b + 2, b)
                    tokens(2 * i + b, b)
            for b in range(2):
                tokens(N - 2 + b, b)

        @block.gpsimd
        def _(pool):
            with pool.Fori(0, N // 2) as i:
                for b in range(2):
                    n = 2 * i + b
                    pool.wait_ge(rows_ready, n + 3)
                    pool.wait_ge(tok_ps, n + 1)
                    nc.gpsimd.tensor_tensor(mid[:, b, :], image(n), rows[:, b, W:W + PIX],
                                            ALU.add).then_inc(mid_ready, 1)

        @block.tensor
        def _(pe):
            pe.wait_ge(mean_ready, 1)
            nc.tensor.matmul(MEAN, gavg[:], mean_c[:], start=True, stop=True).then_inc(mean_ps, 1)
            pe.wait_ge(var_ready, 1)
            nc.tensor.matmul(VAR, gavg[:], sq[:], start=True, stop=True).then_inc(var_ps, 1)
            pe.sem_inc(tok_ps, 2)
            with pe.Fori(0, N // 2) as i:
                for b in range(2):
                    n = 2 * i + b
                    pe.wait_ge(mid_ready, n + 1)
                    pe.wait_ge(tok_ready, n + 1)
                    for half in range(2):
                        o = ps[:, b, half * P:(half + 1) * P]
                        at = half * P
                        nc.tensor.matmul(o, rows[:, b, at:at + P], top.ident[:], start=True, stop=False)
                        nc.tensor.matmul(o, rows[:, b, at + 2 * W:at + 2 * W + P], top.ident[:], start=False, stop=False)
                        last = nc.tensor.matmul(o, mid[:, b, at:at + P], top.ident[:], start=False, stop=True)
                    last.then_inc(tok_ps, 1)

        @block.vector
        def _(dve):
            step = Chain(dve, dve_chain)
            stats = top.gn_stats
            nc.vector.memset(pad[:], 0.0).then_inc(rows_ready, 2)
            channel_means(nc, step, stats, mean_c[:]).then_inc(mean_ready, 1)
            dve.wait_ge(mean_ready, 1)
            step(variances(nc, step, stats, dev[:], sq[:], PIX))
            dve.wait_ge(mean_ps, 1)
            step(nc.vector.tensor_copy(top.mean[:], MEAN))
            step(nc.vector.tensor_tensor(dev[:], mean_c[:], top.mean[:], ALU.subtract))
            step(nc.vector.tensor_tensor(dev[:], dev[:], dev[:], ALU.mult))
            nc.vector.tensor_tensor(sq[:], sq[:], dev[:], ALU.add).then_inc(var_ready, 1)
            dve.wait_ge(std_ready, 1)
            step(nc.vector.reciprocal(top.rstd[:], top.rstd[:]))
            nc.vector.scalar_tensor_tensor(shift[:], top.mean[:], -1.0, top.rstd[:], ALU.mult,
                                           ALU.mult).then_inc(norm_ready, 1)

            def row_sums(n, b):
                dve.wait_ge(pad_ready, n + 1)
                dve.wait_ge(tok_ps, n + 1)
                p = pad[:, b, :].rearrange("p (r c) -> p r c", c=PW)
                o = rows[:, b, :].rearrange("p (r c) -> p r c", c=W)
                nc.vector.tensor_tensor(o, p[:, :, 0:W], p[:, :, 1:1 + W], ALU.add).then_inc(rows_half, 1)
                dve.wait_ge(rows_half, n + 1)
                nc.vector.tensor_tensor(o, o, p[:, :, 2:2 + W], ALU.add).then_inc(rows_ready, 1)

            def statistics(n):
                dve.wait_ge(tok_ready, n + 3)
                token_statistics(nc, top, n)

            row_sums(0, 0)
            row_sums(1, 1)
            with dve.Fori(0, N // 2 - 1) as i:
                for b in range(2):
                    row_sums(2 * i + b + 2, b)
                    statistics(2 * i + b)
            for b in range(2):
                statistics(N - 2 + b)


def prepare_norm(nc, top, block, k, tag):
    chain, var_ready, std_ready, norm_ready = (
        k.sem(f"{tag}_{s}") for s in ("ln_chain", "ln_var_rd", "ln_std_rd", "ln_rd"))
    tmp = k.sb(f"{tag}_ln_tmp", [P, TILES])

    def on_vector(dve):
        step = Chain(dve, chain)
        step(channel_means(nc, step, top.ln_stats, top.ln_mean[:]))
        variances(nc, step, top.ln_stats, tmp[:], top.ln_rstd[:], C).then_inc(var_ready, 1)
        dve.wait_ge(std_ready, 1)
        nc.vector.reciprocal(top.ln_rstd[:], top.ln_rstd[:]).then_inc(norm_ready, 1)
        dve.wait_ge(norm_ready, 1)

    def on_scalar(act):
        act.wait_ge(var_ready, 1)
        nc.scalar.activation(top.ln_rstd[:], top.ln_rstd[:], ACT.Sqrt, bias=top.eps5[:]).then_inc(std_ready, 1)

    return on_vector, on_scalar


def wait_apart(eng, sem, value, passed):
    eng.wait_ge(sem, value)
    eng.sem_inc(passed, 1)


def image_loop(eng, body, ahead=0):
    body(0, 0, True, False)
    with eng.Fori(0, (N - 2) // 2) as i:
        for b in (1, 2):
            body(2 * i + b, b % 2, False, False)
    body(N - 1, (N - 1) % 2, False, True)


def softmax_attention(nc, top, wq_dram, wk_dram, wv_dram, wo_dram, bq_dram, bk_dram, bv_dram, bo_dram):
    T, ps, ident = top.T, top.ps, top.ident
    NH, HD = 8, 16
    HG = 4
    SCALE = HD ** -0.5
    WARMERS = (0,0,0,0,1,1,2,1)
    ROW_MAX = HD
    with ExitStack() as ctx:
        k = Kit(nc, ctx)
        wq = k.sb("wq", [P, 2, P])
        wk = k.sb("wk", [P, 2, P])
        wv = k.sb("wv", [P, P])
        wo = k.sb("wo", [P, P])
        bq = k.sb("bq", [P, 2])
        bk = k.sb("bk", [P, 2])
        bv = k.sb("bv", [P, 1])
        bo = k.sb("bo", [P, 2, P])
        upper = k.sb("upper", [P, 1])
        lower = k.sb("lower", [P, 1])
        one_row = k.sb("one_row", [P, 1])
        bq_up = k.sb("bq_up", [P, 2])
        bq_low = k.sb("bq_low", [P, 2])
        xn = k.sb("xn_c", [P, 2, 2, C])
        xT = k.sb("xT_c", [P, 2, PIX])
        q_low = k.sb("q_low", [P, 2, 2, PIX], F32R)
        q_up = k.sb("q_up", [P, 2, 2, PIX], F32R)
        qa = k.sb("qa", [P, 2, 2, PIX], F32R)
        qb = k.sb("qb", [P, 2, 2, PIX], F32R)
        ka = k.sb("ka", [P, 2, 2, PIX], F32R)
        kl = k.sb("kl", [P, 2, 2, PIX])
        kb = k.sb("kb", [P, 2, 2, PIX], F32R)
        negmax = k.sb("negmax", [P, 2, 2, P])
        vaug = k.sb("vaug", [P, 2, 2, NH, 32])
        prob = k.sb("prob", [P, NH, 2, PIX])
        heads_T = k.sb("heads_T", [P, 2, PIX])
        inv = k.sb("inv", [P, 2 * NH])
        heads = k.sb("heads", [P, 2, P])
        att = k.sb("att", [P, PIX])
        w_in, masks_ready, chain, chain2, zeros_ready = (
            k.sem(f"c_{s}") for s in ("w_in", "masks", "chain", "chain2", "zeros"))
        xn_ready, xT_ps, xT_ready, q_ps, k_ps, v_ps = (
            k.sem(f"c_{s}") for s in ("xn_rd", "xT_ps", "xT_rd", "q_ps", "k_ps", "v_ps"))
        q_low_ready, q_up_ready, qa_ready, ka_ready, kl_ready, kb_ready, v_ready = (
            k.sem(f"c_{s}") for s in ("q_low_rd", "q_up_rd", "qa_rd", "ka_rd", "kl_rd", "kb_rd", "v_rd"))
        max_ps, max_ready, maxT_ps, qb_ready, score_ps, prob_ready = (
            k.sem(f"c_{s}") for s in ("max_ps", "max_rd", "maxT_ps", "qb_rd", "score_ps", "prob_rd"))
        passed_pool = k.sem("c_passed_pool")
        pv_ps, headsT_ready, heads_ps, inv_ready, heads_ready, att_ps, att_ready, out_ps, bo_added, tok_ready = (
            k.sem(f"c_{s}") for s in ("pv_ps", "headsT_rd", "heads_ps", "inv_rd", "heads_rd", "att_ps", "att_rd",
                                      "out_ps", "bo_added", "tok_rd"))

        Q = ps[:, 4, :].rearrange("p (g t) -> p g t", g=2)
        K = ps[:, 5, :].rearrange("p (g t) -> p g t", g=2)
        MAXT = K
        PV = ps[:, 6, :].rearrange("p (g t) -> p g t", g=2)
        HEADS = ps[:, 6, :].rearrange("p (t g c) -> p t g c", t=2, g=2)
        ATT = ps[:, 6, 0:PIX]
        OUT = ps[:, 6, PIX:2 * PIX]
        XT = ps[:, 7, 0:PIX]
        V = ps[:, 7, PIX:2 * PIX]

        block = ctx.enter_context(nc.Block())
        norm_on_vector, norm_on_scalar = prepare_norm(nc, top, block, k, "c")

        @block.sync
        def _(sp):
            for dst, src in ((wq, wq_dram), (wk, wk_dram)):
                sp.dma_start(dst[:].rearrange("p g c -> p (g c)"), src).then_inc(w_in, 16)
            for dst, src in ((wv, wv_dram), (wo, wo_dram), (bq, bq_dram), (bk, bk_dram), (bv, bv_dram)):
                sp.dma_start(dst[:], src).then_inc(w_in, 16)
            for t in range(2):
                sp.dma_start(bo[:, t, :], bo_dram.partition_broadcast(P)).then_inc(w_in, 16)

        @block.gpsimd
        def _(pool):
            nc.gpsimd.memset(vaug[:, 1], 0.0).then_inc(chain2, 1)
            pool.wait_ge(chain2, 1)
            nc.gpsimd.memset(vaug[:, 1, :, :, 0:1], 1.0).then_inc(zeros_ready, 1)
            pool.wait_ge(masks_ready, 1)
            pool.wait_ge(w_in, 9 * 16)

            def keys_low(n, b, first, last):
                wait_apart(pool, kl_ready, n + 1, passed_pool)
                nc.gpsimd.tensor_scalar(kb[:, b], kl[:, b], upper[:], one_row[:], ALU.mult,
                                        ALU.add).then_inc(kb_ready, 1)
                pool.wait_ge(xn_ready, n + 1)
                t = T[:, bass.ds(2 * n, 2), :]
                nc.gpsimd.tensor_tensor(t, t, bo[:], ALU.add).then_inc(bo_added, 1)

            image_loop(pool, keys_low)

        @block.scalar
        def _(act):
            norm_on_scalar(act)
            act.wait_ge(w_in, 9 * 16)
            act.wait_ge(masks_ready, 1)
            act.wait_ge(zeros_ready, 2)

            def transposed(m, b):
                act.wait_ge(xT_ps, m + 1)
                nc.scalar.activation(xT[:, b, :], XT, ACT.Copy).then_inc(xT_ready, 1)

            def queries(m, b):
                act.wait_ge(q_ps, m + 1)
                for g in range(2):
                    last = nc.scalar.activation(q_low[:, b, g], Q[:, g], ACT.Identity, bias=bq_low[:, g:g + 1],
                                                scale=lower[:])
                last.then_inc(q_low_ready, 1)

            def queries_up(m, b):
                act.wait_ge(qa_ready, m + 1)
                for g in range(2):
                    last = nc.scalar.activation(q_up[:, b, g], Q[:, g], ACT.Identity, bias=bq_up[:, g:g + 1],
                                                scale=upper[:])
                last.then_inc(q_up_ready, 1)

            def keys(m, b):
                act.wait_ge(k_ps, m + 1)
                for g in range(2):
                    last = nc.scalar.activation(ka[:, b, g], K[:, g], ACT.Identity, bias=bk[:, g:g + 1])
                last.then_inc(ka_ready, 1)

            def values(m, b):
                act.wait_ge(v_ps, m + 1)
                nc.scalar.activation(vaug[:, b, :, :, 1:1 + HD],
                                     V.rearrange("p (t h d) -> p t h d", t=2, d=HD), ACT.Copy).then_inc(v_ready, 1)

            def exps(n, h, first):
                act.wait_ge(score_ps, NH * n + h + 1)
                if not first:
                    act.wait_ge(pv_ps, 2 * n - 1 + h // HG)
                nc.scalar.activation(prob[:, h].rearrange("p t q -> p (t q)"), ps[:, h % 2, :], ACT.Exp,
                                     scale=SCALE).then_inc(prob_ready, 1)

            transposed(0, 0)
            queries(0, 0)
            queries_up(0, 0)
            keys(0, 0)
            values(0, 0)

            def unnormed(n):
                act.wait_ge(pv_ps, 2 * n + 2)
                nc.scalar.activation(heads_T[:], PV, ACT.Copy).then_inc(headsT_ready, 1)

            def attention(n):
                act.wait_ge(att_ps, n + 1)
                nc.scalar.activation(att[:], ATT, ACT.Identity, bias=bv[:]).then_inc(att_ready, 1)

            def image(n, b, first, last):
                if not last:
                    transposed(n + 1, 1 - b)
                exps(n, 0, first)
                if not last:
                    queries(n + 1, 1 - b)
                exps(n, 1, first)
                if not last:
                    keys(n + 1, 1 - b)
                if not first:
                    attention(n - 1)
                exps(n, 2, first)
                if not last:
                    queries_up(n + 1, 1 - b)
                exps(n, 3, first)
                if not last:
                    values(n + 1, 1 - b)
                for h in range(4, NH):
                    exps(n, h, first)
                unnormed(n)

            image_loop(act, image)
            attention(N - 1)

        @block.tensor
        def _(pe):
            pe.wait_ge(w_in, 9 * 16)

            def transpose(m, b, first=False):
                pe.wait_ge(xn_ready, m + 1)
                if not first:
                    pe.wait_ge(v_ready, m)
                for t in range(2):
                    last = nc.tensor.transpose(XT[:, t * P:(t + 1) * P], xn[:, b, t, :], ident[:])
                last.then_inc(xT_ps, 1)

            def project_q(m, b):
                pe.wait_ge(xT_ready, m + 1)
                for g in range(2):
                    last = nc.tensor.matmul(Q[:, g], wq[:, g, :], xT[:, b, :], start=True, stop=True)
                last.then_inc(q_ps, 1)

            def project_k(m, b):
                for g in range(2):
                    last = nc.tensor.matmul(K[:, g], wk[:, g, :], xT[:, b, :], start=True, stop=True)
                last.then_inc(k_ps, 1)

            def project_v(m, b):
                for t in range(2):
                    last = nc.tensor.matmul(V[:, t * P:(t + 1) * P], xT[:, b, t * P:(t + 1) * P], wv[:],
                                            start=True, stop=True)
                last.then_inc(v_ps, 1)

            def max_scores(m, b, h, first=False):
                g, rows = h // HG, slice(32 * (h % HG), 32 * (h % HG) + 32)
                if h == 0:
                    pe.wait_ge(qa_ready, m + 1)
                    pe.wait_ge(ka_ready, m + 1)
                if not first or h >= 2:
                    pe.wait_ge(max_ready, NH * m + h - 1)
                for t in range(2):
                    last = nc.tensor.matmul(ps[:, 2 + h % 2, t * PIX:(t + 1) * PIX],
                                            qa[rows, b, g, t * P:(t + 1) * P], ka[rows, b, g, :],
                                            start=True, stop=True)
                last.then_inc(max_ps, 1)

            def transpose_maxima(n):
                pe.wait_ge(max_ready, NH * n + NH)
                pe.wait_ge(kb_ready, n + 1)
                for g in range(2):
                    for t in range(2):
                        last = nc.tensor.transpose(MAXT[:, g, t * P:(t + 1) * P], negmax[:, t, g, :], ident[:])
                last.then_inc(maxT_ps, 1)

            def scores(n, b, h, first):
                g, rows = h // HG, slice(32 * (h % HG), 32 * (h % HG) + 32)
                if h == 0:
                    pe.wait_ge(qb_ready, n + 1)
                if not first or h >= 2:
                    pe.wait_ge(prob_ready, NH * n + h - 1)
                for _ in range(WARMERS[h]):
                    nc.tensor.matmul(ps[:, h % 2, :], ka[:, b, g, 0:P], qa[:, b].rearrange("p g t -> p (g t)"),
                                     start=True, stop=True)
                for t in range(2):
                    o = ps[:, h % 2, t * PIX:(t + 1) * PIX]
                    keys = slice(t * P, (t + 1) * P)
                    nc.tensor.matmul(o, ka[rows, b, g, keys], qa[rows, b, g, :], start=True, stop=False)
                    last = nc.tensor.matmul(o, kb[rows, b, g, keys], qb[rows, b, g, :], start=False, stop=True)
                last.then_inc(score_ps, 1)

            def probs_v(n, b, g, first):
                pe.wait_ge(prob_ready, NH * n + HG * (g + 1))
                pe.wait_ge(v_ready, n + 1)
                if g == 0 and not first:
                    pe.wait_ge(tok_ready, n)
                for t in range(2):
                    for j in range(HG):
                        last = nc.tensor.matmul(PV[32 * j:32 * j + 32, g, :], vaug[:, b, t, HG * g + j, :],
                                                prob[:, HG * g + j, t, :], start=(t == 0), stop=(t == 1),
                                                skip_group_check=True)
                last.then_inc(pv_ps, 1)

            def heads_to_tokens(n):
                pe.wait_ge(headsT_ready, n + 1)
                for t in range(2):
                    for g in range(2):
                        last = nc.tensor.transpose(HEADS[:, t, g, :], heads_T[:, g, t * P:(t + 1) * P], ident[:])
                last.then_inc(heads_ps, 1)

            def heads_to_channels(n):
                pe.wait_ge(heads_ready, n + 1)
                for t in range(2):
                    last = nc.tensor.transpose(ATT[:, t * P:(t + 1) * P], heads[:, t, :], ident[:])
                last.then_inc(att_ps, 1)

            def output(n):
                pe.wait_ge(att_ready, n + 1)
                for t in range(2):
                    last = nc.tensor.matmul(OUT[:, t * C:(t + 1) * C], att[:, t * P:(t + 1) * P], wo[:],
                                            start=True, stop=True)
                last.then_inc(out_ps, 1)

            transpose(0, 0, True)
            project_q(0, 0)
            project_k(0, 0)
            project_v(0, 0)
            for h in range(NH):
                max_scores(0, 0, h, True)

            def image(n, b, first, last):
                transpose_maxima(n)
                if not last:
                    transpose(n + 1, 1 - b)
                if not first:
                    heads_to_tokens(n - 1)
                scores(n, b, 0, first)
                if not last:
                    project_q(n + 1, 1 - b)
                scores(n, b, 1, first)
                if not last:
                    project_k(n + 1, 1 - b)
                if not first:
                    heads_to_channels(n - 1)
                scores(n, b, 2, first)
                if not last:
                    project_v(n + 1, 1 - b)
                scores(n, b, 3, first)
                if not first:
                    output(n - 1)

                def maxima(*heads):
                    if not last:
                        for h in heads:
                            max_scores(n + 1, 1 - b, h)

                maxima(0)
                scores(n, b, 4, first)
                maxima(1)
                probs_v(n, b, 0, first)
                maxima(2)
                scores(n, b, 5, first)
                maxima(3)
                scores(n, b, 6, first)
                maxima(4)
                scores(n, b, 7, first)
                maxima(5, 6, 7)
                probs_v(n, b, 1, first)

            image_loop(pe, image)
            heads_to_tokens(N - 1)
            heads_to_channels(N - 1)
            output(N - 1)

        @block.vector
        def _(dve):
            step = Chain(dve, chain)
            nc.vector.memset(vaug[:, 0, :, :, 1:], 0.0)
            nc.vector.memset(vaug[:, 0, :, :, 0:1], 1.0).then_inc(zeros_ready, 1)
            nc.vector.memset(negmax[:], 0.0)
            norm_on_vector(dve)
            rows = ident[:].rearrange("p (j r) -> p j r", r=32)
            XY = mybir.AxisListType.XY
            nc.vector.tensor_reduce(upper[:], rows[:, :, 0:HD], XY, ALU.add)
            nc.vector.tensor_reduce(lower[:], rows[:, :, HD:32], XY, ALU.add)
            step(nc.vector.tensor_reduce(one_row[:], rows[:, :, ROW_MAX:ROW_MAX + 1], XY, ALU.add))
            dve.wait_ge(w_in, 9 * 16)
            nc.vector.tensor_scalar(bq_up[:], bq[:], upper[:], None, ALU.mult)
            nc.vector.tensor_scalar(bq_low[:], bq[:], lower[:], None, ALU.mult).then_inc(masks_ready, 1)

            def normed(m, b):
                for t in range(2):
                    tile = 2 * m + t
                    last = nc.vector.tensor_scalar(
                        xn[:, b, t, :], T[:, bass.ds(tile, 1), :].rearrange("p t c -> p (t c)"),
                        top.ln_mean[:, bass.ds(tile, 1)], top.ln_rstd[:, bass.ds(tile, 1)], ALU.subtract, ALU.mult)
                last.then_inc(xn_ready, 1)

            def queries(m, b):
                dve.wait_ge(q_low_ready, m + 1)
                for g in range(2):
                    last = nc.vector.scalar_tensor_tensor(qa[:, b, g], Q[:, g], bq[:, g:g + 1], q_low[:, b, g],
                                                          ALU.add, ALU.subtract)
                last.then_inc(qa_ready, 1)

            def keys(m, b):
                dve.wait_ge(ka_ready, m + 1)
                for g in range(2):
                    last = nc.vector.scalar_tensor_tensor(kl[:, b, g], K[:, g], bk[:, g:g + 1], ka[:, b, g],
                                                          ALU.add, ALU.subtract)
                last.then_inc(kl_ready, 1)

            def maxima(m, h):
                dve.wait_ge(max_ps, NH * m + h + 1)
                col = 32 * (h % HG) + ROW_MAX
                nc.vector.tensor_reduce(negmax[:, :, h // HG, col:col + 1],
                                        ps[:, 2 + h % 2, :].rearrange("p (t k) -> p t k", t=2), AX_X, ALU.max,
                                        negate=True).then_inc(max_ready, 1)

            def queries_low(n, b):
                dve.wait_ge(q_up_ready, n + 1)
                dve.wait_ge(maxT_ps, n + 1)
                nc.vector.tensor_tensor(qb[:, b], MAXT, q_up[:, b], ALU.add).then_inc(qb_ready, 1)

            def normalise(n):
                dve.wait_ge(heads_ps, n + 1)
                h = ps[:, 6, :].rearrange("p (h r) -> p h r", r=32)
                nc.vector.reciprocal(inv[:], h[:, :, 0]).then_inc(inv_ready, 1)
                dve.wait_ge(inv_ready, n + 1)
                nc.vector.tensor_tensor(heads[:].rearrange("p t (h d) -> p (t h) d", d=HD), h[:, :, 1:1 + HD],
                                        inv[:].unsqueeze(2).broadcast_to([P, 2 * NH, HD]),
                                        ALU.mult).then_inc(heads_ready, 1)

            def add_output(n):
                dve.wait_ge(out_ps, n + 1)
                dve.wait_ge(bo_added, n + 1)
                t = T[:, bass.ds(2 * n, 2), :].rearrange("p t c -> p (t c)")
                nc.vector.tensor_tensor(t, OUT, t, ALU.add).then_inc(tok_ready, 1)
                dve.wait_ge(tok_ready, n + 1)
                token_statistics(nc, top, n)

            normed(0, 0)
            queries(0, 0)
            keys(0, 0)
            for h in range(NH):
                maxima(0, h)

            def image(n, b, first, last):
                if not last:
                    normed(n + 1, 1 - b)
                queries_low(n, b)
                if not first:
                    normalise(n - 1)
                if not last:
                    queries(n + 1, 1 - b)
                    keys(n + 1, 1 - b)
                    maxima(n + 1, 0)
                if not first:
                    add_output(n - 1)
                if not last:
                    for h in range(1, NH):
                        maxima(n + 1, h)

            image_loop(dve, image)
            normalise(N - 1)
            add_output(N - 1)


def token_statistics(nc, top, n):
    for a in range(2):
        t = 2 * n + a
        last = nc.vector.bn_stats(top.ln_stats[:, bass.ds(t, 1), :].rearrange("p a s -> p (a s)"),
                                  top.T[:, bass.ds(t, 1), :].rearrange("p a c -> p (a c)"))
    return last


def linear_attention(nc, top, wq_dram, wkv_dram):
    T, ps, ident = top.T, top.ps, top.ident
    NH, HD = 8, 16
    EPS = 1e-6
    AW = C + NH
    with ExitStack() as ctx:
        k = Kit(nc, ctx)
        wq = k.sb("e_wq", [P, C])
        wkv = k.sb("e_wkv", [P, 2 * C])
        own = k.sb("e_own", [P, AW])
        xn = k.sb("e_xn", [P, 2, 2, C])
        xT = k.sb("e_xT", [P, 2, PIX])
        q_exp = k.sb("e_q_exp", [P, PIX])
        q_pos = k.sb("e_q_pos", [P, PIX])
        q = k.sb("e_q", [P, 2, PIX])
        k_exp = k.sb("e_k_exp", [P, 2, C])
        k_pos = k.sb("e_k_pos", [P, 2, C])
        kf = k.sb("e_k", [P, 2, 2, C])
        v = k.sb("e_v", [P, 2, 2, C + 1])
        kv = k.sb("e_kv", [P, 2, AW])
        inv = k.sb("e_inv", [P, 2, NH])
        heads = k.sb("e_heads", [P, 2, 2, C])
        w_in, chain, chain_pool, own_ready, ones_ready = (
            k.sem(f"e_{s}") for s in ("w_in", "chain", "chain_pool", "own_rd", "ones_rd"))
        xn_ready, xT_ps, xT_ready, q_ps, kv_ps, q_parts, kv_parts, qf_ready, kf_ready = (
            k.sem(f"e_{s}") for s in ("xn_rd", "xT_ps", "xT_rd", "q_ps", "kv_ps", "q_parts", "kv_parts",
                                      "qf_rd", "kf_rd"))
        sum_ps, sum_ready, out_ps, inv_ready, heads_ready, tok_ready = (
            k.sem(f"e_{s}") for s in ("sum_ps", "sum_rd", "out_ps", "inv_rd", "heads_rd", "tok_rd"))

        XT = lambda b: ps[:, 4 * b, 0:PIX]
        Q = lambda b: ps[:, 4 * b, PIX:2 * PIX]
        KV = lambda b: ps[:, 4 * b + 1, :].rearrange("p (t w c) -> p t w c", t=2, w=2)
        SUM = lambda b: ps[:, 4 * b + 2, 0:C + 1]
        OUT = lambda b: ps[:, 4 * b + 3, 0:2 * AW].rearrange("p (t c) -> p t c", t=2)

        block = ctx.enter_context(nc.Block())
        norm_on_vector, norm_on_scalar = prepare_norm(nc, top, block, k, "e")

        @block.sync
        def _(sp):
            sp.dma_start(wq[:], wq_dram).then_inc(w_in, 16)
            sp.dma_start(wkv[:], wkv_dram).then_inc(w_in, 16)

        @block.gpsimd
        def _(pool):
            step = Chain(pool, chain_pool)
            nc.gpsimd.memset(v[:, :, :, C:], 1.0).then_inc(ones_ready, 1)
            step(nc.gpsimd.memset(own[:], 1.0))
            for cols, width in ((own[:, 0:C].rearrange("p (h d) -> p h d", d=HD), HD),
                                (own[:, C:].unsqueeze(2), 1)):
                step(nc.gpsimd.affine_select(out=cols, in_=cols, compare_op=ALU.is_ge, fill=0.0, base=0,
                                             pattern=[[-HD, NH], [0, width]], channel_multiplier=1))
                step(nc.gpsimd.affine_select(out=cols, in_=cols, compare_op=ALU.is_ge, fill=0.0, base=HD - 1,
                                             pattern=[[HD, NH], [0, width]], channel_multiplier=-1))
            nc.gpsimd.memset(top.pool_scratch[:], 0.0).then_inc(own_ready, 1)

            def add_output(n, b, first, last):
                pool.wait_ge(heads_ready, n + 1)
                t = T[:, bass.ds(2 * n, 2), :]
                nc.gpsimd.tensor_tensor(t, t, heads[:, b], ALU.add).then_inc(tok_ready, 1)

            image_loop(pool, add_output)

        @block.scalar
        def _(act):
            norm_on_scalar(act)
            act.wait_ge(ones_ready, 1)

            def transposed(m, b):
                act.wait_ge(xT_ps, m + 1)
                nc.scalar.activation(xT[:, b, :], XT(b), ACT.Copy).then_inc(xT_ready, 1)

            def parts(m, b, first):
                act.wait_ge(q_ps, m + 1)
                if not first:
                    act.wait_ge(qf_ready, m)
                nc.scalar.activation(q_exp[:], Q(b), ACT.Exp)
                nc.scalar.activation(q_pos[:], Q(b), ACT.Relu).then_inc(q_parts, 1)
                act.wait_ge(kv_ps, m + 1)
                if not first:
                    act.wait_ge(kf_ready, m)
                nc.scalar.activation(k_exp[:], KV(b)[:, :, 0, :], ACT.Exp)
                nc.scalar.activation(k_pos[:], KV(b)[:, :, 0, :], ACT.Relu)
                nc.scalar.activation(v[:, b, :, 0:C], KV(b)[:, :, 1, :], ACT.Copy).then_inc(kv_parts, 1)

            def image(n, b, first, last):
                if not last:
                    transposed(n + 1, 1 - b)
                parts(n, b, first)

            transposed(0, 0)
            image_loop(act, image)

        @block.tensor
        def _(pe):
            pe.wait_ge(w_in, 2 * 16)

            def transpose(m, b):
                pe.wait_ge(xn_ready, m + 1)
                for t in range(2):
                    last = nc.tensor.transpose(XT(b)[:, t * P:(t + 1) * P], xn[:, b, t, :], ident[:])
                last.then_inc(xT_ps, 1)

            def project(n, b):
                pe.wait_ge(xT_ready, n + 1)
                nc.tensor.matmul(Q(b), wq[:], xT[:, b, :], start=True, stop=True).then_inc(q_ps, 1)
                for t in range(2):
                    last = nc.tensor.matmul(KV(b)[:, t].rearrange("p w c -> p (w c)"), xT[:, b, t * P:(t + 1) * P],
                                            wkv[:], start=True, stop=True)
                last.then_inc(kv_ps, 1)

            def sum_tokens(n, b):
                pe.wait_ge(kf_ready, n + 1)
                for t in range(2):
                    last = nc.tensor.matmul(SUM(b), kf[:, b, t, :], v[:, b, t, :], start=(t == 0), stop=(t == 1))
                last.then_inc(sum_ps, 1)

            def output(n, b):
                pe.wait_ge(sum_ready, n + 1)
                for t in range(2):
                    last = nc.tensor.matmul(OUT(b)[:, t, :], q[:, b, t * P:(t + 1) * P], kv[:, b, :],
                                            start=True, stop=True)
                last.then_inc(out_ps, 1)

            def image(n, b, first, last):
                if not last:
                    transpose(n + 1, 1 - b)
                project(n, b)
                if not first:
                    output(n - 1, 1 - b)
                sum_tokens(n, b)

            transpose(0, 0)
            image_loop(pe, image)
            output(N - 1, 1)

        @block.vector
        def _(dve):
            norm_on_vector(dve)
            dve.wait_ge(own_ready, 1)

            def normed(m, b):
                for t in range(2):
                    tile = 2 * m + t
                    last = nc.vector.tensor_scalar(
                        xn[:, b, t, :], T[:, bass.ds(tile, 1), :].rearrange("p t c -> p (t c)"),
                        top.ln_mean[:, bass.ds(tile, 1)], top.ln_rstd[:, bass.ds(tile, 1)], ALU.subtract, ALU.mult)
                last.then_inc(xn_ready, 1)

            def features(n, b):
                dve.wait_ge(q_parts, n + 1)
                nc.vector.scalar_tensor_tensor(q[:, b, :], q_exp[:], 1.0, q_pos[:], ALU.min,
                                               ALU.add).then_inc(qf_ready, 1)
                dve.wait_ge(kv_parts, n + 1)
                nc.vector.scalar_tensor_tensor(kf[:, b], k_exp[:], 1.0, k_pos[:], ALU.min,
                                               ALU.add).then_inc(kf_ready, 1)

            def sums(n, b):
                dve.wait_ge(sum_ps, n + 1)
                nc.vector.tensor_tensor(kv[:, b, 0:C], SUM(b)[:, 0:C], own[:, 0:C], ALU.mult)
                nc.vector.tensor_scalar(kv[:, b, C:], own[:, C:], SUM(b)[:, C:], None, ALU.mult).then_inc(sum_ready, 1)

            def normalise(n, b):
                dve.wait_ge(out_ps, n + 1)
                nc.vector.tensor_scalar(inv[:], OUT(b)[:, :, C:], EPS, None, ALU.add).then_inc(inv_ready, 1)
                dve.wait_ge(inv_ready, 2 * n + 1)
                nc.vector.reciprocal(inv[:], inv[:]).then_inc(inv_ready, 1)
                dve.wait_ge(inv_ready, 2 * n + 2)
                for t in range(2):
                    last = nc.vector.tensor_tensor(
                        heads[:, b, t, :].rearrange("p (h d) -> p h d", d=HD),
                        OUT(b)[:, t, 0:C].rearrange("p (h d) -> p h d", d=HD),
                        inv[:, t, :].unsqueeze(2).broadcast_to([P, NH, HD]), ALU.mult)
                last.then_inc(heads_ready, 1)

            def statistics(n):
                dve.wait_ge(tok_ready, n + 1)
                token_statistics(nc, top, n)

            def image(n, b, first, last):
                if not last:
                    normed(n + 1, 1 - b)
                features(n, b)
                if not first:
                    normalise(n - 1, 1 - b)
                sums(n, b)
                if not first:
                    statistics(n - 1)

            normed(0, 0)
            image_loop(dve, image)
            normalise(N - 1, 1)
            statistics(N - 1)


class Step:

    def __init__(self, i, c):
        self.i, self.c = i, c

    def __add__(self, d):
        return Step(self.i, self.c + d)

    @property
    def n(self):
        return 4 * self.i + self.c

    @property
    def round(self):
        return self.i + self.c // 4

    @property
    def b(self):
        return self.c % 2

    @property
    def b4(self):
        return self.c % 4

    @property
    def reuses(self):
        return not (isinstance(self.i, int) and self.c < 4)


def pipeline(eng, stages, items):
    lags = [lag for lag, _ in stages]
    start, end = max(lags) + 4, items - 1 + min(lags)
    rounds = (end - start) // 4

    def step(at, known=None):
        for lag, body in stages:
            item = None if known is None else known - lag
            if item is None or 0 <= item < items:
                body(at + -lag, item == 0, item == items - 1)

    for s in range(min(lags), start):
        step(Step(0, s), s)
    with eng.Fori(0, rounds) as i:
        for c in range(4):
            step(Step(i, start + c))
    for s in range(start + 4 * rounds, items + max(lags)):
        step(Step(0, s), s)


class Moe:

    E, TOP = 8, 2
    SLOT_TILES = -(-(TOP * TOK + E * (P - 1)) // P) // 4 * 4

    def __init__(self, nc, k, hidden, tag):
        self.F = hidden
        self.tag = tag
        self.w_in, self.w_out = (k.sb(f"{tag}_{s}", shape) for s, shape in
                                 (("w_in", [P, self.E, 2 * hidden]), ("w_out", [P, self.E, hidden // P, C])))
        self.gather = k.sb(f"{tag}_gather", [P, self.SLOT_TILES], U32)
        self.scatter = k.sb(f"{tag}_scatter", [P, self.SLOT_TILES], U32)
        self.expert = k.sb(f"{tag}_expert", [P, self.SLOT_TILES], I32)
        self.weight = k.sb(f"{tag}_weight", [P, self.TOP, TILES])
        self.weights_in = k.sem(f"{tag}_weights_in")
        self.xn_dram = nc.dram_tensor(f"{tag}_normed", [TOK, C], F32, kind="Internal").ap()
        self.y_dram = nc.dram_tensor(f"{tag}_results", [TOK * self.TOP, C], F32, kind="Internal").ap()


def route(nc, top, moe, router_dram, w_in_dram, w_out_dram):
    T, ps, ident = top.T, top.ps, top.ident
    E, SLOT_TILES = moe.E, moe.SLOT_TILES
    GROUP = 4
    NEVER = 4.0 * TOK

    def group_loop(eng, body):
        groups = TILES // GROUP
        body(0, 0, True, False)
        with eng.Fori(0, (groups - 2) // 2) as i:
            for b in (1, 2):
                body(2 * i + b, b % 2, False, False)
        body(groups - 1, (groups - 1) % 2, False, True)

    tag = moe.tag
    with ExitStack() as ctx:
        k = Kit(nc, ctx)
        sb = lambda name, shape, dt=F32: k.sb(f"{tag}_{name}", shape, dt)
        sem = lambda *names: [k.sem(f"{tag}_{s}") for s in names]
        router = sb("router", [P, E])
        xn = top.X[:].rearrange("p (t c) -> p t c", c=C)
        xT = sb("xT", [P, 2, GROUP * P])
        logits = sb("logits", [P, TILES, E])
        rest = sb("rest", [P, TILES, E])
        same = sb("same", [P, TILES, E])
        chosen = sb("chosen", [P, 2, TILES, E])
        both = sb("both", [P, TILES, E])
        best = sb("best", [P, 2, TILES])
        rank = sb("rank", [P, TILES])
        ratio = sb("ratio", [P, TILES])
        scan = sb("scan", [P, 2, TILES, E])
        total = sb("total", [P, TILES, E])
        place = sb("place", [P, TILES, E])
        beyond = sb("beyond", [P, E, TILES])
        used = sb("used", [P, E])
        ends = sb("ends", [P, 2, E])
        base = sb("base", [P, E])
        slot = sb("slot", [P, 2, TILES])
        slot_i = sb("slot_i", [P, 2, TILES], I32)
        part_i = sb("part_i", [P, 2, 2, TILES], I32)
        part = sb("part", [P, 2, 2, TILES])
        passed = sb("passed", [P, SLOT_TILES, E])
        tile_expert = sb("tile_expert", [P, SLOT_TILES])
        descending = sb("descending", [P, E])
        up_to = sb("up_to", [P, P])
        multiples = sb("multiples", [P, TILES])
        number = sb("number", [P, TILES])
        before = sb("before", [P, P])
        ones = sb("ones", [P, P])
        tile_hot = sb("tile_hot", [P, 2, GROUP, 2, SLOT_TILES])
        column = sb("column", [P, 2, GROUP, 2, SLOT_TILES], F32R)
        row = sb("row", [P, 2, 2, GROUP, P], F32R)
        found = sb("found", [P, 2, SLOT_TILES])
        token = sb("token", [P, SLOT_TILES])
        empty = sb("empty", [P, SLOT_TILES])
        target = sb("target", [P, SLOT_TILES])
        router_in, xn_stored, chain, chain_pool, consts_ready = sem(
            "router_in", "xn_stored", "chain", "chain_pool", "consts_rd")
        xn_ready, xT_ps, xT_ready, logit_ps, logit_ready = sem("xn_rd", "xT_ps", "xT_rd", "logit_ps", "logit_rd")
        gap_ready, ratio_ready, both_ready, count_ps, row_ready, table_ps = sem(
            "gap_rd", "ratio_rd", "both_rd", "count_ps", "row_rd", "table_ps")
        part_ready, tile_ready, column_ready = sem("part_rd", "tile_rd", "column_rd")

        PLACE = ps[:, 4, 0:TILES * E]
        TOTAL = ps[:, 4, TILES * E:2 * TILES * E]
        FOUND = ps[:, 5:7, 0:SLOT_TILES]

        block = ctx.enter_context(nc.Block())
        norm_on_vector, norm_on_scalar = prepare_norm(nc, top, block, k, tag)

        @block.sync
        def _(sp):
            sp.dma_start(router[:], router_dram).then_inc(router_in, 16)
            groups = moe.xn_dram.rearrange("(p g t) c -> g p t c", p=P, t=GROUP)
            for g in range(TILES // GROUP):
                sp.wait_ge(xn_ready, g + 1)
                sp.dma_start(groups[g], xn[:, g * GROUP:(g + 1) * GROUP, :]).then_inc(xn_stored, 16)
            for dst, src in ((moe.w_in, w_in_dram), (moe.w_out, w_out_dram)):
                sp.dma_start(dst[:], src).then_inc(moe.weights_in, 16)
            sp.wait_ge(xn_stored, 16 * (TILES // GROUP))

        @block.gpsimd
        def _(pool):
            step = Chain(pool, chain_pool)
            whole = dict(allow_small_or_imprecise_dtypes=True)
            nc.gpsimd.iota(up_to[:], pattern=[[1, P]], base=0, channel_multiplier=0, **whole)
            nc.gpsimd.iota(descending[:], pattern=[[-1, E]], base=E, channel_multiplier=0, **whole)
            nc.gpsimd.iota(multiples[:], pattern=[[P, TILES]], base=0, channel_multiplier=0, **whole)
            nc.gpsimd.iota(number[:], pattern=[[1, TILES]], base=1, channel_multiplier=TILES, **whole)
            nc.gpsimd.memset(ones[:], 1.0)
            step(nc.gpsimd.memset(before[:], 1.0))
            nc.gpsimd.affine_select(out=before[:], in_=before[:], compare_op=ALU.is_ge, fill=0.0, base=-1,
                                    pattern=[[1, P]], channel_multiplier=-1).then_inc(consts_ready, 1)

        @block.scalar
        def _(act):
            norm_on_scalar(act)
            act.sem_inc(logit_ready, 2)

            def copy_group(g, b):
                act.wait_ge(xT_ps, g + 1)
                act.wait_ge(logit_ps, g + 1)
                nc.scalar.activation(xT[:, b, :], ps[:, b, :], ACT.Copy).then_inc(xT_ready, 1)

            def copy_logits(g, b):
                act.wait_ge(logit_ps, g + 3)
                nc.scalar.activation(logits[:, bass.ds(g * GROUP, GROUP), :].rearrange("p t e -> p (t e)"),
                                     ps[:, 2 + b, 0:GROUP * E], ACT.Copy).then_inc(logit_ready, 1)

            copy_group(0, 0)
            with act.Fori(0, TILES // GROUP // 2 - 1) as i:
                for b in range(2):
                    copy_group(2 * i + b + 1, 1 - b)
                    copy_logits(2 * i + b, b)
            copy_group(TILES // GROUP - 1, 1)
            copy_logits(TILES // GROUP - 2, 0)
            copy_logits(TILES // GROUP - 1, 1)
            act.wait_ge(gap_ready, 1)
            nc.scalar.activation(ratio[:], rank[:], ACT.Exp).then_inc(ratio_ready, 1)
            act.sem_inc(column_ready, 2)

            def columns(g, b, first, last):
                act.wait_ge(tile_ready, g + 1)
                act.wait_ge(table_ps, g + 1)
                for t in range(GROUP):
                    ins = nc.scalar.activation(column[:, b, t], tile_hot[:, b, t], ACT.Copy,
                                               scale=number[:, bass.ds(g * GROUP + t, 1)])
                ins.then_inc(column_ready, 1)

            group_loop(act, columns)

        @block.tensor
        def _(pe):
            pe.wait_ge(router_in, 16)
            pe.sem_inc(logit_ps, 2)
            pe.sem_inc(xT_ready, 2)

            def transpose_group(g):
                pe.wait_ge(xn_ready, g + 1)
                pe.wait_ge(xT_ready, g + 1)
                for t in range(GROUP):
                    last = nc.tensor.transpose(ps[:, g % 2, t * P:(t + 1) * P], xn[:, g * GROUP + t, :], ident[:])
                last.then_inc(xT_ps, 1)

            def logits_group(g):
                b = g % 2
                pe.wait_ge(xT_ready, g + 3)
                pe.wait_ge(logit_ready, g + 1)
                for t in range(GROUP):
                    last = nc.tensor.matmul(ps[:, 2 + b, t * E:(t + 1) * E], xT[:, b, t * P:(t + 1) * P],
                                            router[:], start=True, stop=True)
                last.then_inc(logit_ps, 1)

            transpose_group(0)
            for g in range(TILES // GROUP):
                if g + 1 < TILES // GROUP:
                    transpose_group(g + 1)
                logits_group(g)
            pe.wait_ge(consts_ready, 1)
            pe.wait_ge(both_ready, 1)
            m = both[:].rearrange("p t e -> p (t e)")
            nc.tensor.matmul(PLACE, before[:], m, start=True, stop=True)
            nc.tensor.matmul(TOTAL, ones[:], m, start=True, stop=True).then_inc(count_ps, 1)
            pe.sem_inc(table_ps, 2)


            def add_group(g, b, first, last):
                pe.wait_ge(row_ready, g + 1)
                pe.wait_ge(column_ready, g + 3)
                for t in range(GROUP):
                    for c in range(2):
                        ins = nc.tensor.matmul(
                            FOUND[:, c, :], row[:, b, c, t, :],
                            column[:, b, t, c, :],
                            start=first and t == 0, stop=last and t == GROUP - 1)
                ins.then_inc(table_ps, 1)

            group_loop(pe, add_group)

        @block.vector
        def _(dve):
            step = Chain(dve, chain)
            norm_on_vector(dve)
            with dve.Fori(0, TILES // GROUP) as g:
                for t in range(GROUP):
                    tile = g * GROUP + t
                    last = nc.vector.tensor_scalar(
                        xn[:, bass.ds(tile, 1), :].rearrange("p t c -> p (t c)"),
                        T[:, bass.ds(tile, 1), :].rearrange("p t c -> p (t c)"),
                        top.ln_mean[:, bass.ds(tile, 1)], top.ln_rstd[:, bass.ds(tile, 1)], ALU.subtract, ALU.mult)
                last.then_inc(xn_ready, 1)
            dve.wait_ge(consts_ready, 1)
            dve.wait_ge(logit_ready, TILES // GROUP + 2)
            by_tile = lambda ap: ap.unsqueeze(2).broadcast_to([P, TILES, E])
            by_expert = lambda ap: ap.unsqueeze(1).broadcast_to([P, TILES, E])
            for c, left in enumerate((logits, rest)):
                step(nc.vector.tensor_reduce(best[:, c], left[:], AX_X, ALU.max))
                step(nc.vector.tensor_tensor(same[:], left[:], by_tile(best[:, c]), ALU.is_equal))
                step(nc.vector.tensor_tensor(same[:], same[:], by_expert(descending[:]), ALU.mult))
                step(nc.vector.tensor_reduce(rank[:], same[:], AX_X, ALU.max))
                step(nc.vector.tensor_tensor(chosen[:, c], by_expert(descending[:]), by_tile(rank[:]), ALU.is_equal))
                if c == 0:
                    step(nc.vector.scalar_tensor_tensor(rest[:], chosen[:, 0], -1e30, logits[:], ALU.mult, ALU.add))
            nc.vector.tensor_tensor(both[:], chosen[:, 0], chosen[:, 1], ALU.add).then_inc(both_ready, 1)
            nc.vector.tensor_tensor(rank[:], best[:, 1], best[:, 0], ALU.subtract).then_inc(gap_ready, 1)
            dve.wait_ge(count_ps, 1)
            flat = lambda ap: ap.rearrange("p t e -> p (t e)")
            step(nc.vector.tensor_copy(flat(total[:]), TOTAL))
            src, shift = total[:], 1
            for i in range(5):
                dst = scan[:, i % 2]
                nc.vector.tensor_copy(dst[:, 0:shift], src[:, 0:shift])
                step(nc.vector.tensor_tensor(dst[:, shift:], src[:, shift:], src[:, 0:TILES - shift], ALU.add))
                src, shift = dst, 2 * shift
            count = src[:, TILES - 1]
            step(nc.vector.tensor_tensor(beyond[:], count.unsqueeze(2).broadcast_to([P, E, TILES]),
                                         multiples[:].unsqueeze(1).broadcast_to([P, E, TILES]), ALU.is_gt))
            step(nc.vector.tensor_reduce(used[:], beyond[:], AX_X, ALU.add))
            sums, shift = used[:], 1
            for i in range(3):
                dst = ends[:, i % 2]
                nc.vector.tensor_copy(dst[:, 0:shift], sums[:, 0:shift])
                step(nc.vector.tensor_tensor(dst[:, shift:], sums[:, shift:], sums[:, 0:E - shift], ALU.add))
                sums, shift = dst, 2 * shift
            step(nc.vector.tensor_tensor(base[:], sums, used[:], ALU.subtract))
            step(nc.vector.tensor_tensor(place[:], src, total[:], ALU.subtract))
            step(nc.vector.tensor_tensor(flat(place[:]), PLACE, flat(place[:]), ALU.add))
            step(nc.vector.scalar_tensor_tensor(place[:], by_expert(base[:]), float(P), place[:], ALU.mult, ALU.add))
            for c in range(2):
                step(nc.vector.tensor_tensor(same[:], chosen[:, c], place[:], ALU.mult))
                step(nc.vector.tensor_reduce(slot[:, c], same[:], AX_X, ALU.add))
            step(nc.vector.tensor_copy(slot_i[:], slot[:]))
            nc.vector.tensor_scalar(part_i[:, 0], slot_i[:], 7, None, ALU.logical_shift_right)
            step(nc.vector.tensor_scalar(part_i[:, 1], slot_i[:], P - 1, None, ALU.bitwise_and))
            nc.vector.tensor_copy(part[:], part_i[:]).then_inc(part_ready, 1)
            dve.wait_ge(part_ready, 1)


            def rows(g, b, first, last):
                dve.wait_ge(column_ready, g + 1)
                nc.vector.tensor_tensor(
                    tile_hot[:, b], up_to[:, 0:SLOT_TILES].unsqueeze(1).unsqueeze(1).broadcast_to([P, GROUP, 2, SLOT_TILES]),
                    part[:, 0, :, bass.ds(g * GROUP, GROUP)].rearrange("p c t -> p t c").unsqueeze(3).broadcast_to(
                        [P, GROUP, 2, SLOT_TILES]), ALU.is_equal).then_inc(tile_ready, 1)
                dve.wait_ge(table_ps, g + 1)
                ins = nc.vector.tensor_tensor(
                    row[:, b], up_to[:].unsqueeze(1).unsqueeze(1).broadcast_to([P, 2, GROUP, P]),
                    part[:, 1, :, bass.ds(g * GROUP, GROUP)].unsqueeze(3).broadcast_to([P, 2, GROUP, P]),
                    ALU.is_equal).then_inc(row_ready, 1)

            group_loop(dve, rows)
            step(nc.vector.tensor_tensor(passed[:], up_to[:, 0:SLOT_TILES].unsqueeze(2).broadcast_to([P, SLOT_TILES, E]),
                                         sums.unsqueeze(1).broadcast_to([P, SLOT_TILES, E]), ALU.is_ge))
            step(nc.vector.tensor_reduce(tile_expert[:], passed[:], AX_X, ALU.add))
            nc.vector.tensor_scalar(moe.expert[:], tile_expert[:], float(E - 1), None, ALU.min)
            dve.wait_ge(ratio_ready, 1)
            step(nc.vector.tensor_scalar(moe.weight[:, 0], ratio[:], 1.0, None, ALU.add))
            step(nc.vector.reciprocal(moe.weight[:, 0], moe.weight[:, 0]))
            nc.vector.tensor_tensor(moe.weight[:, 1], ratio[:], moe.weight[:, 0], ALU.mult)
            dve.wait_ge(table_ps, TILES // GROUP + 2)
            step(nc.vector.tensor_copy(found[:], FOUND))
            step(nc.vector.tensor_tensor(token[:], found[:, 0], found[:, 1], ALU.add))
            nc.vector.tensor_scalar(moe.gather[:], token[:], 1.0, 0.0, ALU.subtract, ALU.max)
            nc.vector.tensor_scalar(empty[:], token[:], 0.0, NEVER, ALU.is_equal, ALU.mult)
            step(nc.vector.tensor_scalar(target[:], token[:], 2.0, -2.0, ALU.mult, ALU.add))
            step(nc.vector.tensor_tensor(target[:], target[:], empty[:], ALU.add))
            nc.vector.scalar_tensor_tensor(moe.scatter[:], found[:, 1], 0.0, target[:], ALU.is_gt, ALU.add)


def experts(nc, top, moe):
    ps, ident = top.ps, top.ident
    F, SLOT_TILES = moe.F, moe.SLOT_TILES
    CHUNKS = F // P
    tag = moe.tag
    with ExitStack() as ctx:
        k = Kit(nc, ctx)
        sb = lambda name, shape, dt=F32: k.sb(f"{tag}_{name}", shape, dt)
        sem = lambda *names: [k.sem(f"{tag}_{s}") for s in names]
        xg = sb("xg", [P, 4, C])
        xgT = sb("xgT", [P, 2, P])
        silu = sb("silu", [P, 2, F])
        h = sb("h", [P, 2, F])
        hT = sb("hT", [P, 2, F])
        y = sb("y", [P, 4, C])
        from_row = sb("from_row", [P, 4, 1], U32)
        to_row = sb("to_row", [P, 4, 1], U32)
        gathered, scattered = (sem(*(f"{s}{b}" for b in range(4))) for s in ("gathered", "scattered"))
        xg_ps, xg_ready, gu_ps, silu_ready, h_ready, h_ps, hT_ready, y_ps, y_ready, passed = sem(
            "xg_ps", "xg_rd", "gu_ps", "silu_rd", "h_rd", "h_ps", "hT_rd", "y_ps", "y_rd", "passed")
        from_ready, to_ready = sem("from_rd", "to_rd")

        if 2 * F <= 512:
            GATE = lambda b: ps[:, 2 * b, 0:F]
            UP = lambda b: ps[:, 2 * b, F:2 * F]
        else:
            GATE = lambda b: ps[:, 2 * b, 0:F]
            UP = lambda b: ps[:, 2 * b + 1, 0:F]
        XT = lambda b: ps[:, 6, b * P:(b + 1) * P]
        HT = lambda b: ps[:, 4 + b, 0:F]
        Y = lambda b: ps[:, 7, b * C:(b + 1) * C]

        block = ctx.enter_context(nc.Block())

        @block.gpsimd
        def _(pool):
            def gather(at, first, last):
                wait_apart(pool, xg_ps, at.n + 1, passed)
                wait_apart(pool, from_ready, at.n + 1, passed)
                nc.gpsimd.indirect_dma_start(
                    xg[:, at.b4, :], None, moe.xn_dram,
                    bass.IndirectOffsetOnAxis(ap=from_row[:, at.b4, :], axis=0)).then_inc(gathered[at.b4], 16)

            def scatter(at, first, last):
                wait_apart(pool, to_ready, at.n + 1, passed)
                wait_apart(pool, y_ready, at.n + 3, passed)
                nc.gpsimd.indirect_dma_start(
                    moe.y_dram, bass.IndirectOffsetOnAxis(ap=to_row[:, at.b4, :], axis=0),
                    y[:, at.b4, :], None, bounds_check=TOK * moe.TOP - 1,
                    oob_is_err=False).then_inc(scattered[at.b4], 16)

            pipeline(pool, [(-3, gather), (2, scatter)], SLOT_TILES)
            for b in range(4):
                pool.wait_ge(scattered[b], 16 * (SLOT_TILES // 4))

        @block.tensor
        def _(pe):
            pe.wait_ge(moe.weights_in, 2 * 16)
            pe.sem_inc(xg_ps, 4)
            pe.sem_inc(h_ps, 2)
            pe.sem_inc(y_ps, 2)

            expert = [pe.alloc_register(f"{tag}_expert{b}") for b in range(4)]

            nc.disable_value_cache = True

            def expert_of(at):
                return bass.RuntimeValue.of_register_unchecked(expert[at.b4]).with_bounds(min_val=0, max_val=moe.E - 1)

            def load_expert(at, first, last):
                pe.reg_load(expert[at.b4], moe.expert[0:1, bass.ds(at.n, 1)])

            def transpose_x(at, first, last):
                pe.wait_ge(gathered[at.b4], 16 * (at.round + 1))
                pe.wait_ge(xg_ready, at.n + 1)
                nc.tensor.transpose(XT(at.b), xg[:, at.b4, :], ident[:]).then_inc(xg_ps, 1)

            def gate_up(at, first, last):
                pe.wait_ge(xg_ready, at.n + 2)
                pe.wait_ge(h_ready, at.n + 1)
                w = moe.w_in[:, bass.ds(expert_of(at), 1), :].rearrange("p e f -> p (e f)")
                if 2 * F <= 512:
                    ins = nc.tensor.matmul(ps[:, 2 * at.b, 0:2 * F], xgT[:, at.b, :], w, start=True, stop=True)
                else:
                    for o, cols in ((GATE(at.b), slice(0, F)), (UP(at.b), slice(F, 2 * F))):
                        ins = nc.tensor.matmul(o, xgT[:, at.b, :], w[:, cols], start=True, stop=True)
                ins.then_inc(gu_ps, 1)

            def transpose_h(at, first, last):
                pe.wait_ge(h_ready, at.n + 3)
                pe.wait_ge(hT_ready, at.n + 1)
                for c in range(CHUNKS):
                    ins = nc.tensor.transpose(HT(at.b)[:, c * P:(c + 1) * P], h[:, at.b, c * P:(c + 1) * P], ident[:])
                ins.then_inc(h_ps, 1)

            def down(at, first, last):
                pe.wait_ge(hT_ready, at.n + 3)
                pe.wait_ge(y_ready, at.n + 2)
                for c in range(CHUNKS):
                    ins = nc.tensor.matmul(Y(at.b), hT[:, at.b, c * P:(c + 1) * P],
                                           moe.w_out[:, bass.ds(expert_of(at), 1), c, :].rearrange("p e c -> p (e c)"),
                                           start=(c == 0), stop=(c == CHUNKS - 1))
                ins.then_inc(y_ps, 1)

            pipeline(pe, [(0, gate_up), (-1, load_expert), (-1, transpose_x), (1, transpose_h), (2, down)], SLOT_TILES)
            nc.disable_value_cache = False

        @block.scalar
        def _(act):
            act.sem_inc(xg_ready, 1)
            act.sem_inc(hT_ready, 2)

            def gate(at, first, last):
                act.wait_ge(gu_ps, at.n + 1)
                act.wait_ge(h_ready, at.n + 1)
                nc.scalar.activation(silu[:, at.b, :], GATE(at.b), ACT.Silu).then_inc(silu_ready, 1)

            def copy_x(at, first, last):
                act.wait_ge(xg_ps, at.n + 5)
                nc.scalar.activation(xgT[:, at.b, :], XT(at.b), ACT.Copy).then_inc(xg_ready, 1)

            def copy_h(at, first, last):
                act.wait_ge(h_ps, at.n + 3)
                act.wait_ge(y_ps, at.n + 1)
                nc.scalar.activation(hT[:, at.b, :], HT(at.b), ACT.Copy).then_inc(hT_ready, 1)

            pipeline(act, [(0, gate), (-1, copy_x), (1, copy_h)], SLOT_TILES)

        @block.vector
        def _(dve):
            dve.sem_inc(h_ready, 2)
            dve.sem_inc(y_ready, 2)

            def hidden(at, first, last):
                dve.wait_ge(silu_ready, at.n + 1)
                dve.wait_ge(h_ps, at.n + 1)
                nc.vector.tensor_tensor(h[:, at.b, :], UP(at.b), silu[:, at.b, :], ALU.mult).then_inc(h_ready, 1)

            def result(at, first, last):
                dve.wait_ge(y_ps, at.n + 3)
                if at.reuses:
                    dve.wait_ge(scattered[at.b4], 16 * at.round)
                nc.vector.tensor_copy(to_row[:, at.b4, :], moe.scatter[:, bass.ds(at.n, 1)]).then_inc(to_ready, 1)
                nc.vector.tensor_copy(y[:, at.b4, :], Y(at.b)).then_inc(y_ready, 1)

            def source(at, first, last):
                if at.reuses:
                    dve.wait_ge(gathered[at.b4], 16 * at.round)
                nc.vector.tensor_copy(from_row[:, at.b4, :], moe.gather[:, bass.ds(at.n, 1)]).then_inc(from_ready, 1)

            pipeline(dve, [(0, hidden), (2, result), (-4, source)], SLOT_TILES)


def combine(nc, top, moe, out):
    T = top.T
    with ExitStack() as ctx:
        k = Kit(nc, ctx)
        tag = moe.tag
        PARTS = 8
        STEP = TILES // PARTS
        ys = k.sb(f"{tag}_ys", [P, TILES, moe.TOP, C])
        ys_in = [k.sem(f"{tag}_ys_in{i}") for i in range(PARTS)]
        scaled, first_added, added, stored = (
            k.sem(f"{tag}_{s}") for s in ("scaled", "first_added", "added", "stored"))
        block = ctx.enter_context(nc.Block())

        @block.sync
        def _(sp):
            parts = moe.y_dram.rearrange("(p i t c) d -> i p t c d", t=STEP, p=P, c=moe.TOP)
            for i in range(PARTS):
                sp.dma_start(ys[:, i * STEP:(i + 1) * STEP], parts[i]).then_inc(ys_in[i], 16)
            if out is not None:
                out_parts = out.rearrange("(i t p) c -> i p t c", t=STEP, p=P)
                for i in range(PARTS):
                    sp.wait_ge(added, i + 1)
                    sp.dma_start(out_parts[i], T[:, i * STEP:(i + 1) * STEP, :]).then_inc(stored, 16)
                sp.wait_ge(stored, 16 * PARTS)

        @block.scalar
        def _(act):
            for i in range(PARTS):
                act.wait_ge(ys_in[i], 16)
                for t in range(i * STEP, (i + 1) * STEP):
                    ins = nc.scalar.activation(ys[:, t, 1], ys[:, t, 1], ACT.Copy, scale=moe.weight[:, 1, t:t + 1])
                ins.then_inc(scaled, 1)

        @block.gpsimd
        def _(pool):
            for i in range(PARTS):
                tiles = slice(i * STEP, (i + 1) * STEP)
                pool.wait_ge(scaled, i + 1)
                pool.wait_ge(first_added, i + 1)
                nc.gpsimd.tensor_tensor(T[:, tiles], T[:, tiles], ys[:, tiles, 1], ALU.add).then_inc(added, 1)

        @block.vector
        def _(dve):
            def statistics(i):
                dve.wait_ge(added, i + 1)
                for t in range(i * STEP, (i + 1) * STEP):
                    nc.vector.bn_stats(top.ln_stats[:, t, :], T[:, t, :])

            for i in range(PARTS):
                dve.wait_ge(ys_in[i], 16)
                for t in range(i * STEP, (i + 1) * STEP):
                    ins = nc.vector.scalar_tensor_tensor(T[:, t, :], ys[:, t, 0], moe.weight[:, 0, t:t + 1], T[:, t, :],
                                                         ALU.mult, ALU.add)
                ins.then_inc(first_added, 1)
                if out is None and i > 0:
                    statistics(i - 1)
            if out is None:
                statistics(PARTS - 1)


def experts_layer(nc, top, hidden, tag, router_dram, w_in_dram, w_out_dram, out=None):
    with ExitStack() as ctx:
        moe = Moe(nc, Kit(nc, ctx), hidden, tag)
        route(nc, top, moe, router_dram, w_in_dram, w_out_dram)
        experts(nc, top, moe)
        combine(nc, top, moe, out)


class Top:

    def __init__(self, nc, ctx):
        k = Kit(nc, ctx)
        self.X = k.sb("X", [P, TOK])
        self.T = k.sb("T", [P, TILES, C])
        self.ps = ctx.enter_context(nc.psum_tensor("ps", [P, 8, 512], F32))
        self.ident = k.sb("ident", [P, P])
        self.pool_scratch = k.sb("pool_scratch", [P, 1])
        self.gavg = k.sb("gavg", [P, P])
        self.eps5 = k.sb("eps5", [P, 1])
        self.mean = k.sb("mean", [P, N])
        self.rstd = k.sb("rstd", [P, N])
        self.gn_stats = k.sb("gn_stats", [P, N, 6])
        self.ln_stats = k.sb("ln_stats", [P, TILES, 6])
        self.ln_mean = k.sb("ln_mean", [P, TILES])
        self.ln_rstd = k.sb("ln_rstd", [P, TILES])


def layouts(i):
    import numpy as np

    i = {k: np.asarray(v) for k, v in i.items()}
    idx1 = np.zeros((TAP_TILES, QUADS), np.int64)
    idx2 = np.zeros((TAP_TILES, QUADS), np.int64)
    for t in range(TAP_TILES):
        for q in range(QUADS):
            (row, col), _ = tap_of(t, q)
            idx1[t, q] = row * KS + col
            if row % 2 == 0 and col % 2 == 0:
                idx2[t, q] = row // 2 * 3 + col // 2

    def tap_values(v, idx):
        return np.repeat(v.reshape(-1)[idx].T, CM, axis=0)

    fuse = i["L0_conv_fuse_w"].reshape(C, 2 * CM).T
    out = {
        "x": i["x"].transpose(1, 0, 2, 3).reshape(C, TOK),
        "cw": np.tile(i["L0_conv_conv_w"].reshape(CM, C).T, (1, QUADS)),
        "cb": np.tile(i["L0_conv_conv_b"].reshape(CM, 1), (QUADS, 1)),
        "f1": np.tile(fuse[:CM], (QUADS, 1)),
        "f2": np.tile(fuse[CM:], (QUADS, 1)),
        "fuse": fuse,
        "ab": np.concatenate([i["L0_conv_adap_bias"], i["L0_conv_atrous_bias"]]).reshape(2 * CM, 1),
        "fb": i["L0_conv_fuse_b"].reshape(C, 1),
        "taps": np.stack([tap_values(i["L0_conv_conv_kernel_w"], idx1), tap_values(i["L0_conv_conv_kernel_b"], idx1),
                          tap_values(i["L0_conv_conv_kernel2_w"], idx2), tap_values(i["L0_conv_conv_kernel2_b"], idx2)],
                         axis=1),
        "scal": np.concatenate([i[f"L0_conv_{n}"].reshape(-1) for n in
                                ("conv_k_w", "conv_k_b", "conv_k2_w", "conv_k2_b")]),
    }

    def heads_apart(w, front, copies):
        w = w.reshape(w.shape[0], 8, 16)
        o = np.zeros((w.shape[0], 8, 32), w.dtype)
        for c in range(copies):
            o[:, :, front + 16 * c:front + 16 * c + 16] = w
        return o.reshape(w.shape[0], 256)

    def as_partitions(v):
        return v.reshape(2, P).T

    out |= {
        "wq": heads_apart(i["L2_attn_Wq"], 0, 2),
        "wk": heads_apart(i["L2_attn_Wk"], 0, 2),
        "wv": i["L2_attn_Wv"],
        "wo": i["L2_attn_Wo"],
        "bq": as_partitions(heads_apart(i["L2_attn_bq"][None], 0, 2)),
        "bk": as_partitions(heads_apart(i["L2_attn_bk"][None], 0, 2)),
        "bv": i["L2_attn_bv"][:, None],
        "bo": i["L2_attn_bo"],
        "lin_wq": i["L3_attn_Wq"].T,
        "lin_wkv": i["L3_attn_Wkv"].T,
    }

    def expert_weights(gate, up, down):
        e, f, c = down.shape
        return (np.concatenate([gate, up], axis=2).transpose(1, 0, 2),
                down.reshape(e, f // P, P, c).transpose(2, 0, 1, 3))

    out["d_router"] = i["L2_ffn_router_w"].T
    out["d_in"], out["d_out"] = expert_weights(i["L2_ffn_w_gate"], i["L2_ffn_w_up"], i["L2_ffn_w_down"])
    out["f_router"] = i["L3_ffn_Wg"]
    out["f_in"], out["f_out"] = expert_weights(i["L3_ffn_W"], i["L3_ffn_V"], i["L3_ffn_W2"])
    return {k: np.ascontiguousarray(v) for k, v in out.items()}


def program(nc, d, out):
    Kit.used.clear()
    with ExitStack() as ctx:
        top = Top(nc, ctx)
        adaptive_conv(nc, top, *[d[n] for n in ("x", "cw", "cb", "f1", "f2", "fuse", "ab", "fb", "taps", "scal")])
        box_conv(nc, top)
        softmax_attention(nc, top, *[d[n] for n in ("wq", "wk", "wv", "wo", "bq", "bk", "bv", "bo")])
        clear_semaphores(nc)
        experts_layer(nc, top, 256, "d", d["d_router"], d["d_in"], d["d_out"])
        linear_attention(nc, top, d["lin_wq"], d["lin_wkv"])
        experts_layer(nc, top, 512, "f", d["f_router"], d["f_in"], d["f_out"], out)


def kernel(**inputs):
    import concourse.bacc as _bacc
    from concourse.bass_utils import run_bass_kernel_spmd as _run

    nc = _bacc.Bacc("TRN2", target_bir_lowering=False, num_devices=1)
    laid_out = layouts(inputs)
    drams = {name: nc.dram_tensor(f"in_{name}", a.shape, mybir.dt.from_np(a.dtype), kind="ExternalInput").ap()
             for name, a in laid_out.items()}
    out = nc.dram_tensor("out_tokens", (TOK, C), F32, kind="ExternalOutput").ap()
    program(nc, drams, out)
    r = _run(nc, [{f"in_{name}": a for name, a in laid_out.items()}], core_ids=[0])
    tokens = r.results[0]["out_tokens"]
    return tokens.reshape(N, PIX, C).transpose(0, 2, 1).reshape(N, C, H, W)
```

```python
from contextlib import ExitStack

import concourse.bass as bass
from concourse import mybir

F32 = mybir.dt.float32
F32R = mybir.dt.float32r
U32 = mybir.dt.uint32
I32 = mybir.dt.int32
ALU = mybir.AluOpType
ACT = mybir.ActivationFunctionType
AX_X = mybir.AxisListType.X

P = 128
N, C, H, W = 16, 128, 16, 16
PIX = H * W
TOK = N * PIX
TILES = TOK // P
GN_GROUP = C // 32
CM = 32
QUADS = P // CM
KS = 5
TAP_TILES = 7
FR, FC = 21, 20
GN_EPS, LN_EPS = 1e-5, 1e-5


def tap_of(t, quad):
    if t < KS:
        return (t, quad), True
    if t == KS:
        return (quad, KS - 1), True
    return (KS - 1, KS - 1), quad == QUADS - 1


class Chain:

    def __init__(self, eng, sem, base=0):
        self.eng, self.sem, self.n = eng, sem, base

    def __call__(self, ins):
        ins.then_inc(self.sem, 1)
        self.n = self.n + 1
        self.eng.wait_ge(self.sem, self.n)


class Kit:

    used = []

    def __init__(self, nc, ctx):
        self.nc, self.ctx = nc, ctx

    def sb(self, name, shape, dt=F32):
        return self.ctx.enter_context(self.nc.sbuf_tensor(name, shape, dt))

    def sem(self, name):
        s = self.ctx.enter_context(self.nc.semaphore(name))
        Kit.used.append(s)
        return s


class Step:

    def __init__(self, i, c, width):
        self.i, self.c, self.width = i, c, width

    def __add__(self, d):
        return Step(self.i, self.c + d, self.width)

    @property
    def n(self):
        return self.width * self.i + self.c

    @property
    def round(self):
        return self.i + self.c // self.width

    @property
    def b(self):
        return self.c % 2

    @property
    def b4(self):
        return self.c % 4

    @property
    def reuses(self):
        return not (isinstance(self.i, int) and self.c < self.width)


def pipeline(eng, stages, items, width=4):
    lags = [lag for lag, _ in stages]
    start, end = max(lags) + width, items - 1 + min(lags)
    rounds = (end - start) // width

    def step(at, known=None):
        for lag, body in stages:
            item = None if known is None else known - lag
            if item is None or 0 <= item < items:
                body(at + -lag, item == 0, item == items - 1)

    for s in range(min(lags), start):
        step(Step(0, s, width), s)
    with eng.Fori(0, rounds) as i:
        for c in range(width):
            step(Step(i, start + c, width))
    for s in range(start + width * rounds, items + max(lags)):
        step(Step(0, s, width), s)


def clear_semaphores(nc):
    numbers = sorted(s.num for s in Kit.used)
    assert numbers[-1] - numbers[0] + 1 == len(numbers)
    Kit.used.clear()
    with nc.Block() as block:
        @block.gpsimd
        def _(pool):
            nc.gpsimd.sem_clear(range(numbers[0], numbers[-1] + 1))


def channel_means(nc, step, stats, out):
    step(nc.vector.tensor_tensor(out, stats[:, :, 1], stats[:, :, 4], ALU.add))
    return nc.vector.tensor_scalar(out, out, 0.5, None, ALU.mult)


def variances(nc, step, stats, tmp, out, count):
    step(nc.vector.tensor_tensor(tmp, stats[:, :, 1], stats[:, :, 4], ALU.subtract))
    step(nc.vector.scalar_tensor_tensor(tmp, tmp, 0.25, tmp, ALU.mult, ALU.mult))
    step(nc.vector.tensor_tensor(out, stats[:, :, 2], stats[:, :, 5], ALU.add))
    return nc.vector.scalar_tensor_tensor(out, out, 1.0 / count, tmp, ALU.mult, ALU.add)


def adaptive_conv(nc, top, x_dram, cw_dram, cb_dram, f1_dram, f2_dram, fuse_dram, ab_dram, fb_dram,
                  taps_dram, scal_dram):
    X, ps = top.X, top.ps
    with ExitStack() as ctx:
        k = Kit(nc, ctx)
        xn = top.T[:].rearrange("p t c -> p (t c)")
        cw = k.sb("cw", [P, P])
        cb = k.sb("cb", [P, 1])
        f1 = k.sb("f1", [P, P])
        f2 = k.sb("f2", [P, P])
        fuse = k.sb("fuse", [2 * CM, P])
        ab = k.sb("ab", [2 * CM, 1])
        fb = k.sb("fb", [P, 1])
        taps = k.sb("taps", [P, 4, TAP_TILES])
        scal = k.sb("scal", [P, 6])
        gavg = top.gavg
        stats = k.sb("stats", [P, N, 6])
        mean_c = k.sb("mean_c", [P, N])
        dev = k.sb("dev", [P, N])
        sq = k.sb("sq", [P, N])
        shift = k.sb("shift_a", [P, N])
        pooled = k.sb("pooled", [P, N])
        g = k.sb("g", [P, N])
        kimg = k.sb("kimg", [P, N, TAP_TILES])
        kdom = k.sb("kdom", [P, TAP_TILES])
        counts = k.sb("counts", [P, 2, TAP_TILES])
        gk = k.sb("gk", [P, 2, N, TAP_TILES])
        cbias = k.sb("cbias", [P, 1])
        wimg = k.sb("wimg", [P, 2, TAP_TILES, P])
        fcol = k.sb("fcol", [P, N, FR * FC])
        frow = k.sb("frow", [P, N, FR * FC])
        fcol_v = fcol[:].rearrange("p n (r c) -> p n r c", c=FC)
        frow_v = frow[:].rearrange("p n (r c) -> p n r c", c=FC)
        x_in = [k.sem(f"x_in{i}") for i in range(4)]
        w_in, taps_in = k.sem("w_in"), k.sem("taps_in")
        pool_chain, dve_chain = k.sem("pool_chain_a"), k.sem("dve_chain_a")
        consts_ready, pads_ready = k.sem("consts_ready"), k.sem("pads_ready")
        mean_ready, mean_ps, var_ready, var_ps = (k.sem(s) for s in ("mean_rd", "mean_ps", "var_rd", "var_ps"))
        std_ready, xn_ready = k.sem("std_ready"), k.sem("xn_ready")
        pooled_ready, g_ps, g_ready, bias_ps = (k.sem(s) for s in ("pooled_rd", "g_ps", "g_rd", "bias_ps"))
        feat_ps, feat_act, shift_ready = k.sem("feat_ps"), k.sem("feat_act"), k.sem("shift_rd")
        wimg_ready, wimg_used, out_read = (k.sem(s) for s in ("wimg_rd", "wimg_used", "out_read"))
        wimg_half, lone_ready, gk_ready = k.sem("wimg_half"), k.sem("lone_rd"), k.sem("gk_rd")
        BOTH, LONE = (0, 2, 4, 5, 6), (1, 3)

        MEAN, VAR = ps[:, 4, 0:N], ps[:, 4, N:2 * N]
        G, BIAS = ps[:, 5, 0:N], ps[:, 5, N:N + 1]

        block = ctx.enter_context(nc.Block())

        @block.sync
        def _(sp):
            for i in range(4):
                sp.dma_start(X[:, i * (TOK // 4):(i + 1) * (TOK // 4)],
                             x_dram[:, i * (TOK // 4):(i + 1) * (TOK // 4)]).then_inc(x_in[i], 16)
            for dst, src in ((cw, cw_dram), (cb, cb_dram), (f1, f1_dram), (f2, f2_dram), (fuse, fuse_dram),
                             (ab, ab_dram), (fb, fb_dram)):
                sp.dma_start(dst[:], src).then_inc(w_in, 16)
            sp.dma_start(taps[:], taps_dram).then_inc(taps_in, 16)
            sp.dma_start(scal[:], scal_dram.partition_broadcast(P)).then_inc(taps_in, 16)

        @block.gpsimd
        def _(pool):
            step = Chain(pool, pool_chain)
            step(nc.gpsimd.memset(top.ident[:], 1.0))
            step(nc.gpsimd.affine_select(out=top.ident[:], in_=top.ident[:], compare_op=ALU.is_equal, fill=0.0,
                                         base=0, pattern=[[-1, P]], channel_multiplier=1))
            step(nc.gpsimd.memset(gavg[:], 1.0 / GN_GROUP))
            gv = gavg[:].rearrange("p (g r) -> p g r", r=GN_GROUP)
            step(nc.gpsimd.affine_select(out=gv, in_=gv, compare_op=ALU.is_ge, fill=0.0, base=0,
                                         pattern=[[-GN_GROUP, P // GN_GROUP], [0, GN_GROUP]], channel_multiplier=1))
            nc.gpsimd.affine_select(out=gv, in_=gv, compare_op=ALU.is_ge, fill=0.0, base=GN_GROUP - 1,
                                    pattern=[[GN_GROUP, P // GN_GROUP], [0, GN_GROUP]],
                                    channel_multiplier=-1).then_inc(consts_ready, 1)
            nc.gpsimd.memset(fcol[:], 0.0)
            nc.gpsimd.memset(frow[:], 0.0).then_inc(pads_ready, 1)

        @block.scalar
        def _(act):
            act.wait_ge(var_ps, 1)
            act.wait_ge(std_ready, 1)
            nc.scalar.activation(top.rstd[:], VAR, ACT.Sqrt, bias=top.eps5[:]).then_inc(std_ready, 1)
            act.wait_ge(shift_ready, 1)

            def normed(pair):
                for a in range(2):
                    n = 2 * pair + a
                    last = nc.scalar.activation(xn[:, bass.ds(n * PIX, PIX)], X[:, bass.ds(n * PIX, PIX)], ACT.Identity,
                                                bias=shift[:, bass.ds(n, 1)], scale=top.rstd[:, bass.ds(n, 1)])
                last.then_inc(xn_ready, 1)

            def features(pair, b):
                act.wait_ge(feat_ps, pair + 1)
                src = ps[:, b, :].rearrange("p (n r c) -> p n r c", n=2, c=W)
                for q in range(QUADS):
                    rows = slice(q * CM, (q + 1) * CM)
                    for dst, r0, c0 in ((fcol_v, 3, 3 - q), (frow_v, 3 - q, 2)):
                        o = dst[rows, bass.ds(2 * pair, 2), r0:r0 + H, c0:c0 + W]
                        last = nc.scalar.activation(o, src[rows], ACT.Relu, bias=cb[rows])
                last.then_inc(feat_act, 1)

            def lone_taps(pair):
                for a in range(2):
                    n = 2 * pair + a
                    act.wait_ge(wimg_used, n + 1)
                    for t in LONE:
                        last = nc.scalar.activation(wimg[:, a, t, :], f1[:], ACT.Copy,
                                                    scale=gk[:, 0, bass.ds(n, 1), t])
                    last.then_inc(lone_ready, 1)

            for pair in range(2):
                normed(pair)
            act.wait_ge(w_in, 7 * 16)
            act.wait_ge(pads_ready, 1)
            act.wait_ge(gk_ready, 2)
            with act.Fori(0, N // 4 - 1) as i:
                for b in range(2):
                    features(2 * i + b, b)
                    normed(2 * i + b + 2)
                    lone_taps(2 * i + b)
            for b in range(2):
                features(N // 2 - 2 + b, b)
                lone_taps(N // 2 - 2 + b)

        @block.tensor
        def _(pe):
            pe.wait_ge(mean_ready, 1)
            pe.wait_ge(consts_ready, 1)
            nc.tensor.matmul(MEAN, gavg[:], mean_c[:], start=True, stop=True).then_inc(mean_ps, 1)
            pe.wait_ge(var_ready, 1)
            nc.tensor.matmul(VAR, gavg[:], sq[:], start=True, stop=True).then_inc(var_ps, 1)
            pe.wait_ge(w_in, 7 * 16)
            pe.wait_ge(pooled_ready, 1)
            nc.tensor.matmul(G, cw[:], pooled[:], start=True, stop=True).then_inc(g_ps, 1)
            pe.wait_ge(g_ready, 1)
            nc.tensor.matmul(BIAS, fuse[:], ab[:], start=True, stop=True).then_inc(bias_ps, 1)

            def features(pair, b):
                pe.wait_ge(xn_ready, pair + 1)
                nc.tensor.matmul(ps[:, b, :], cw[:], xn[:, bass.ds(pair * 2 * PIX, 2 * PIX)],
                                 start=True, stop=True).then_inc(feat_ps, 1)

            def convolve(pair, b):
                for a in range(2):
                    pe.wait_ge(wimg_ready, 2 * pair + a + 1)
                    pe.wait_ge(lone_ready, 2 * pair + a + 1)
                    for t in range(TAP_TILES):
                        src, r0, c0 = (fcol_v, 1 + t, 1) if t < KS else (frow_v, 1 + t - KS, KS - 1)
                        rhs = src[:, bass.ds(2 * pair + a, 1), r0:r0 + H, c0:c0 + W]
                        last = nc.tensor.matmul(ps[:, 2 + b, a * PIX:(a + 1) * PIX], wimg[:, a, t, :],
                                                rhs.rearrange("p n r c -> p (n r) c"),
                                                start=(t == 0), stop=(t == TAP_TILES - 1))
                    last.then_inc(wimg_used, 1)

            for b in range(2):
                features(b, b)
            keep_warm(nc, top, 3, 7, xn)
            with pe.Fori(0, N // 4 - 1) as i:
                for b in range(2):
                    pair = 2 * i + b
                    pe.wait_ge(feat_act, pair + 1)
                    pe.wait_ge(out_read, pair + 1)
                    convolve(pair, b)
                    features(pair + 2, b)
            for b in range(2):
                pair = N // 2 - 2 + b
                pe.wait_ge(feat_act, pair + 1)
                pe.wait_ge(out_read, pair + 1)
                convolve(pair, b)

        @block.vector
        def _(dve):
            step = Chain(dve, dve_chain)
            nc.vector.memset(top.eps5[:], GN_EPS).then_inc(std_ready, 1)
            step(nc.vector.memset(counts[:, 0, :], 1.0))
            step(nc.vector.memset(counts[:, 1, :], 0.0))
            for q in range(QUADS):
                for t in range(TAP_TILES):
                    (row, col), real = tap_of(t, q)
                    rows = slice(q * CM, (q + 1) * CM)
                    if not real:
                        step(nc.vector.memset(counts[rows, 0, t:t + 1], 0.0))
                    elif row % 2 == 0 and col % 2 == 0:
                        step(nc.vector.memset(counts[rows, 1, t:t + 1], 1.0))
            for n in range(N):
                if n % 4 == 0:
                    dve.wait_ge(x_in[n // 4], 16)
                last = nc.vector.bn_stats(stats[:, n, :], X[:, n * PIX:(n + 1) * PIX])
            step(last)
            channel_means(nc, step, stats, mean_c[:]).then_inc(mean_ready, 1)
            dve.wait_ge(mean_ready, 1)
            step(variances(nc, step, stats, dev[:], sq[:], PIX))
            dve.wait_ge(mean_ps, 1)
            step(nc.vector.tensor_copy(top.mean[:], MEAN))
            step(nc.vector.tensor_tensor(dev[:], mean_c[:], top.mean[:], ALU.subtract))
            step(nc.vector.tensor_tensor(dev[:], dev[:], dev[:], ALU.mult))
            nc.vector.tensor_tensor(sq[:], sq[:], dev[:], ALU.add).then_inc(var_ready, 1)
            dve.wait_ge(std_ready, 2)
            step(nc.vector.reciprocal(top.rstd[:], top.rstd[:]))
            step(nc.vector.tensor_tensor(pooled[:], mean_c[:], top.mean[:], ALU.subtract))
            nc.vector.scalar_tensor_tensor(shift[:], top.mean[:], -1.0, top.rstd[:], ALU.mult,
                                           ALU.mult).then_inc(shift_ready, 1)
            nc.vector.tensor_tensor(pooled[:], pooled[:], top.rstd[:], ALU.mult).then_inc(pooled_ready, 1)
            dve.wait_ge(g_ps, 1)
            dve.wait_ge(w_in, 7 * 16)
            dve.wait_ge(taps_in, 2 * 16)
            nc.vector.tensor_scalar(g[:], G, cb[:], 0.0, ALU.add, ALU.max).then_inc(g_ready, 1)
            dve.wait_ge(g_ready, 1)
            for m in range(2):
                each = lambda ap: ap.unsqueeze(1).broadcast_to([P, N, TAP_TILES])
                step(nc.vector.tensor_tensor(kimg[:], g[:].unsqueeze(2).broadcast_to([P, N, TAP_TILES]),
                                             each(taps[:, 2 * m, :]), ALU.mult))
                step(nc.vector.tensor_tensor(kimg[:], kimg[:], each(taps[:, 2 * m + 1, :]), ALU.add))
                step(nc.vector.tensor_reduce(kdom[:], kimg[:].rearrange("p n t -> p t n"), AX_X, ALU.add))
                step(nc.vector.tensor_scalar(kdom[:], kdom[:], 1.0 / N, scal[:, 3 * m + 1:3 * m + 2],
                                             ALU.mult, ALU.mult))
                step(nc.vector.tensor_scalar(kdom[:], kdom[:], scal[:, 3 * m + 2:3 * m + 3], None, ALU.add))
                step(nc.vector.scalar_tensor_tensor(kimg[:], kimg[:], scal[:, 3 * m:3 * m + 1], each(kdom[:]),
                                                    ALU.mult, ALU.add))
                nc.vector.scalar_tensor_tensor(gk[:, m, :, :], kimg[:], 0.0, each(counts[:, m, :]), ALU.max,
                                               ALU.mult).then_inc(gk_ready, 1)
                dve.wait_ge(gk_ready, m + 1)
            dve.wait_ge(bias_ps, 1)
            step(nc.vector.tensor_tensor(cbias[:], BIAS, fb[:], ALU.add))

            def stationary(pair, a):
                n = 2 * pair + a
                dve.wait_ge(wimg_used, n + 1)
                for t in BOTH:
                    last = nc.vector.tensor_scalar(wimg[:, a, t, :], f1[:], gk[:, 0, bass.ds(n, 1), t], None, ALU.mult)
                last.then_inc(wimg_half, 1)
                dve.wait_ge(wimg_half, n + 1)
                for t in BOTH:
                    last = nc.vector.scalar_tensor_tensor(wimg[:, a, t, :], f2[:], gk[:, 1, bass.ds(n, 1), t],
                                                          wimg[:, a, t, :], ALU.mult, ALU.add)
                last.then_inc(wimg_ready, 1)

            def outputs(pair, b):
                dve.wait_ge(wimg_used, 2 * pair + 4)
                at = X[:, bass.ds(pair * 2 * PIX, 2 * PIX)]
                nc.vector.scalar_tensor_tensor(at, ps[:, 2 + b, :], cbias[:], at, ALU.add,
                                               ALU.add).then_inc(out_read, 1)
                dve.wait_ge(out_read, pair + 3)
                for a in range(2):
                    n = 2 * pair + a
                    nc.vector.bn_stats(top.gn_stats[:, bass.ds(n, 1), :].rearrange("p a s -> p (a s)"),
                                       X[:, bass.ds(n * PIX, PIX)])

            dve.sem_inc(wimg_used, 2)
            dve.sem_inc(out_read, 2)
            for a in range(2):
                stationary(0, a)
            with dve.Fori(0, N // 4 - 1) as i:
                for b in range(2):
                    for a in range(2):
                        stationary(2 * i + b + 1, a)
                    outputs(2 * i + b, b)
            for a in range(2):
                stationary(N // 2 - 1, a)
            outputs(N // 2 - 2, 0)
            outputs(N // 2 - 1, 1)


def box_conv(nc, top, load_next):
    X, T, ps = top.X, top.T, top.ps
    PH, PW = H + 2, W + 2
    with ExitStack() as ctx:
        k = Kit(nc, ctx)
        mean_c = k.sb("mean_c2", [P, N])
        dev = k.sb("dev2", [P, N])
        sq = k.sb("sq2", [P, N])
        shift = k.sb("shift", [P, N])
        pad = k.sb("pad", [P, 4, PH * PW])
        rows = k.sb("rows", [P, 4, PH * W])
        mid = k.sb("mid", [P, 4, PIX])
        gavg = top.gavg
        dve_chain = k.sem("dve_chain_b")
        mean_ready, mean_ps, var_ready, var_ps, std_ready, norm_ready = (
            k.sem(s) for s in ("b_mean_rd", "b_mean_ps", "b_var_rd", "b_var_ps", "b_std_rd", "b_norm_rd"))
        pad_ready, rows_half, rows_ready, mid_ready, tok_ps, tok_ready = (
            k.sem(s) for s in ("pad_rd", "rows_half", "rows_rd", "mid_rd", "tok_ps", "tok_rd"))
        MEAN, VAR = ps[:, 4, 0:N], ps[:, 4, N:2 * N]
        image = lambda n: X[:, bass.ds(n * PIX, PIX)]

        block = ctx.enter_context(nc.Block())

        @block.sync
        def _(sp):
            load_next(sp)

        @block.scalar
        def _(act):
            act.wait_ge(var_ps, 1)
            nc.scalar.activation(top.rstd[:], VAR, ACT.Sqrt, bias=top.eps5[:]).then_inc(std_ready, 1)
            act.wait_ge(norm_ready, 1)

            act.sem_inc(tok_ready, 4)

            def normed(at, first, last):
                act.wait_ge(rows_ready, at.n + 1)
                inner = pad[:, at.b4, :].rearrange("p (r c) -> p r c", c=PW)[:, 1:1 + H, 1:1 + W]
                nc.scalar.activation(inner, image(at.n).rearrange("p (r c) -> p r c", c=W), ACT.Identity,
                                     bias=shift[:, bass.ds(at.n, 1)],
                                     scale=top.rstd[:, bass.ds(at.n, 1)]).then_inc(pad_ready, 1)

            def tokens(at, first, last):
                act.wait_ge(tok_ps, at.n + 5)
                nc.scalar.activation(T[:, bass.ds(2 * at.n, 2), :].rearrange("p t c -> p (t c)"),
                                     ps[:, at.b4, 0:2 * P], ACT.Copy).then_inc(tok_ready, 1)

            pipeline(act, [(-2, normed), (1, tokens)], N)

        @block.gpsimd
        def _(pool):
            nc.gpsimd.memset(pad[:], 0.0).then_inc(rows_ready, 4)

            def middle(at, first, last):
                pool.wait_ge(rows_ready, at.n + 5)
                pool.wait_ge(tok_ps, at.n + 1)
                nc.gpsimd.tensor_tensor(mid[:, at.b4, :], image(at.n), rows[:, at.b4, W:W + PIX],
                                        ALU.add).then_inc(mid_ready, 1)

            pipeline(pool, [(0, middle)], N)

        @block.tensor
        def _(pe):
            pe.wait_ge(mean_ready, 1)
            nc.tensor.matmul(MEAN, gavg[:], mean_c[:], start=True, stop=True).then_inc(mean_ps, 1)
            pe.wait_ge(var_ready, 1)
            nc.tensor.matmul(VAR, gavg[:], sq[:], start=True, stop=True).then_inc(var_ps, 1)
            pe.sem_inc(tok_ps, 4)

            def transpose(at, first, last):
                pe.wait_ge(mid_ready, at.n + 1)
                pe.wait_ge(tok_ready, at.n + 1)
                for half in range(2):
                    o = ps[:, at.b4, half * P:(half + 1) * P]
                    row = half * P
                    nc.tensor.matmul(o, rows[:, at.b4, row:row + P], top.ident[:], start=True, stop=False)
                    nc.tensor.matmul(o, rows[:, at.b4, row + 2 * W:row + 2 * W + P], top.ident[:], start=False,
                                     stop=False)
                    ins = nc.tensor.matmul(o, mid[:, at.b4, row:row + P], top.ident[:], start=False, stop=True)
                ins.then_inc(tok_ps, 1)

            pipeline(pe, [(0, transpose)], N)

        @block.vector
        def _(dve):
            step = Chain(dve, dve_chain)
            stats = top.gn_stats
            channel_means(nc, step, stats, mean_c[:]).then_inc(mean_ready, 1)
            dve.wait_ge(mean_ready, 1)
            step(variances(nc, step, stats, dev[:], sq[:], PIX))
            dve.wait_ge(mean_ps, 1)
            step(nc.vector.tensor_copy(top.mean[:], MEAN))
            step(nc.vector.tensor_tensor(dev[:], mean_c[:], top.mean[:], ALU.subtract))
            step(nc.vector.tensor_tensor(dev[:], dev[:], dev[:], ALU.mult))
            nc.vector.tensor_tensor(sq[:], sq[:], dev[:], ALU.add).then_inc(var_ready, 1)
            dve.wait_ge(std_ready, 1)
            step(nc.vector.reciprocal(top.rstd[:], top.rstd[:]))
            nc.vector.scalar_tensor_tensor(shift[:], top.mean[:], -1.0, top.rstd[:], ALU.mult,
                                           ALU.mult).then_inc(norm_ready, 1)

            def row_sums(at, first, last):
                dve.wait_ge(pad_ready, at.n + 1)
                dve.wait_ge(tok_ps, at.n + 1)
                p = pad[:, at.b4, :].rearrange("p (r c) -> p r c", c=PW)
                o = rows[:, at.b4, :].rearrange("p (r c) -> p r c", c=W)
                nc.vector.tensor_tensor(o, p[:, :, 0:W], p[:, :, 1:1 + W], ALU.add).then_inc(rows_half, 1)
                dve.wait_ge(rows_half, at.n + 1)
                nc.vector.tensor_tensor(o, o, p[:, :, 2:2 + W], ALU.add).then_inc(rows_ready, 1)

            def statistics(at, first, last):
                dve.wait_ge(tok_ready, at.n + 5)
                token_statistics(nc, top, at.n)

            pipeline(dve, [(0, row_sums), (3, statistics)], N)


def keep_warm(nc, top, products, bank, rhs=None):
    rhs = top.T[:].rearrange("p t c -> p (t c)") if rhs is None else rhs
    for _ in range(products):
        nc.tensor.matmul(top.ps[:, bank, :], top.ident[:], rhs[:, 0:512], start=True, stop=True)


def prepare_norm(nc, top, block, k, tag):
    chain, var_ready, std_ready, norm_ready = (
        k.sem(f"{tag}_{s}") for s in ("ln_chain", "ln_var_rd", "ln_std_rd", "ln_rd"))
    tmp = k.sb(f"{tag}_ln_tmp", [P, TILES])

    def on_vector(dve):
        step = Chain(dve, chain)
        step(channel_means(nc, step, top.ln_stats, top.ln_mean[:]))
        variances(nc, step, top.ln_stats, tmp[:], top.ln_rstd[:], C).then_inc(var_ready, 1)
        dve.wait_ge(std_ready, 1)
        nc.vector.reciprocal(top.ln_rstd[:], top.ln_rstd[:]).then_inc(norm_ready, 1)
        dve.wait_ge(norm_ready, 1)

    def on_scalar(act):
        act.wait_ge(var_ready, 1)
        nc.scalar.activation(top.ln_rstd[:], top.ln_rstd[:], ACT.Sqrt, bias=top.eps5[:]).then_inc(std_ready, 1)

    return on_vector, on_scalar


def wait_apart(eng, sem, value, passed):
    eng.wait_ge(sem, value)
    eng.sem_inc(passed, 1)


def image_loop(eng, body):
    body(0, 0, True, False)
    with eng.Fori(0, (N - 2) // 2) as i:
        for b in (1, 2):
            body(2 * i + b, b % 2, False, False)
    body(N - 1, (N - 1) % 2, False, True)


class AttentionWeights:

    def __init__(self, k):
        self.wq = k.sb("wq", [P, 2, P])
        self.wk = k.sb("wk", [P, 2, P])
        self.wv = k.sb("wv", [P, P])
        self.wo = k.sb("wo", [P, P])
        self.bq = k.sb("bq", [P, 2])
        self.bk = k.sb("bk", [P, 2])
        self.bv = k.sb("bv", [P, 1])
        self.bo = k.sb("bo", [P, 2, P])
        self.loaded = k.sem("attention_weights_in")

    def load(self, sp, wq, wk, wv, wo, bq, bk, bv, bo):
        for dst, src in ((self.wq, wq), (self.wk, wk)):
            sp.dma_start(dst[:].rearrange("p g c -> p (g c)"), src).then_inc(self.loaded, 16)
        for dst, src in ((self.wv, wv), (self.wo, wo), (self.bq, bq), (self.bk, bk), (self.bv, bv)):
            sp.dma_start(dst[:], src).then_inc(self.loaded, 16)
        for t in range(2):
            sp.dma_start(self.bo[:, t, :], bo.partition_broadcast(P)).then_inc(self.loaded, 16)


def softmax_attention(nc, top, weights):
    T, ps, ident = top.T, top.ps, top.ident
    NH, HD = 8, 16
    HG = 4
    SCALE = HD ** -0.5
    ROW_MAX = HD
    with ExitStack() as ctx:
        k = Kit(nc, ctx)
        wq, wk, wv, wo = weights.wq, weights.wk, weights.wv, weights.wo
        bq, bk, bv, bo = weights.bq, weights.bk, weights.bv, weights.bo
        w_in = weights.loaded
        upper = k.sb("upper", [P, 1])
        lower = k.sb("lower", [P, 1])
        warm = k.sb("warm", [P, 1])
        one_row = k.sb("one_row", [P, 1])
        bq_up = k.sb("bq_up", [P, 2])
        bq_low = k.sb("bq_low", [P, 2])
        xn = k.sb("xn_c", [P, 2, 2, C])
        xT = k.sb("xT_c", [P, 2, PIX])
        q_low = k.sb("q_low", [P, 2, 2, PIX], F32R)
        q_up = k.sb("q_up", [P, 2, 2, PIX], F32R)
        qa = k.sb("qa", [P, 2, 2, PIX], F32R)
        qb = k.sb("qb", [P, 2, 2, PIX], F32R)
        ka = k.sb("ka", [P, 2, 2, PIX], F32R)
        kl = k.sb("kl", [P, 2, 2, PIX])
        kb = k.sb("kb", [P, 2, 2, PIX], F32R)
        negmax = k.sb("negmax", [P, 2, 2, P])
        vaug = k.sb("vaug", [P, 2, 2, NH, 32])
        prob = k.sb("prob", [P, NH, 2, PIX])
        heads_T = k.sb("heads_T", [P, 2, PIX])
        inv = k.sb("inv", [P, 2 * NH])
        heads = k.sb("heads", [P, 2, P])
        att = k.sb("att", [P, PIX])
        masks_ready, chain, chain2, zeros_ready = (
            k.sem(f"c_{s}") for s in ("masks", "chain", "chain2", "zeros"))
        xn_ready, xT_ps, xT_ready, q_ps, k_ps, v_ps = (
            k.sem(f"c_{s}") for s in ("xn_rd", "xT_ps", "xT_rd", "q_ps", "k_ps", "v_ps"))
        q_low_ready, q_up_ready, qa_ready, ka_ready, kl_ready, kb_ready, v_ready = (
            k.sem(f"c_{s}") for s in ("q_low_rd", "q_up_rd", "qa_rd", "ka_rd", "kl_rd", "kb_rd", "v_rd"))
        max_ps, max_ready, maxT_ps, qb_ready, score_ps, prob_ready = (
            k.sem(f"c_{s}") for s in ("max_ps", "max_rd", "maxT_ps", "qb_rd", "score_ps", "prob_rd"))
        passed_pool = k.sem("c_passed_pool")
        pv_ps, headsT_ready, heads_ps, inv_ready, heads_ready, att_ps, att_ready, out_ps, bo_added, tok_ready = (
            k.sem(f"c_{s}") for s in ("pv_ps", "headsT_rd", "heads_ps", "inv_rd", "heads_rd", "att_ps", "att_rd",
                                      "out_ps", "bo_added", "tok_rd"))

        Q = ps[:, 4, :].rearrange("p (g t) -> p g t", g=2)
        K = ps[:, 5, :].rearrange("p (g t) -> p g t", g=2)
        MAXT = K
        PV = ps[:, 6, :].rearrange("p (g t) -> p g t", g=2)
        HEADS = ps[:, 6, :].rearrange("p (t g c) -> p t g c", t=2, g=2)
        ATT = ps[:, 6, 0:PIX]
        OUT = ps[:, 6, PIX:2 * PIX]
        XT = ps[:, 7, 0:PIX]
        V = ps[:, 7, PIX:2 * PIX]

        block = ctx.enter_context(nc.Block())
        norm_on_vector, norm_on_scalar = prepare_norm(nc, top, block, k, "c")

        @block.gpsimd
        def _(pool):
            nc.gpsimd.memset(vaug[:, 1], 0.0).then_inc(chain2, 1)
            pool.wait_ge(chain2, 1)
            nc.gpsimd.memset(vaug[:, 1, :, :, 0:1], 1.0).then_inc(zeros_ready, 1)
            pool.wait_ge(masks_ready, 1)
            pool.wait_ge(w_in, 9 * 16)

            def keys_low(n, b, first, last):
                wait_apart(pool, kl_ready, n + 1, passed_pool)
                nc.gpsimd.tensor_scalar(kb[:, b], kl[:, b], upper[:], one_row[:], ALU.mult,
                                        ALU.add).then_inc(kb_ready, 1)
                pool.wait_ge(xn_ready, n + 1)
                t = T[:, bass.ds(2 * n, 2), :]
                nc.gpsimd.tensor_tensor(t, t, bo[:], ALU.add).then_inc(bo_added, 1)

            image_loop(pool, keys_low)

        @block.scalar
        def _(act):
            norm_on_scalar(act)
            nc.scalar.activation(warm[:], top.eps5[:], ACT.Exp)
            act.wait_ge(w_in, 9 * 16)
            act.wait_ge(masks_ready, 1)
            act.wait_ge(zeros_ready, 2)

            def transposed(m, b):
                act.wait_ge(xT_ps, m + 1)
                nc.scalar.activation(xT[:, b, :], XT, ACT.Copy).then_inc(xT_ready, 1)

            def queries(m, b):
                act.wait_ge(q_ps, m + 1)
                for g in range(2):
                    last = nc.scalar.activation(q_low[:, b, g], Q[:, g], ACT.Identity, bias=bq_low[:, g:g + 1],
                                                scale=lower[:])
                last.then_inc(q_low_ready, 1)

            def queries_up(m, b):
                act.wait_ge(qa_ready, m + 1)
                for g in range(2):
                    last = nc.scalar.activation(q_up[:, b, g], Q[:, g], ACT.Identity, bias=bq_up[:, g:g + 1],
                                                scale=upper[:])
                last.then_inc(q_up_ready, 1)

            def keys(m, b):
                act.wait_ge(k_ps, m + 1)
                for g in range(2):
                    last = nc.scalar.activation(ka[:, b, g], K[:, g], ACT.Identity, bias=bk[:, g:g + 1])
                last.then_inc(ka_ready, 1)

            def values(m, b):
                act.wait_ge(v_ps, m + 1)
                nc.scalar.activation(vaug[:, b, :, :, 1:1 + HD],
                                     V.rearrange("p (t h d) -> p t h d", t=2, d=HD), ACT.Copy).then_inc(v_ready, 1)

            def exps(n, h, first):
                act.wait_ge(score_ps, NH * n + h + 1)
                if not first:
                    act.wait_ge(pv_ps, 2 * n - 1 + h // HG)
                nc.scalar.activation(prob[:, h].rearrange("p t q -> p (t q)"), ps[:, h % 2, :], ACT.Exp,
                                     scale=SCALE).then_inc(prob_ready, 1)

            transposed(0, 0)
            queries(0, 0)
            queries_up(0, 0)
            keys(0, 0)
            values(0, 0)

            def unnormed(n):
                act.wait_ge(pv_ps, 2 * n + 2)
                nc.scalar.activation(heads_T[:], PV, ACT.Copy).then_inc(headsT_ready, 1)

            def attention(n):
                act.wait_ge(att_ps, n + 1)
                nc.scalar.activation(att[:], ATT, ACT.Identity, bias=bv[:]).then_inc(att_ready, 1)

            def image(n, b, first, last):
                if not last:
                    transposed(n + 1, 1 - b)
                exps(n, 0, first)
                if not last:
                    queries(n + 1, 1 - b)
                exps(n, 1, first)
                if not last:
                    keys(n + 1, 1 - b)
                if not first:
                    attention(n - 1)
                exps(n, 2, first)
                if not last:
                    queries_up(n + 1, 1 - b)
                exps(n, 3, first)
                if not last:
                    values(n + 1, 1 - b)
                for h in range(4, NH):
                    exps(n, h, first)
                unnormed(n)

            image_loop(act, image)
            attention(N - 1)

        @block.tensor
        def _(pe):
            pe.wait_ge(w_in, 9 * 16)

            def transpose(m, b, first=False):
                pe.wait_ge(xn_ready, m + 1)
                if not first:
                    pe.wait_ge(v_ready, m)
                for t in range(2):
                    last = nc.tensor.transpose(XT[:, t * P:(t + 1) * P], xn[:, b, t, :], ident[:])
                last.then_inc(xT_ps, 1)

            def project_q(m, b):
                pe.wait_ge(xT_ready, m + 1)
                for g in range(2):
                    last = nc.tensor.matmul(Q[:, g], wq[:, g, :], xT[:, b, :], start=True, stop=True)
                last.then_inc(q_ps, 1)

            def project_k(m, b):
                for g in range(2):
                    last = nc.tensor.matmul(K[:, g], wk[:, g, :], xT[:, b, :], start=True, stop=True)
                last.then_inc(k_ps, 1)

            def project_v(m, b):
                for t in range(2):
                    last = nc.tensor.matmul(V[:, t * P:(t + 1) * P], xT[:, b, t * P:(t + 1) * P], wv[:],
                                            start=True, stop=True)
                last.then_inc(v_ps, 1)

            def max_scores(m, b, h, first=False):
                g, rows = h // HG, slice(32 * (h % HG), 32 * (h % HG) + 32)
                if h == 0:
                    pe.wait_ge(qa_ready, m + 1)
                    pe.wait_ge(ka_ready, m + 1)
                if not first or h >= 2:
                    pe.wait_ge(max_ready, NH * m + h - 1)
                for t in range(2):
                    last = nc.tensor.matmul(ps[:, 2 + h % 2, t * PIX:(t + 1) * PIX],
                                            qa[rows, b, g, t * P:(t + 1) * P], ka[rows, b, g, :],
                                            start=True, stop=True)
                last.then_inc(max_ps, 1)

            def transpose_maxima(n):
                pe.wait_ge(max_ready, NH * n + NH)
                pe.wait_ge(kb_ready, n + 1)
                for g in range(2):
                    for t in range(2):
                        last = nc.tensor.transpose(MAXT[:, g, t * P:(t + 1) * P], negmax[:, t, g, :], ident[:])
                last.then_inc(maxT_ps, 1)

            def scores(n, b, h, first):
                g, rows = h // HG, slice(32 * (h % HG), 32 * (h % HG) + 32)
                if h == 0:
                    pe.wait_ge(qb_ready, n + 1)
                if not first or h >= 2:
                    pe.wait_ge(prob_ready, NH * n + h - 1)
                if g == 1:
                    nc.tensor.matmul(ps[:, h % 2, :], ka[:, b, g, 0:P], qa[:, b].rearrange("p g t -> p (g t)"),
                                     start=True, stop=True)
                for t in range(2):
                    o = ps[:, h % 2, t * PIX:(t + 1) * PIX]
                    keys = slice(t * P, (t + 1) * P)
                    nc.tensor.matmul(o, ka[rows, b, g, keys], qa[rows, b, g, :], start=True, stop=False)
                    last = nc.tensor.matmul(o, kb[rows, b, g, keys], qb[rows, b, g, :], start=False, stop=True)
                last.then_inc(score_ps, 1)

            def probs_v(n, b, g, first):
                pe.wait_ge(prob_ready, NH * n + HG * (g + 1))
                pe.wait_ge(v_ready, n + 1)
                if g == 0 and not first:
                    pe.wait_ge(tok_ready, n)
                for t in range(2):
                    for j in range(HG):
                        last = nc.tensor.matmul(PV[32 * j:32 * j + 32, g, :], vaug[:, b, t, HG * g + j, :],
                                                prob[:, HG * g + j, t, :], start=(t == 0), stop=(t == 1),
                                                skip_group_check=True)
                last.then_inc(pv_ps, 1)

            def heads_to_tokens(n):
                pe.wait_ge(headsT_ready, n + 1)
                for t in range(2):
                    for g in range(2):
                        last = nc.tensor.transpose(HEADS[:, t, g, :], heads_T[:, g, t * P:(t + 1) * P], ident[:])
                last.then_inc(heads_ps, 1)

            def heads_to_channels(n):
                pe.wait_ge(heads_ready, n + 1)
                for t in range(2):
                    last = nc.tensor.transpose(ATT[:, t * P:(t + 1) * P], heads[:, t, :], ident[:])
                last.then_inc(att_ps, 1)

            def output(n):
                pe.wait_ge(att_ready, n + 1)
                for t in range(2):
                    last = nc.tensor.matmul(OUT[:, t * C:(t + 1) * C], att[:, t * P:(t + 1) * P], wo[:],
                                            start=True, stop=True)
                last.then_inc(out_ps, 1)

            keep_warm(nc, top, 2, 6)
            transpose(0, 0, True)
            project_q(0, 0)
            project_k(0, 0)
            project_v(0, 0)
            for h in range(NH):
                max_scores(0, 0, h, True)

            def image(n, b, first, last):
                transpose_maxima(n)
                if not last:
                    transpose(n + 1, 1 - b)
                if not first:
                    heads_to_tokens(n - 1)
                scores(n, b, 0, first)
                if not last:
                    project_q(n + 1, 1 - b)
                scores(n, b, 1, first)
                if not last:
                    project_k(n + 1, 1 - b)
                if not first:
                    heads_to_channels(n - 1)
                scores(n, b, 2, first)
                if not last:
                    project_v(n + 1, 1 - b)
                scores(n, b, 3, first)
                if not first:
                    output(n - 1)

                def maxima(*heads):
                    if not last:
                        for h in heads:
                            max_scores(n + 1, 1 - b, h)

                maxima(0)
                scores(n, b, 4, first)
                maxima(1)
                probs_v(n, b, 0, first)
                maxima(2)
                scores(n, b, 5, first)
                maxima(3)
                scores(n, b, 6, first)
                maxima(4)
                scores(n, b, 7, first)
                maxima(5, 6, 7)
                probs_v(n, b, 1, first)

            image_loop(pe, image)
            heads_to_tokens(N - 1)
            heads_to_channels(N - 1)
            output(N - 1)

        @block.vector
        def _(dve):
            step = Chain(dve, chain)
            nc.vector.memset(vaug[:, 0, :, :, 1:], 0.0)
            nc.vector.memset(vaug[:, 0, :, :, 0:1], 1.0).then_inc(zeros_ready, 1)
            nc.vector.memset(negmax[:], 0.0)
            norm_on_vector(dve)
            rows = ident[:].rearrange("p (j r) -> p j r", r=32)
            XY = mybir.AxisListType.XY
            nc.vector.tensor_reduce(upper[:], rows[:, :, 0:HD], XY, ALU.add)
            nc.vector.tensor_reduce(lower[:], rows[:, :, HD:32], XY, ALU.add)
            step(nc.vector.tensor_reduce(one_row[:], rows[:, :, ROW_MAX:ROW_MAX + 1], XY, ALU.add))
            dve.wait_ge(w_in, 9 * 16)
            nc.vector.tensor_scalar(bq_up[:], bq[:], upper[:], None, ALU.mult)
            nc.vector.tensor_scalar(bq_low[:], bq[:], lower[:], None, ALU.mult).then_inc(masks_ready, 1)

            def normed(m, b):
                for t in range(2):
                    tile = 2 * m + t
                    last = nc.vector.tensor_scalar(
                        xn[:, b, t, :], T[:, bass.ds(tile, 1), :].rearrange("p t c -> p (t c)"),
                        top.ln_mean[:, bass.ds(tile, 1)], top.ln_rstd[:, bass.ds(tile, 1)], ALU.subtract, ALU.mult)
                last.then_inc(xn_ready, 1)

            def queries(m, b):
                dve.wait_ge(q_low_ready, m + 1)
                for g in range(2):
                    last = nc.vector.scalar_tensor_tensor(qa[:, b, g], Q[:, g], bq[:, g:g + 1], q_low[:, b, g],
                                                          ALU.add, ALU.subtract)
                last.then_inc(qa_ready, 1)

            def keys(m, b):
                dve.wait_ge(ka_ready, m + 1)
                for g in range(2):
                    last = nc.vector.scalar_tensor_tensor(kl[:, b, g], K[:, g], bk[:, g:g + 1], ka[:, b, g],
                                                          ALU.add, ALU.subtract)
                last.then_inc(kl_ready, 1)

            def maxima(m, h):
                dve.wait_ge(max_ps, NH * m + h + 1)
                col = 32 * (h % HG) + ROW_MAX
                nc.vector.tensor_reduce(negmax[:, :, h // HG, col:col + 1],
                                        ps[:, 2 + h % 2, :].rearrange("p (t k) -> p t k", t=2), AX_X, ALU.max,
                                        negate=True).then_inc(max_ready, 1)

            def queries_low(n, b):
                dve.wait_ge(q_up_ready, n + 1)
                dve.wait_ge(maxT_ps, n + 1)
                nc.vector.tensor_tensor(qb[:, b], MAXT, q_up[:, b], ALU.add).then_inc(qb_ready, 1)

            def normalise(n):
                dve.wait_ge(heads_ps, n + 1)
                h = ps[:, 6, :].rearrange("p (h r) -> p h r", r=32)
                nc.vector.reciprocal(inv[:], h[:, :, 0]).then_inc(inv_ready, 1)
                dve.wait_ge(inv_ready, n + 1)
                nc.vector.tensor_tensor(heads[:].rearrange("p t (h d) -> p (t h) d", d=HD), h[:, :, 1:1 + HD],
                                        inv[:].unsqueeze(2).broadcast_to([P, 2 * NH, HD]),
                                        ALU.mult).then_inc(heads_ready, 1)

            def add_output(n):
                dve.wait_ge(out_ps, n + 1)
                dve.wait_ge(bo_added, n + 1)
                t = T[:, bass.ds(2 * n, 2), :].rearrange("p t c -> p (t c)")
                nc.vector.tensor_tensor(t, OUT, t, ALU.add).then_inc(tok_ready, 1)
                dve.wait_ge(tok_ready, n + 1)
                token_statistics(nc, top, n)

            normed(0, 0)
            queries(0, 0)
            keys(0, 0)
            for h in range(NH):
                maxima(0, h)

            def image(n, b, first, last):
                if not last:
                    normed(n + 1, 1 - b)
                queries_low(n, b)
                if not first:
                    normalise(n - 1)
                if not last:
                    queries(n + 1, 1 - b)
                    keys(n + 1, 1 - b)
                    maxima(n + 1, 0)
                if not first:
                    add_output(n - 1)
                if not last:
                    for h in range(1, NH):
                        maxima(n + 1, h)

            image_loop(dve, image)
            normalise(N - 1)
            add_output(N - 1)


def token_statistics(nc, top, n):
    for a in range(2):
        t = 2 * n + a
        last = nc.vector.bn_stats(top.ln_stats[:, bass.ds(t, 1), :].rearrange("p a s -> p (a s)"),
                                  top.T[:, bass.ds(t, 1), :].rearrange("p a c -> p (a c)"))
    return last


class Moe:

    E, TOP = 8, 2
    SLOT_TILES = (TOP * TOK + E * (P - 1)) // P

    def __init__(self, nc, k, hidden, tag):
        self.F = hidden
        self.tag = tag
        self.split = 2 * hidden > 512
        if self.split:
            self.w_high, self.w_low = (k.sb(f"{tag}_{s}", [P, self.E, 2 * hidden], F32R) for s in ("w_high", "w_low"))
        else:
            self.w_in = k.sb(f"{tag}_w_in", [P, self.E, 2 * hidden])
        self.w_out = k.sb(f"{tag}_w_out", [P, self.E, hidden // P, C])
        self.gather = k.sb(f"{tag}_gather", [P, self.SLOT_TILES], U32)
        self.scatter = k.sb(f"{tag}_scatter", [P, self.SLOT_TILES], U32)
        self.expert = k.sb(f"{tag}_expert", [P, self.SLOT_TILES], I32)
        self.weight = k.sb(f"{tag}_weight", [P, self.TOP, TILES])
        self.weights_in = k.sem(f"{tag}_weights_in")
        self.xn_dram = nc.dram_tensor(f"{tag}_normed", [TOK, C], F32, kind="Internal").ap()
        self.y_dram = nc.dram_tensor(f"{tag}_results", [TOK * self.TOP, C], F32, kind="Internal").ap()


class WeightSplit:

    def __init__(self, nc, k, moe, w_in_dram):
        self.nc, self.moe, self.dram = nc, moe, w_in_dram
        self.raw = k.sb("raw_weights", [P, 2, moe.F])
        self.loaded = [k.sem(f"raw_in{b}") for b in range(2)]
        self.high_ready, self.low_ready = k.sem("w_high_rd"), k.sem("w_low_rd")
        assert 2 * moe.E == N

    def piece(self, w, at):
        return w[:, bass.ds(at.round, 1), at.b * self.moe.F:(at.b + 1) * self.moe.F].rearrange("p e f -> p (e f)")

    def load(self, sp):
        sp.sem_inc(self.low_ready, 2)

        def body(at, first, last):
            sp.wait_ge(self.low_ready, at.n + 1)
            sp.dma_start(self.raw[:, at.b, :], self.piece(self.dram, at)).then_inc(self.loaded[at.b], 16)

        pipeline(sp, [(0, body)], N, 2)

    def high(self, act):
        def body(at, first, last):
            act.wait_ge(self.loaded[at.b], 16 * (at.round + 1))
            self.nc.scalar.activation(self.piece(self.moe.w_high, at), self.raw[:, at.b, :],
                                      ACT.Copy).then_inc(self.high_ready, 1)
        return body

    def low(self, pool):
        def body(at, first, last):
            pool.wait_ge(self.high_ready, at.n + 1)
            self.nc.gpsimd.tensor_tensor(self.piece(self.moe.w_low, at), self.raw[:, at.b, :],
                                         self.piece(self.moe.w_high, at), ALU.subtract).then_inc(self.low_ready, 1)
        return body


def linear_attention(nc, top, wq_dram, wkv_dram, moe, w_in_dram):
    T, ps, ident = top.T, top.ps, top.ident
    NH, HD = 8, 16
    EPS = 1e-6
    AW = C + NH
    with ExitStack() as ctx:
        k = Kit(nc, ctx)
        wq = k.sb("e_wq", [P, C])
        wkv = k.sb("e_wkv", [P, 2 * C])
        own = k.sb("e_own", [P, AW])
        xn = k.sb("e_xn", [P, 2, 2, C])
        xT = k.sb("e_xT", [P, 2, PIX])
        q_exp = k.sb("e_q_exp", [P, PIX])
        q_pos = k.sb("e_q_pos", [P, PIX])
        q = k.sb("e_q", [P, 2, PIX])
        k_exp = k.sb("e_k_exp", [P, 2, C])
        k_pos = k.sb("e_k_pos", [P, 2, C])
        kf = k.sb("e_k", [P, 2, 2, C])
        v = k.sb("e_v", [P, 2, 2, C + 1])
        kv = k.sb("e_kv", [P, 2, AW])
        inv = k.sb("e_inv", [P, 2, NH])
        heads = k.sb("e_heads", [P, 2, 2, C])
        w_in, chain, chain_pool, own_ready, ones_ready = (
            k.sem(f"e_{s}") for s in ("w_in", "chain", "chain_pool", "own_rd", "ones_rd"))
        xn_ready, xT_ps, xT_ready, q_ps, kv_ps, q_parts, kv_parts, qf_ready, kf_ready = (
            k.sem(f"e_{s}") for s in ("xn_rd", "xT_ps", "xT_rd", "q_ps", "kv_ps", "q_parts", "kv_parts",
                                      "qf_rd", "kf_rd"))
        sum_ps, sum_ready, out_ps, inv_ready, heads_ready, tok_ready = (
            k.sem(f"e_{s}") for s in ("sum_ps", "sum_rd", "out_ps", "inv_rd", "heads_rd", "tok_rd"))

        XT = lambda b: ps[:, 4 * b, 0:PIX]
        Q = lambda b: ps[:, 4 * b, PIX:2 * PIX]
        KV = lambda b: ps[:, 4 * b + 1, :].rearrange("p (t w c) -> p t w c", t=2, w=2)
        SUM = lambda b: ps[:, 4 * b + 2, 0:C + 1]
        OUT = lambda b: ps[:, 4 * b + 3, 0:2 * AW].rearrange("p (t c) -> p t c", t=2)

        block = ctx.enter_context(nc.Block())
        norm_on_vector, norm_on_scalar = prepare_norm(nc, top, block, k, "e")
        split = WeightSplit(nc, k, moe, w_in_dram)

        @block.sync
        def _(sp):
            sp.dma_start(wq[:], wq_dram).then_inc(w_in, 16)
            sp.dma_start(wkv[:], wkv_dram).then_inc(w_in, 16)
            split.load(sp)

        @block.gpsimd
        def _(pool):
            step = Chain(pool, chain_pool)
            nc.gpsimd.memset(v[:, :, :, C:], 1.0).then_inc(ones_ready, 1)
            step(nc.gpsimd.memset(own[:], 1.0))
            for cols, within in ((own[:, 0:C].rearrange("p (h d) -> p h d", d=HD), [[0, HD]]), (own[:, C:], [])):
                step(nc.gpsimd.affine_select(out=cols, in_=cols, compare_op=ALU.is_ge, fill=0.0, base=0,
                                             pattern=[[-HD, NH]] + within, channel_multiplier=1))
                step(nc.gpsimd.affine_select(out=cols, in_=cols, compare_op=ALU.is_ge, fill=0.0, base=HD - 1,
                                             pattern=[[HD, NH]] + within, channel_multiplier=-1))
            nc.gpsimd.memset(top.pool_scratch[:], 0.0).then_inc(own_ready, 1)

            pool.sem_inc(tok_ready, 2)

            def add_output(at, first, last):
                pool.wait_ge(heads_ready, at.n + 3)
                t = T[:, bass.ds(2 * at.n, 2), :]
                nc.gpsimd.tensor_tensor(t, t, heads[:, at.b], ALU.add).then_inc(tok_ready, 1)

            pipeline(pool, [(0, add_output), (0, split.low(pool))], N, 2)


        @block.scalar
        def _(act):
            norm_on_scalar(act)
            act.wait_ge(ones_ready, 1)
            act.sem_inc(q_parts, 2)
            act.sem_inc(kv_parts, 2)

            def transposed(at, first, last):
                act.wait_ge(xT_ps, at.n + 3)
                nc.scalar.activation(xT[:, at.b, :], XT(at.b), ACT.Copy).then_inc(xT_ready, 1)

            def parts(at, first, last):
                act.wait_ge(q_ps, at.n + 1)
                act.wait_ge(qf_ready, at.n + 1)
                nc.scalar.activation(q_exp[:], Q(at.b), ACT.Exp)
                nc.scalar.activation(q_pos[:], Q(at.b), ACT.Relu).then_inc(q_parts, 1)
                act.wait_ge(kv_ps, at.n + 1)
                act.wait_ge(kf_ready, at.n + 1)
                act.wait_ge(sum_ps, at.n + 1)
                nc.scalar.activation(k_exp[:], KV(at.b)[:, :, 0, :], ACT.Exp)
                nc.scalar.activation(k_pos[:], KV(at.b)[:, :, 0, :], ACT.Relu)
                nc.scalar.activation(v[:, at.b, :, 0:C], KV(at.b)[:, :, 1, :], ACT.Copy).then_inc(kv_parts, 1)

            pipeline(act, [(-1, transposed), (0, parts), (1, split.high(act))], N, 2)

        @block.tensor
        def _(pe):
            pe.wait_ge(w_in, 2 * 16)
            pe.sem_inc(xT_ps, 2)
            pe.sem_inc(sum_ps, 2)
            pe.sem_inc(out_ps, 2)

            def transpose(at, first, last):
                pe.wait_ge(xn_ready, at.n + 1)
                pe.wait_ge(q_parts, at.n + 1)
                for t in range(2):
                    ins = nc.tensor.transpose(XT(at.b)[:, t * P:(t + 1) * P], xn[:, at.b, t, :], ident[:])
                ins.then_inc(xT_ps, 1)

            def project(at, first, last):
                pe.wait_ge(xT_ready, at.n + 1)
                pe.wait_ge(kv_parts, at.n + 1)
                nc.tensor.matmul(Q(at.b), wq[:], xT[:, at.b, :], start=True, stop=True).then_inc(q_ps, 1)
                for t in range(2):
                    ins = nc.tensor.matmul(KV(at.b)[:, t].rearrange("p w c -> p (w c)"),
                                           xT[:, at.b, t * P:(t + 1) * P], wkv[:], start=True, stop=True)
                ins.then_inc(kv_ps, 1)

            def sum_tokens(at, first, last):
                pe.wait_ge(kf_ready, at.n + 2)
                pe.wait_ge(sum_ready, at.n + 1)
                for t in range(2):
                    ins = nc.tensor.matmul(SUM(at.b), kf[:, at.b, t, :], v[:, at.b, t, :], start=(t == 0), stop=(t == 1))
                ins.then_inc(sum_ps, 1)

            def output(at, first, last):
                pe.wait_ge(sum_ready, at.n + 3)
                pe.wait_ge(heads_ready, at.n + 1)
                for t in range(2):
                    ins = nc.tensor.matmul(OUT(at.b)[:, t, :], q[:, at.b, t * P:(t + 1) * P], kv[:, at.b, :],
                                           start=True, stop=True)
                ins.then_inc(out_ps, 1)

            pipeline(pe, [(2, output), (-1, transpose), (0, project), (1, sum_tokens)], N, 2)

        @block.vector
        def _(dve):
            norm_on_vector(dve)
            dve.wait_ge(own_ready, 1)
            for s in (qf_ready, kf_ready):
                dve.sem_inc(s, 1)
            for s in (sum_ready, heads_ready):
                dve.sem_inc(s, 2)

            def normed(at, first, last):
                dve.wait_ge(xT_ps, at.n + 1)
                for t in range(2):
                    tile = 2 * at.n + t
                    ins = nc.vector.tensor_scalar(
                        xn[:, at.b, t, :], T[:, bass.ds(tile, 1), :].rearrange("p t c -> p (t c)"),
                        top.ln_mean[:, bass.ds(tile, 1)], top.ln_rstd[:, bass.ds(tile, 1)], ALU.subtract, ALU.mult)
                ins.then_inc(xn_ready, 1)

            def features(at, first, last):
                dve.wait_ge(q_parts, at.n + 3)
                dve.wait_ge(out_ps, at.n + 1)
                nc.vector.scalar_tensor_tensor(q[:, at.b, :], q_exp[:], 1.0, q_pos[:], ALU.min,
                                               ALU.add).then_inc(qf_ready, 1)
                dve.wait_ge(kv_parts, at.n + 3)
                nc.vector.scalar_tensor_tensor(kf[:, at.b], k_exp[:], 1.0, k_pos[:], ALU.min,
                                               ALU.add).then_inc(kf_ready, 1)

            def sums(at, first, last):
                dve.wait_ge(sum_ps, at.n + 3)
                dve.wait_ge(out_ps, at.n + 1)
                nc.vector.tensor_tensor(kv[:, at.b, 0:C], SUM(at.b)[:, 0:C], own[:, 0:C], ALU.mult)
                nc.vector.tensor_scalar(kv[:, at.b, C:], own[:, C:], SUM(at.b)[:, C:], None,
                                        ALU.mult).then_inc(sum_ready, 1)

            def normalise(at, first, last):
                dve.wait_ge(out_ps, at.n + 3)
                nc.vector.tensor_scalar(inv[:], OUT(at.b)[:, :, C:], EPS, None, ALU.add).then_inc(inv_ready, 1)
                dve.wait_ge(inv_ready, 2 * at.n + 1)
                nc.vector.reciprocal(inv[:], inv[:]).then_inc(inv_ready, 1)
                dve.wait_ge(inv_ready, 2 * at.n + 2)
                dve.wait_ge(tok_ready, at.n + 1)
                for t in range(2):
                    ins = nc.vector.tensor_tensor(
                        heads[:, at.b, t, :].rearrange("p (h d) -> p h d", d=HD),
                        OUT(at.b)[:, t, 0:C].rearrange("p (h d) -> p h d", d=HD),
                        inv[:, t, :].unsqueeze(2).broadcast_to([P, NH, HD]), ALU.mult)
                ins.then_inc(heads_ready, 1)

            def statistics(at, first, last):
                dve.wait_ge(tok_ready, at.n + 3)
                token_statistics(nc, top, at.n)

            pipeline(dve, [(2, normalise), (-2, normed), (0, features), (1, sums), (3, statistics)], N, 2)


def route(nc, top, moe, router_dram, w_in_dram, w_out_dram):
    T, ps, ident = top.T, top.ps, top.ident
    E, SLOT_TILES = moe.E, moe.SLOT_TILES
    TABLE = SLOT_TILES + SLOT_TILES % 2
    GROUP = 4
    NEVER = 4.0 * TOK

    def group_loop(eng, body):
        groups = TILES // GROUP
        body(0, 0, True, False)
        with eng.Fori(0, (groups - 2) // 2) as i:
            for b in (1, 2):
                body(2 * i + b, b % 2, False, False)
        body(groups - 1, (groups - 1) % 2, False, True)

    tag = moe.tag
    with ExitStack() as ctx:
        k = Kit(nc, ctx)
        sb = lambda name, shape, dt=F32: k.sb(f"{tag}_{name}", shape, dt)
        sem = lambda *names: [k.sem(f"{tag}_{s}") for s in names]
        router = sb("router", [P, E])
        xn = top.X[:].rearrange("p (t c) -> p t c", c=C)
        xT = sb("xT", [P, 2, GROUP * P])
        logits = sb("logits", [P, TILES, E])
        rest = sb("rest", [P, TILES, E])
        same = sb("same", [P, TILES, E])
        chosen = sb("chosen", [P, 2, TILES, E])
        both = sb("both", [P, TILES, E])
        best = sb("best", [P, 2, TILES])
        rank = sb("rank", [P, TILES])
        ratio = sb("ratio", [P, TILES])
        scan = sb("scan", [P, 2, TILES, E])
        total = sb("total", [P, TILES, E])
        place = sb("place", [P, TILES, E])
        beyond = sb("beyond", [P, E, TILES])
        used = sb("used", [P, E])
        ends = sb("ends", [P, 2, E])
        base = sb("base", [P, E])
        slot = sb("slot", [P, 2, TILES])
        slot_i = sb("slot_i", [P, 2, TILES], I32)
        part_i = sb("part_i", [P, 2, 2, TILES], I32)
        part = sb("part", [P, 2, 2, TILES])
        passed = sb("passed", [P, SLOT_TILES, E])
        tile_expert = sb("tile_expert", [P, SLOT_TILES])
        descending = sb("descending", [P, E])
        up_to = sb("up_to", [P, P])
        multiples = sb("multiples", [P, TILES])
        number = sb("number", [P, TILES])
        before = sb("before", [P, P])
        ones = sb("ones", [P, P])
        tile_hot = sb("tile_hot", [P, 2, GROUP, 2, TABLE])
        column = sb("column", [P, 2, GROUP, 2, TABLE], F32R)
        row = sb("row", [P, 2, 2, GROUP, P], F32R)
        found = sb("found", [P, 2, SLOT_TILES])
        token = sb("token", [P, SLOT_TILES])
        empty = sb("empty", [P, SLOT_TILES])
        target = sb("target", [P, SLOT_TILES])
        router_in, xn_stored, chain, chain_pool, consts_ready = sem(
            "router_in", "xn_stored", "chain", "chain_pool", "consts_rd")
        xn_ready, xT_ps, xT_ready, logit_ps, logit_ready = sem("xn_rd", "xT_ps", "xT_rd", "logit_ps", "logit_rd")
        gap_ready, ratio_ready, both_ready, count_ps, row_ready, table_ps = sem(
            "gap_rd", "ratio_rd", "both_rd", "count_ps", "row_rd", "table_ps")
        part_ready, tile_ready, column_ready = sem("part_rd", "tile_rd", "column_rd")


        PLACE = ps[:, 4, 0:TILES * E]
        TOTAL = ps[:, 4, TILES * E:2 * TILES * E]
        FOUND = ps[:, 5:7, 0:TABLE]

        block = ctx.enter_context(nc.Block())
        norm_on_vector, norm_on_scalar = prepare_norm(nc, top, block, k, tag)

        @block.sync
        def _(sp):
            sp.dma_start(router[:], router_dram).then_inc(router_in, 16)
            groups = moe.xn_dram.rearrange("(p g t) c -> g p t c", p=P, t=GROUP)
            for g in range(TILES // GROUP):
                sp.wait_ge(xn_ready, g + 1)
                sp.dma_start(groups[g], xn[:, g * GROUP:(g + 1) * GROUP, :]).then_inc(xn_stored, 16)
            if not moe.split:
                sp.dma_start(moe.w_in[:], w_in_dram).then_inc(moe.weights_in, 16)
            sp.dma_start(moe.w_out[:], w_out_dram).then_inc(moe.weights_in, 16)
            sp.wait_ge(xn_stored, 16 * (TILES // GROUP))

        @block.gpsimd
        def _(pool):
            step = Chain(pool, chain_pool)
            whole = dict(allow_small_or_imprecise_dtypes=True)
            nc.gpsimd.iota(up_to[:], pattern=[[1, P]], base=0, channel_multiplier=0, **whole)
            nc.gpsimd.iota(descending[:], pattern=[[-1, E]], base=E, channel_multiplier=0, **whole)
            nc.gpsimd.iota(multiples[:], pattern=[[P, TILES]], base=0, channel_multiplier=0, **whole)
            nc.gpsimd.iota(number[:], pattern=[[1, TILES]], base=1, channel_multiplier=TILES, **whole)
            nc.gpsimd.memset(ones[:], 1.0)
            step(nc.gpsimd.memset(before[:], 1.0))
            nc.gpsimd.affine_select(out=before[:], in_=before[:], compare_op=ALU.is_ge, fill=0.0, base=-1,
                                    pattern=[[1, P]], channel_multiplier=-1).then_inc(consts_ready, 1)

        @block.scalar
        def _(act):
            norm_on_scalar(act)
            act.sem_inc(logit_ready, 2)

            def copy_group(g, b):
                act.wait_ge(xT_ps, g + 1)
                act.wait_ge(logit_ps, g + 1)
                nc.scalar.activation(xT[:, b, :], ps[:, b, :], ACT.Copy).then_inc(xT_ready, 1)

            def copy_logits(g, b):
                act.wait_ge(logit_ps, g + 3)
                nc.scalar.activation(logits[:, bass.ds(g * GROUP, GROUP), :].rearrange("p t e -> p (t e)"),
                                     ps[:, 2 + b, 0:GROUP * E], ACT.Copy).then_inc(logit_ready, 1)

            copy_group(0, 0)
            with act.Fori(0, TILES // GROUP // 2 - 1) as i:
                for b in range(2):
                    copy_group(2 * i + b + 1, 1 - b)
                    copy_logits(2 * i + b, b)
            copy_group(TILES // GROUP - 1, 1)
            copy_logits(TILES // GROUP - 2, 0)
            copy_logits(TILES // GROUP - 1, 1)
            act.wait_ge(gap_ready, 1)
            nc.scalar.activation(ratio[:], rank[:], ACT.Exp).then_inc(ratio_ready, 1)
            act.sem_inc(column_ready, 2)

            def columns(g, b, first, last):
                act.wait_ge(tile_ready, g + 1)
                act.wait_ge(table_ps, g + 1)
                for t in range(GROUP):
                    ins = nc.scalar.activation(column[:, b, t], tile_hot[:, b, t], ACT.Copy,
                                               scale=number[:, bass.ds(g * GROUP + t, 1)])
                ins.then_inc(column_ready, 1)

            group_loop(act, columns)

        @block.tensor
        def _(pe):
            keep_warm(nc, top, 3, 7)
            pe.wait_ge(router_in, 16)
            pe.sem_inc(logit_ps, 2)
            pe.sem_inc(xT_ready, 2)

            def transpose_group(g):
                pe.wait_ge(xn_ready, g + 1)
                pe.wait_ge(xT_ready, g + 1)
                for t in range(GROUP):
                    last = nc.tensor.transpose(ps[:, g % 2, t * P:(t + 1) * P], xn[:, g * GROUP + t, :], ident[:])
                last.then_inc(xT_ps, 1)

            def logits_group(g):
                b = g % 2
                pe.wait_ge(xT_ready, g + 3)
                pe.wait_ge(logit_ready, g + 1)
                for t in range(GROUP):
                    last = nc.tensor.matmul(ps[:, 2 + b, t * E:(t + 1) * E], xT[:, b, t * P:(t + 1) * P],
                                            router[:], start=True, stop=True)
                last.then_inc(logit_ps, 1)

            transpose_group(0)
            for g in range(TILES // GROUP):
                if g + 1 < TILES // GROUP:
                    transpose_group(g + 1)
                logits_group(g)
            pe.wait_ge(consts_ready, 1)
            pe.wait_ge(both_ready, 1)
            m = both[:].rearrange("p t e -> p (t e)")
            nc.tensor.matmul(PLACE, before[:], m, start=True, stop=True)
            nc.tensor.matmul(TOTAL, ones[:], m, start=True, stop=True).then_inc(count_ps, 1)
            pe.sem_inc(table_ps, 2)


            def add_group(g, b, first, last):
                pe.wait_ge(row_ready, g + 1)
                pe.wait_ge(column_ready, g + 3)
                for t in range(GROUP):
                    for c in range(2):
                        ins = nc.tensor.matmul(
                            FOUND[:, c, :], row[:, b, c, t, :],
                            column[:, b, t, c, :],
                            start=first and t == 0, stop=last and t == GROUP - 1)
                ins.then_inc(table_ps, 1)

            group_loop(pe, add_group)

        @block.vector
        def _(dve):
            step = Chain(dve, chain)
            norm_on_vector(dve)
            with dve.Fori(0, 2) as i:
                for t in range(TILES // 2):
                    tile = i * (TILES // 2) + t
                    ins = nc.vector.tensor_scalar(
                        xn[:, bass.ds(tile, 1), :].rearrange("p t c -> p (t c)"),
                        T[:, bass.ds(tile, 1), :].rearrange("p t c -> p (t c)"),
                        top.ln_mean[:, bass.ds(tile, 1)], top.ln_rstd[:, bass.ds(tile, 1)], ALU.subtract, ALU.mult)
                    if t % GROUP == GROUP - 1:
                        ins.then_inc(xn_ready, 1)
            dve.wait_ge(consts_ready, 1)
            dve.wait_ge(logit_ready, TILES // GROUP + 2)
            by_tile = lambda ap: ap.unsqueeze(2).broadcast_to([P, TILES, E])
            by_expert = lambda ap: ap.unsqueeze(1).broadcast_to([P, TILES, E])
            for c, left in enumerate((logits, rest)):
                step(nc.vector.tensor_reduce(best[:, c], left[:], AX_X, ALU.max))
                step(nc.vector.tensor_tensor(same[:], left[:], by_tile(best[:, c]), ALU.is_equal))
                step(nc.vector.tensor_tensor(same[:], same[:], by_expert(descending[:]), ALU.mult))
                step(nc.vector.tensor_reduce(rank[:], same[:], AX_X, ALU.max))
                step(nc.vector.tensor_tensor(chosen[:, c], by_expert(descending[:]), by_tile(rank[:]), ALU.is_equal))
                if c == 0:
                    step(nc.vector.scalar_tensor_tensor(rest[:], chosen[:, 0], -1e30, logits[:], ALU.mult, ALU.add))
            nc.vector.tensor_tensor(both[:], chosen[:, 0], chosen[:, 1], ALU.add).then_inc(both_ready, 1)
            nc.vector.tensor_tensor(rank[:], best[:, 1], best[:, 0], ALU.subtract).then_inc(gap_ready, 1)
            dve.wait_ge(count_ps, 1)
            flat = lambda ap: ap.rearrange("p t e -> p (t e)")
            step(nc.vector.tensor_copy(flat(total[:]), TOTAL))
            src, shift = total[:], 1
            for i in range(5):
                dst = scan[:, i % 2]
                nc.vector.tensor_copy(dst[:, 0:shift], src[:, 0:shift])
                step(nc.vector.tensor_tensor(dst[:, shift:], src[:, shift:], src[:, 0:TILES - shift], ALU.add))
                src, shift = dst, 2 * shift
            count = src[:, TILES - 1]
            step(nc.vector.tensor_tensor(beyond[:], count.unsqueeze(2).broadcast_to([P, E, TILES]),
                                         multiples[:].unsqueeze(1).broadcast_to([P, E, TILES]), ALU.is_gt))
            step(nc.vector.tensor_reduce(used[:], beyond[:], AX_X, ALU.add))
            sums, shift = used[:], 1
            for i in range(3):
                dst = ends[:, i % 2]
                nc.vector.tensor_copy(dst[:, 0:shift], sums[:, 0:shift])
                step(nc.vector.tensor_tensor(dst[:, shift:], sums[:, shift:], sums[:, 0:E - shift], ALU.add))
                sums, shift = dst, 2 * shift
            step(nc.vector.tensor_tensor(base[:], sums, used[:], ALU.subtract))
            step(nc.vector.tensor_tensor(place[:], src, total[:], ALU.subtract))
            step(nc.vector.tensor_tensor(flat(place[:]), PLACE, flat(place[:]), ALU.add))
            step(nc.vector.scalar_tensor_tensor(place[:], by_expert(base[:]), float(P), place[:], ALU.mult, ALU.add))
            for c in range(2):
                step(nc.vector.tensor_tensor(same[:], chosen[:, c], place[:], ALU.mult))
                step(nc.vector.tensor_reduce(slot[:, c], same[:], AX_X, ALU.add))
            step(nc.vector.tensor_copy(slot_i[:], slot[:]))
            nc.vector.tensor_scalar(part_i[:, 0], slot_i[:], 7, None, ALU.logical_shift_right)
            step(nc.vector.tensor_scalar(part_i[:, 1], slot_i[:], P - 1, None, ALU.bitwise_and))
            nc.vector.tensor_copy(part[:], part_i[:]).then_inc(part_ready, 1)
            dve.wait_ge(part_ready, 1)


            def rows(g, b, first, last):
                dve.wait_ge(column_ready, g + 1)
                nc.vector.tensor_tensor(
                    tile_hot[:, b], up_to[:, 0:TABLE].unsqueeze(1).unsqueeze(1).broadcast_to([P, GROUP, 2, TABLE]),
                    part[:, 0, :, bass.ds(g * GROUP, GROUP)].rearrange("p c t -> p t c").unsqueeze(3).broadcast_to(
                        [P, GROUP, 2, TABLE]), ALU.is_equal).then_inc(tile_ready, 1)
                dve.wait_ge(table_ps, g + 1)
                nc.vector.tensor_tensor(
                    row[:, b], up_to[:].unsqueeze(1).unsqueeze(1).broadcast_to([P, 2, GROUP, P]),
                    part[:, 1, :, bass.ds(g * GROUP, GROUP)].unsqueeze(3).broadcast_to([P, 2, GROUP, P]),
                    ALU.is_equal).then_inc(row_ready, 1)

            group_loop(dve, rows)
            step(nc.vector.tensor_tensor(passed[:], up_to[:, 0:SLOT_TILES].unsqueeze(2).broadcast_to([P, SLOT_TILES, E]),
                                         sums.unsqueeze(1).broadcast_to([P, SLOT_TILES, E]), ALU.is_ge))
            step(nc.vector.tensor_reduce(tile_expert[:], passed[:], AX_X, ALU.add))
            nc.vector.tensor_scalar(moe.expert[:], tile_expert[:], float(E - 1), None, ALU.min)
            dve.wait_ge(ratio_ready, 1)
            step(nc.vector.tensor_scalar(moe.weight[:, 0], ratio[:], 1.0, None, ALU.add))
            step(nc.vector.reciprocal(moe.weight[:, 0], moe.weight[:, 0]))
            nc.vector.tensor_tensor(moe.weight[:, 1], ratio[:], moe.weight[:, 0], ALU.mult)
            dve.wait_ge(table_ps, TILES // GROUP + 2)
            step(nc.vector.tensor_copy(found[:], FOUND[:, :, 0:SLOT_TILES]))
            step(nc.vector.tensor_tensor(token[:], found[:, 0], found[:, 1], ALU.add))
            nc.vector.tensor_scalar(moe.gather[:], token[:], 1.0, 0.0, ALU.subtract, ALU.max)
            nc.vector.tensor_scalar(empty[:], token[:], 0.0, NEVER, ALU.is_equal, ALU.mult)
            step(nc.vector.tensor_scalar(target[:], token[:], 2.0, -2.0, ALU.mult, ALU.add))
            step(nc.vector.tensor_tensor(target[:], target[:], empty[:], ALU.add))
            nc.vector.scalar_tensor_tensor(moe.scatter[:], found[:, 1], 0.0, target[:], ALU.is_gt, ALU.add)


def experts(nc, top, moe):
    ps, ident = top.ps, top.ident
    F, SLOT_TILES = moe.F, moe.SLOT_TILES
    CHUNKS = F // P
    tag = moe.tag
    with ExitStack() as ctx:
        k = Kit(nc, ctx)
        sb = lambda name, shape, dt=F32: k.sb(f"{tag}_{name}", shape, dt)
        sem = lambda *names: [k.sem(f"{tag}_{s}") for s in names]
        xg = sb("xg", [P, 4, C])
        xgT = sb("xgT", [P, 2, P], F32R if moe.split else F32)
        xgT_low = sb("xgT_low", [P, 2, P], F32R)
        silu = sb("silu", [P, 2, F])
        h = sb("h", [P, 2, F])
        hT = sb("hT", [P, 2, F])
        y = sb("y", [P, 4, C])
        from_row = sb("from_row", [P, 4, 1], U32)
        to_row = sb("to_row", [P, 4, 1], U32)
        gathered, scattered = (sem(*(f"{s}{b}" for b in range(4))) for s in ("gathered", "scattered"))
        xg_ps, xg_ready, gu_ps, silu_ready, h_ready, h_ps, hT_ready, y_ps, y_ready, passed = sem(
            "xg_ps", "xg_rd", "gu_ps", "silu_rd", "h_rd", "h_ps", "hT_rd", "y_ps", "y_rd", "passed")
        from_ready, to_ready, xg_copied = sem("from_rd", "to_rd", "xg_copied")
        if not moe.split:
            xg_copied = xg_ready

        GATE = lambda b: ps[:, 2 * b, 0:F]
        UP = lambda b: ps[:, 2 * b + 1, 0:F] if moe.split else ps[:, 2 * b, F:2 * F]
        XT = lambda b: ps[:, 6, b * P:(b + 1) * P]
        HT = lambda b: ps[:, 4 + b, 0:F]
        Y = lambda b: ps[:, 7, b * C:(b + 1) * C]

        block = ctx.enter_context(nc.Block())

        @block.gpsimd
        def _(pool):
            def gather(at, first, last):
                wait_apart(pool, xg_ps, at.n + 1, passed)
                wait_apart(pool, from_ready, at.n + 1, passed)
                nc.gpsimd.indirect_dma_start(
                    xg[:, at.b4, :], None, moe.xn_dram,
                    bass.IndirectOffsetOnAxis(ap=from_row[:, at.b4, :], axis=0)).then_inc(gathered[at.b4], 16)

            def scatter(at, first, last):
                wait_apart(pool, to_ready, at.n + 1, passed)
                wait_apart(pool, y_ready, at.n + 3, passed)
                nc.gpsimd.indirect_dma_start(
                    moe.y_dram, bass.IndirectOffsetOnAxis(ap=to_row[:, at.b4, :], axis=0),
                    y[:, at.b4, :], None, bounds_check=TOK * moe.TOP - 1,
                    oob_is_err=False).then_inc(scattered[at.b4], 16)

            pipeline(pool, [(-3, gather), (2, scatter)], SLOT_TILES)
            for b in range(4):
                pool.wait_ge(scattered[b], 16 * ((SLOT_TILES - b + 3) // 4))

        @block.tensor
        def _(pe):
            keep_warm(nc, top, 3, 7)
            pe.wait_ge(moe.weights_in, (1 if moe.split else 2) * 16)
            pe.sem_inc(xg_ps, 4)
            pe.sem_inc(h_ps, 2)
            pe.sem_inc(gu_ps, 2)
            pe.sem_inc(y_ps, 2)

            expert = [pe.alloc_register(f"{tag}_expert{b}") for b in range(4)]

            nc.disable_value_cache = True

            def expert_of(at):
                return bass.RuntimeValue.of_register_unchecked(expert[at.b4]).with_bounds(min_val=0, max_val=moe.E - 1)

            def load_expert(at, first, last):
                pe.reg_load(expert[at.b4], moe.expert[0:1, bass.ds(at.n, 1)])

            def transpose_x(at, first, last):
                pe.wait_ge(gathered[at.b4], 16 * (at.round + 1))
                pe.wait_ge(xg_ready, at.n + 1)
                nc.tensor.transpose(XT(at.b), xg[:, at.b4, :], ident[:]).then_inc(xg_ps, 1)

            def gate_up(at, first, last):
                pe.wait_ge(xg_ready, at.n + 2)
                pe.wait_ge(h_ready, at.n + 1)
                of_expert = lambda w: w[:, bass.ds(expert_of(at), 1), :].rearrange("p e f -> p (e f)")
                if not moe.split:
                    ins = nc.tensor.matmul(ps[:, 2 * at.b, 0:2 * F], xgT[:, at.b, :], of_expert(moe.w_in),
                                           start=True, stop=True)
                else:
                    passes = ((xgT, moe.w_high), (xgT, moe.w_low), (xgT_low, moe.w_high))
                    for i, (x, w) in enumerate(passes):
                        for o, cols in ((GATE(at.b), slice(0, F)), (UP(at.b), slice(F, 2 * F))):
                            ins = nc.tensor.matmul(o, x[:, at.b, :], of_expert(w)[:, cols],
                                                   start=(i == 0), stop=(i == len(passes) - 1))
                ins.then_inc(gu_ps, 1)

            def transpose_h(at, first, last):
                pe.wait_ge(h_ready, at.n + 3)
                pe.wait_ge(hT_ready, at.n + 1)
                for c in range(CHUNKS):
                    ins = nc.tensor.transpose(HT(at.b)[:, c * P:(c + 1) * P], h[:, at.b, c * P:(c + 1) * P], ident[:])
                ins.then_inc(h_ps, 1)

            def down(at, first, last):
                pe.wait_ge(hT_ready, at.n + 3)
                pe.wait_ge(y_ready, at.n + 2)
                for c in range(CHUNKS):
                    ins = nc.tensor.matmul(Y(at.b), hT[:, at.b, c * P:(c + 1) * P],
                                           moe.w_out[:, bass.ds(expert_of(at), 1), c, :].rearrange("p e c -> p (e c)"),
                                           start=(c == 0), stop=(c == CHUNKS - 1))
                ins.then_inc(y_ps, 1)

            pipeline(pe, [(0, gate_up), (-1, load_expert), (-1, transpose_x), (1, transpose_h), (2, down)], SLOT_TILES)
            nc.disable_value_cache = False

        @block.scalar
        def _(act):
            if not moe.split:
                act.sem_inc(xg_ready, 1)
            act.sem_inc(hT_ready, 2)

            def gate(at, first, last):
                act.wait_ge(gu_ps, at.n + 3)
                act.wait_ge(h_ready, at.n + 1)
                nc.scalar.activation(silu[:, at.b, :], GATE(at.b), ACT.Silu).then_inc(silu_ready, 1)

            def copy_x(at, first, last):
                act.wait_ge(xg_ps, at.n + 5)
                nc.scalar.activation(xgT[:, at.b, :], XT(at.b), ACT.Copy).then_inc(xg_copied, 1)

            def copy_h(at, first, last):
                act.wait_ge(h_ps, at.n + 3)
                act.wait_ge(y_ps, at.n + 1)
                nc.scalar.activation(hT[:, at.b, :], HT(at.b), ACT.Copy).then_inc(hT_ready, 1)

            pipeline(act, [(0, gate), (-1, copy_x), (1, copy_h)], SLOT_TILES)

        @block.vector
        def _(dve):
            dve.sem_inc(h_ready, 2)
            dve.sem_inc(y_ready, 2)

            def hidden(at, first, last):
                dve.wait_ge(silu_ready, at.n + 1)
                dve.wait_ge(h_ps, at.n + 1)
                nc.vector.tensor_tensor(h[:, at.b, :], UP(at.b), silu[:, at.b, :], ALU.mult).then_inc(h_ready, 1)

            def result(at, first, last):
                dve.wait_ge(y_ps, at.n + 3)
                if at.reuses:
                    dve.wait_ge(scattered[at.b4], 16 * at.round)
                nc.vector.tensor_copy(to_row[:, at.b4, :], moe.scatter[:, bass.ds(at.n, 1)]).then_inc(to_ready, 1)
                nc.vector.tensor_copy(y[:, at.b4, :], Y(at.b)).then_inc(y_ready, 1)

            def low_x(at, first, last):
                dve.wait_ge(xg_copied, at.n + 1)
                dve.wait_ge(gu_ps, at.n + 1)
                nc.vector.tensor_tensor(xgT_low[:, at.b, :], XT(at.b), xgT[:, at.b, :],
                                        ALU.subtract).then_inc(xg_ready, 1)

            def source(at, first, last):
                if at.reuses:
                    dve.wait_ge(gathered[at.b4], 16 * at.round)
                nc.vector.tensor_copy(from_row[:, at.b4, :], moe.gather[:, bass.ds(at.n, 1)]).then_inc(from_ready, 1)

            low = []
            if moe.split:
                dve.sem_inc(xg_ready, 1)
                low = [(-1, low_x)]
            pipeline(dve, low + [(0, hidden), (2, result), (-4, source)], SLOT_TILES)


def combine(nc, top, moe, out):
    T = top.T
    with ExitStack() as ctx:
        k = Kit(nc, ctx)
        tag = moe.tag
        PARTS = 8
        STEP = TILES // PARTS
        ys = k.sb(f"{tag}_ys", [P, TILES, moe.TOP, C])
        ys_in = [k.sem(f"{tag}_ys_in{i}") for i in range(PARTS)]
        scaled, first_added, added, stored = (
            k.sem(f"{tag}_{s}") for s in ("scaled", "first_added", "added", "stored"))
        block = ctx.enter_context(nc.Block())

        @block.sync
        def _(sp):
            parts = moe.y_dram.rearrange("(p i t c) d -> i p t c d", t=STEP, p=P, c=moe.TOP)
            for i in range(PARTS):
                sp.dma_start(ys[:, i * STEP:(i + 1) * STEP], parts[i]).then_inc(ys_in[i], 16)
            if out is not None:
                out_parts = out.rearrange("(i t p) c -> i p t c", t=STEP, p=P)
                for i in range(PARTS):
                    sp.wait_ge(added, i + 1)
                    sp.dma_start(out_parts[i], T[:, i * STEP:(i + 1) * STEP, :]).then_inc(stored, 16)
                sp.wait_ge(stored, 16 * PARTS)

        @block.scalar
        def _(act):
            for i in range(PARTS):
                act.wait_ge(ys_in[i], 16)
                for t in range(i * STEP, (i + 1) * STEP):
                    ins = nc.scalar.activation(ys[:, t, 1], ys[:, t, 1], ACT.Copy, scale=moe.weight[:, 1, t:t + 1])
                ins.then_inc(scaled, 1)

        @block.gpsimd
        def _(pool):
            for i in range(PARTS):
                tiles = slice(i * STEP, (i + 1) * STEP)
                pool.wait_ge(scaled, i + 1)
                pool.wait_ge(first_added, i + 1)
                nc.gpsimd.tensor_tensor(T[:, tiles], T[:, tiles], ys[:, tiles, 1], ALU.add).then_inc(added, 1)

        @block.vector
        def _(dve):
            def statistics(i):
                dve.wait_ge(added, i + 1)
                for t in range(i * STEP, (i + 1) * STEP):
                    nc.vector.bn_stats(top.ln_stats[:, t, :], T[:, t, :])

            for i in range(PARTS):
                dve.wait_ge(ys_in[i], 16)
                for t in range(i * STEP, (i + 1) * STEP):
                    ins = nc.vector.scalar_tensor_tensor(T[:, t, :], ys[:, t, 0], moe.weight[:, 0, t:t + 1], T[:, t, :],
                                                         ALU.mult, ALU.add)
                ins.then_inc(first_added, 1)
                if out is None and i > 0:
                    statistics(i - 1)
            if out is None:
                statistics(PARTS - 1)


def experts_layer(nc, top, moe, router_dram, w_in_dram, w_out_dram, out=None):
    route(nc, top, moe, router_dram, w_in_dram, w_out_dram)
    experts(nc, top, moe)
    combine(nc, top, moe, out)


class Top:

    def __init__(self, nc, ctx):
        k = Kit(nc, ctx)
        self.X = k.sb("X", [P, TOK])
        self.T = k.sb("T", [P, TILES, C])
        self.ps = ctx.enter_context(nc.psum_tensor("ps", [P, 8, 512], F32))
        self.ident = k.sb("ident", [P, P])
        self.pool_scratch = k.sb("pool_scratch", [P, 1])
        self.gavg = k.sb("gavg", [P, P])
        self.eps5 = k.sb("eps5", [P, 1])
        self.mean = k.sb("mean", [P, N])
        self.rstd = k.sb("rstd", [P, N])
        self.gn_stats = k.sb("gn_stats", [P, N, 6])
        self.ln_stats = k.sb("ln_stats", [P, TILES, 6])
        self.ln_mean = k.sb("ln_mean", [P, TILES])
        self.ln_rstd = k.sb("ln_rstd", [P, TILES])


def layouts(i):
    import numpy as np

    i = {k: np.asarray(v) for k, v in i.items()}
    idx1 = np.zeros((TAP_TILES, QUADS), np.int64)
    idx2 = np.zeros((TAP_TILES, QUADS), np.int64)
    for t in range(TAP_TILES):
        for q in range(QUADS):
            (row, col), _ = tap_of(t, q)
            idx1[t, q] = row * KS + col
            if row % 2 == 0 and col % 2 == 0:
                idx2[t, q] = row // 2 * 3 + col // 2

    def tap_values(v, idx):
        return np.repeat(v.reshape(-1)[idx].T, CM, axis=0)

    fuse = i["L0_conv_fuse_w"].reshape(C, 2 * CM).T
    out = {
        "x": i["x"].transpose(1, 0, 2, 3).reshape(C, TOK),
        "cw": np.tile(i["L0_conv_conv_w"].reshape(CM, C).T, (1, QUADS)),
        "cb": np.tile(i["L0_conv_conv_b"].reshape(CM, 1), (QUADS, 1)),
        "f1": np.tile(fuse[:CM], (QUADS, 1)),
        "f2": np.tile(fuse[CM:], (QUADS, 1)),
        "fuse": fuse,
        "ab": np.concatenate([i["L0_conv_adap_bias"], i["L0_conv_atrous_bias"]]).reshape(2 * CM, 1),
        "fb": i["L0_conv_fuse_b"].reshape(C, 1),
        "taps": np.stack([tap_values(i["L0_conv_conv_kernel_w"], idx1), tap_values(i["L0_conv_conv_kernel_b"], idx1),
                          tap_values(i["L0_conv_conv_kernel2_w"], idx2), tap_values(i["L0_conv_conv_kernel2_b"], idx2)],
                         axis=1),
        "scal": np.concatenate([i[f"L0_conv_{n}"].reshape(-1) for n in
                                ("conv_k_w", "conv_k_b", "conv_k2_w", "conv_k2_b")]),
    }

    def heads_apart(w, front, copies):
        w = w.reshape(w.shape[0], 8, 16)
        o = np.zeros((w.shape[0], 8, 32), w.dtype)
        for c in range(copies):
            o[:, :, front + 16 * c:front + 16 * c + 16] = w
        return o.reshape(w.shape[0], 256)

    def as_partitions(v):
        return v.reshape(2, P).T

    out |= {
        "wq": heads_apart(i["L2_attn_Wq"], 0, 2),
        "wk": heads_apart(i["L2_attn_Wk"], 0, 2),
        "wv": i["L2_attn_Wv"],
        "wo": i["L2_attn_Wo"],
        "bq": as_partitions(heads_apart(i["L2_attn_bq"][None], 0, 2)),
        "bk": as_partitions(heads_apart(i["L2_attn_bk"][None], 0, 2)),
        "bv": i["L2_attn_bv"][:, None],
        "bo": i["L2_attn_bo"],
        "lin_wq": i["L3_attn_Wq"].T,
        "lin_wkv": i["L3_attn_Wkv"].T,
    }

    def expert_weights(gate, up, down):
        e, f, c = down.shape
        return (np.concatenate([gate, up], axis=2).transpose(1, 0, 2),
                down.reshape(e, f // P, P, c).transpose(2, 0, 1, 3))

    out["d_router"] = i["L2_ffn_router_w"].T
    out["d_in"], out["d_out"] = expert_weights(i["L2_ffn_w_gate"], i["L2_ffn_w_up"], i["L2_ffn_w_down"])
    out["f_router"] = i["L3_ffn_Wg"]
    out["f_in"], out["f_out"] = expert_weights(i["L3_ffn_W"], i["L3_ffn_V"], i["L3_ffn_W2"])
    return {k: np.ascontiguousarray(v) for k, v in out.items()}


def program(nc, d, out):
    Kit.used.clear()
    with ExitStack() as ctx:
        top = Top(nc, ctx)
        adaptive_conv(nc, top, *[d[n] for n in ("x", "cw", "cb", "f1", "f2", "fuse", "ab", "fb", "taps", "scal")])
        with ExitStack() as attention:
            weights = AttentionWeights(Kit(nc, attention))
            box_conv(nc, top, lambda sp: weights.load(
                sp, *[d[n] for n in ("wq", "wk", "wv", "wo", "bq", "bk", "bv", "bo")]))
            softmax_attention(nc, top, weights)
        clear_semaphores(nc)
        with ExitStack() as layer:
            moe = Moe(nc, Kit(nc, layer), 256, "d")
            experts_layer(nc, top, moe, d["d_router"], d["d_in"], d["d_out"])
        with ExitStack() as layer:
            moe = Moe(nc, Kit(nc, layer), 512, "f")
            linear_attention(nc, top, d["lin_wq"], d["lin_wkv"], moe, d["f_in"])
            experts_layer(nc, top, moe, d["f_router"], d["f_in"], d["f_out"], out)


def kernel(**inputs):
    import concourse.bacc as _bacc
    from concourse.bass_utils import run_bass_kernel_spmd as _run

    nc = _bacc.Bacc("TRN2", target_bir_lowering=False, num_devices=1)
    laid_out = layouts(inputs)
    drams = {name: nc.dram_tensor(f"in_{name}", a.shape, mybir.dt.from_np(a.dtype), kind="ExternalInput").ap()
             for name, a in laid_out.items()}
    out = nc.dram_tensor("out_tokens", (TOK, C), F32, kind="ExternalOutput").ap()
    program(nc, drams, out)
    r = _run(nc, [{f"in_{name}": a for name, a in laid_out.items()}], core_ids=[0])
    tokens = r.results[0]["out_tokens"]
    return tokens.reshape(N, PIX, C).transpose(0, 2, 1).reshape(N, C, H, W)
```
